# Optimizing a Trainium2 kernel written in Bass

```python
import numpy as np
import jax
import jax.numpy as jnp

def _softmax(x, axis=-1):
    return jax.nn.softmax(x, axis=axis)

def _gelu(x):
    return jax.nn.gelu(x, approximate=True)

def _silu(x):
    return jax.nn.silu(x)

def _sigmoid(x):
    return jax.nn.sigmoid(x)

def _layernorm(x, axis=-1, eps=1e-05):
    m = jnp.mean(x, axis=axis, keepdims=True)
    v = jnp.var(x, axis=axis, keepdims=True)
    return (x - m) / jnp.sqrt(v + eps)

def _scatter_add(tgt, idx, src, axis=0):
    return tgt.at[idx].add(src)

def _segment_sum(src, seg, n):
    return jax.ops.segment_sum(src, seg, n)
kernel_name = 'mk_xattn_ffn_d2_seqx_r8_86ee94'

def setup_inputs(seed: int=0):
    np.random.seed(seed)
    _w = jnp.asarray

    def _rec_inputs():
        import jax
        import jax.numpy as jnp
        _rk = jax.random.key(seed)
        x = -0.0003929 + 0.9999 * jax.random.normal(jax.random.fold_in(_rk, 1), (128, 64, 128), jnp.float32)
        _lenS = 64 - jax.random.randint(jax.random.fold_in(_rk, 7), (128,), 0, max(1, 64 // 4) + 1, jnp.int32)
        _lenS2 = 64 - jax.random.randint(jax.random.fold_in(_rk, 8), (128,), 0, max(1, 64 // 4) + 1, jnp.int32)
        _ctx_1024P = jax.random.normal(jax.random.fold_in(_rk, 11), (128, 16, 128), jnp.float32)
        _ctx_1024c = jax.random.dirichlet(jax.random.fold_in(_rk, 511), 0.3 * jnp.ones((16,), jnp.float32), (128, 64))
        _ctx_1024t = jnp.einsum('bsk,bkd->bsd', _ctx_1024c, _ctx_1024P)
        _ctx_1024t = _ctx_1024t * jax.lax.rsqrt(jnp.mean(jnp.square(_ctx_1024t)) + 1e-12) * 0.953939
        ctx_1024 = -1.39393e-06 + 0.999914 * (_ctx_1024t + 0.3 * jax.random.normal(jax.random.fold_in(_rk, 611), (128, 64, 128), jnp.float32))
        _validS = jnp.arange(64)[None, :] < _lenS[:, None]
        _validS2 = jnp.arange(64)[None, :] < _lenS2[:, None]
        _causal = jnp.tril(jnp.ones((64, 64), dtype=bool))
        mask_Bx1xSxS2_ff0 = jnp.where(jnp.ones((128, 1, 64, 64), dtype=bool), 0.0, -1000000000.0).astype(jnp.float32)
        return (x, ctx_1024, mask_Bx1xSxS2_ff0)
    x, ctx_1024, mask_Bx1xSxS2_ff0 = _rec_inputs()

    def _L0_xattn_setup():
        import jax, jax.numpy as jnp
        import numpy as np
        B, C_LEN, Q_LEN, D = (8, 256, 64, 128)
        key = jax.random.key(seed)
        ks = jax.random.split(key, 10)
        scale = 1.0 / np.sqrt(D)
        return {'c': jax.random.normal(ks[0], (B, C_LEN, D), dtype=jnp.float32), 'q': jax.random.normal(ks[1], (B, Q_LEN, D), dtype=jnp.float32), 'w_cq': jax.random.normal(ks[2], (D,), dtype=jnp.float32) * scale, 'b_cq': jax.random.normal(ks[3], (), dtype=jnp.float32) * scale, 'w_c': jax.random.normal(ks[4], (D,), dtype=jnp.float32) * scale, 'b_c': jax.random.normal(ks[5], (), dtype=jnp.float32) * scale, 'w_q': jax.random.normal(ks[6], (D,), dtype=jnp.float32) * scale, 'b_q': jax.random.normal(ks[7], (), dtype=jnp.float32) * scale, 'W_l': jax.random.normal(ks[8], (D, 4 * D), dtype=jnp.float32) * (1.0 / np.sqrt(4 * D)), 'b_l': jax.random.normal(ks[9], (D,), dtype=jnp.float32) * (1.0 / np.sqrt(4 * D))}
    _L0_xattn_all = _L0_xattn_setup()
    _L0_xattn_in = {k: v for k, v in _L0_xattn_all.items() if k in ('w_cq', 'b_cq', 'w_c', 'b_c', 'w_q', 'b_q', 'W_l', 'b_l')}
    del _L0_xattn_all

    def _L0_ffn_setup():
        import jax, jax.numpy as jnp
        import numpy as np
        B, S, DIM = (4, 256, 128)
        E, K, HID = (8, 2, 512)
        key = jax.random.key(seed)
        ks = jax.random.split(key, 8)
        init = lambda k, sh: jax.random.normal(k, sh, jnp.float32) * 0.02
        return {'x': jax.random.normal(ks[0], (B, S, DIM), jnp.float32), 'gate_w': init(ks[1], (DIM, E)), 'gate_b': jnp.zeros((E,), jnp.float32), 'w1': init(ks[2], (E, DIM, HID)), 'b1': jnp.zeros((E, HID), jnp.float32), 'w2': init(ks[3], (E, HID, DIM)), 'b2': jnp.zeros((E, DIM), jnp.float32), 'ws1': init(ks[4], (DIM, HID)), 'bs1': jnp.zeros((HID,), jnp.float32), 'ws2': init(ks[5], (HID, DIM)), 'bs2': jnp.zeros((DIM,), jnp.float32)}
    _L0_ffn_all = _L0_ffn_setup()
    _L0_ffn_in = {k: v for k, v in _L0_ffn_all.items() if k in ('gate_w', 'gate_b', 'w1', 'b1', 'w2', 'b2', 'ws1', 'bs1', 'ws2', 'bs2')}
    del _L0_ffn_all

    def _L1_xattn_setup():
        import jax, jax.numpy as jnp
        import numpy as np
        B, L, H, N, D = (2, 256, 128, 16, 64)
        key = jax.random.key(seed)
        ks = jax.random.split(key, 7)
        s = 0.02
        return {'query_input': jax.random.normal(ks[0], (B, L, H), jnp.float32), 'source_input': jax.random.normal(ks[1], (B, L, H), jnp.float32), 'bias': jnp.zeros((B, 1, L, L), jnp.float32), 'wq': jax.random.normal(ks[2], (H, N, D), jnp.float32) * s, 'wk': jax.random.normal(ks[3], (H, N, D), jnp.float32) * s, 'wv': jax.random.normal(ks[4], (H, N, D), jnp.float32) * s, 'wo': jax.random.normal(ks[5], (N, D, H), jnp.float32) * s}
    _L1_xattn_all = _L1_xattn_setup()
    _L1_xattn_in = {k: v for k, v in _L1_xattn_all.items() if k in ('wq', 'wk', 'wv', 'wo')}
    del _L1_xattn_all

    def _L1_ffn_setup():
        import jax, jax.numpy as jnp
        import numpy as np
        B, S, D = (4, 256, 128)
        N_EXPERTS, EXPERT_SIZE = (16, 32)
        WIDTH = N_EXPERTS * EXPERT_SIZE
        key = jax.random.key(seed)
        k_x, k_w1, k_w2, k_g = jax.random.split(key, 4)
        x = jax.random.normal(k_x, (B, S, D), dtype=jnp.float32)
        w1 = jax.random.normal(k_w1, (D, WIDTH), dtype=jnp.float32) / np.sqrt(D).astype(np.float32)
        b1 = jnp.zeros((WIDTH,), dtype=jnp.float32)
        w2 = jax.random.normal(k_w2, (WIDTH, D), dtype=jnp.float32) / np.sqrt(WIDTH).astype(np.float32)
        b2 = jnp.zeros((D,), dtype=jnp.float32)
        return {'x': x, 'w1': w1, 'b1': b1, 'w2': w2, 'b2': b2}
    _L1_ffn_all = _L1_ffn_setup()
    _L1_ffn_in = {k: v for k, v in _L1_ffn_all.items() if k in ('w1', 'b1', 'w2', 'b2')}
    del _L1_ffn_all
    return {'x': x, 'ctx_1024': ctx_1024, 'mask_Bx1xSxS2_ff0': mask_Bx1xSxS2_ff0, 'L0_xattn_w_cq': _L0_xattn_in['w_cq'], 'L0_xattn_b_cq': _L0_xattn_in['b_cq'], 'L0_xattn_w_c': _L0_xattn_in['w_c'], 'L0_xattn_b_c': _L0_xattn_in['b_c'], 'L0_xattn_w_q': _L0_xattn_in['w_q'], 'L0_xattn_b_q': _L0_xattn_in['b_q'], 'L0_xattn_W_l': _L0_xattn_in['W_l'], 'L0_xattn_b_l': _L0_xattn_in['b_l'], 'L0_ffn_gate_w': _L0_ffn_in['gate_w'], 'L0_ffn_gate_b': _L0_ffn_in['gate_b'], 'L0_ffn_w1': _L0_ffn_in['w1'], 'L0_ffn_b1': _L0_ffn_in['b1'], 'L0_ffn_w2': _L0_ffn_in['w2'], 'L0_ffn_b2': _L0_ffn_in['b2'], 'L0_ffn_ws1': _L0_ffn_in['ws1'], 'L0_ffn_bs1': _L0_ffn_in['bs1'], 'L0_ffn_ws2': _L0_ffn_in['ws2'], 'L0_ffn_bs2': _L0_ffn_in['bs2'], 'L1_xattn_wq': _L1_xattn_in['wq'], 'L1_xattn_wk': _L1_xattn_in['wk'], 'L1_xattn_wv': _L1_xattn_in['wv'], 'L1_xattn_wo': _L1_xattn_in['wo'], 'L1_ffn_w1': _L1_ffn_in['w1'], 'L1_ffn_b1': _L1_ffn_in['b1'], 'L1_ffn_w2': _L1_ffn_in['w2'], 'L1_ffn_b2': _L1_ffn_in['b2']}

def reference(x, ctx_1024, mask_Bx1xSxS2_ff0, L0_xattn_w_cq, L0_xattn_b_cq, L0_xattn_w_c, L0_xattn_b_c, L0_xattn_w_q, L0_xattn_b_q, L0_xattn_W_l, L0_xattn_b_l, L0_ffn_gate_w, L0_ffn_gate_b, L0_ffn_w1, L0_ffn_b1, L0_ffn_w2, L0_ffn_b2, L0_ffn_ws1, L0_ffn_bs1, L0_ffn_ws2, L0_ffn_bs2, L1_xattn_wq, L1_xattn_wk, L1_xattn_wv, L1_xattn_wo, L1_ffn_w1, L1_ffn_b1, L1_ffn_w2, L1_ffn_b2):
    import jax
    import jax.numpy as jnp

    def _L0_xattn_ref(c, q, w_cq, b_cq, w_c, b_c, w_q, b_q, W_l, b_l):
        import jax, jax.numpy as jnp
        import numpy as np
        B, C_LEN, Q_LEN, D = (8, 256, 64, 128)
        cq = jnp.einsum('bcd,bqd,d->bcq', c, q, w_cq) + b_cq
        s = (c @ w_c + b_c)[:, :, None] + (q @ w_q + b_q)[:, None, :] + cq
        a = jax.nn.softmax(s, axis=2)
        c2q_att = jnp.einsum('bcq,bqd->bcd', a, q)
        b_att = jax.nn.softmax(jnp.max(s, axis=2), axis=1)
        q2c_att = jnp.einsum('bc,bcd->bd', b_att, c)[:, None, :]
        x = jnp.concatenate([c, c2q_att, c * c2q_att, c * q2c_att], axis=-1)
        z = x @ W_l.T + b_l
        return z

    def _L0_ffn_ref(x, gate_w, gate_b, w1, b1, w2, b2, ws1, bs1, ws2, bs2):
        import jax, jax.numpy as jnp
        import numpy as np
        B, S, DIM = (4, 256, 128)
        E, K, HID = (8, 2, 512)
        orig_shape = x.shape
        xf = x.reshape(-1, DIM)
        logits = xf @ gate_w + gate_b
        top_w, top_i = jax.lax.top_k(logits, K)
        gw = jax.nn.softmax(top_w, axis=-1).astype(xf.dtype)
        combine = (gw[:, :, None] * jax.nn.one_hot(top_i, E, dtype=xf.dtype)).sum(axis=1)
        out = jnp.zeros_like(xf)
        for e in range(E):
            h = jax.nn.gelu(xf @ w1[e] + b1[e], approximate=False)
            out = out + combine[:, e:e + 1] * (h @ w2[e] + b2[e])
        shared = jax.nn.gelu(xf @ ws1 + bs1, approximate=False) @ ws2 + bs2
        return (out + shared).reshape(orig_shape)

    def _L1_xattn_ref(query_input, source_input, bias, wq, wk, wv, wo):
        import jax, jax.numpy as jnp
        import numpy as np
        B, L, H, N, D = (2, 256, 128, 16, 64)
        q = jnp.einsum('bfh,hnd->bfnd', query_input, wq)
        k = jnp.einsum('bth,hnd->btnd', source_input, wk)
        v = jnp.einsum('bth,hnd->btnd', source_input, wv)
        depth = q.shape[-1]
        q = q * depth ** (-0.5)
        logits = jnp.einsum('btnd,bfnd->bnft', k, q) + bias
        weights = jax.nn.softmax(logits, axis=-1)
        attn = jnp.einsum('bnft,btnd->bfnd', weights, v)
        return jnp.einsum('bfnd,ndh->bfh', attn, wo)

    def _L1_ffn_ref(x, w1, b1, w2, b2):
        import jax, jax.numpy as jnp
        import numpy as np
        B, S, D = (4, 256, 128)
        N_EXPERTS, EXPERT_SIZE = (16, 32)
        WIDTH = N_EXPERTS * EXPERT_SIZE
        h = jax.nn.relu(jnp.einsum('bsd,dw->bsw', x, w1) + b1)
        return jnp.einsum('bsw,wd->bsd', h, w2) + b2
    x = x + _L0_xattn_ref(_layernorm(x, axis=-1), ctx_1024, L0_xattn_w_cq, L0_xattn_b_cq, L0_xattn_w_c, L0_xattn_b_c, L0_xattn_w_q, L0_xattn_b_q, L0_xattn_W_l, L0_xattn_b_l)
    x = x + _L0_ffn_ref(_layernorm(x, axis=-1), L0_ffn_gate_w, L0_ffn_gate_b, L0_ffn_w1, L0_ffn_b1, L0_ffn_w2, L0_ffn_b2, L0_ffn_ws1, L0_ffn_bs1, L0_ffn_ws2, L0_ffn_bs2)
    x = x + _L1_xattn_ref(_layernorm(x, axis=-1), ctx_1024, mask_Bx1xSxS2_ff0, L1_xattn_wq, L1_xattn_wk, L1_xattn_wv, L1_xattn_wo)
    x = x + _L1_ffn_ref(_layernorm(x, axis=-1), L1_ffn_w1, L1_ffn_b1, L1_ffn_w2, L1_ffn_b2)
    return x

_drawn_inputs = setup_inputs


def setup_inputs(seed=0):
    import zlib

    import numpy as np

    out = dict(_drawn_inputs(seed))
    spreads = {'L0_ffn_gate_b': (0.0, 0.1),
     'L0_ffn_b1': (0.0, 0.579),
     'L0_ffn_b2': (0.0, 0.1),
     'L0_ffn_bs1': (0.0, 0.451),
     'L0_ffn_bs2': (0.0, 0.1),
     'L1_ffn_b1': (0.0, 0.1),
     'L1_ffn_b2': (0.0, 0.1)}
    factors = {'L1_xattn_wq': 8.0, 'L1_xattn_wk': 8.0}
    for name, (base, spread) in spreads.items():
        noise = np.random.default_rng([zlib.crc32(name.encode()), seed]).standard_normal(out[name].shape)
        drawn = base * np.exp(spread * noise) if base else spread * noise
        out[name] = jnp.asarray(drawn.astype(out[name].dtype))
    for name, factor in factors.items():
        out[name] = (out[name] * factor).astype(out[name].dtype)
    return out
```

```python
from contextlib import ExitStack

import concourse.bass as bass
from concourse import mybir

ALU = mybir.AluOpType
ACT = mybir.ActivationFunctionType
AX = mybir.AxisListType
F32 = mybir.dt.float32

P = 128
D = 128
S = 64
NB = P // S
GT = 4
GW = GT * P
LN_EPS = 1e-5


def ds(start, size):
    return bass.ds(start, size)


def wait_alone(engine, semaphore, value, passed):
    engine.wait_ge(semaphore, value)
    engine.sem_inc(passed, 1)


class Chain:

    def __init__(self, engine, semaphore, start, passed=None):
        self.engine, self.semaphore, self.start, self.passed, self.n = engine, semaphore, start, passed, 0

    def step(self, instruction, before_stats=False):
        self.n += 1
        instruction.then_inc(self.semaphore, 1)
        if before_stats:
            wait_alone(self.engine, self.semaphore, self.start + self.n, self.passed)
        else:
            self.engine.wait_ge(self.semaphore, self.start + self.n)


class Space:

    def __init__(self, nc, ctx, tag):
        self.nc, self.ctx, self.tag = nc, ctx, tag

    def sb(self, name, shape, dtype=F32):
        return self.ctx.enter_context(self.nc.sbuf_tensor(f"{self.tag}_{name}", shape, dtype))

    def ps(self, name, shape):
        return self.ctx.enter_context(self.nc.psum_tensor(f"{self.tag}_{name}", shape, F32))

    def sem(self, name):
        return self.ctx.enter_context(self.nc.semaphore(f"{self.tag}_{name}"))


def rows(ap):
    return ap.rearrange("b s d -> (b s) d").rearrange("(t p) d -> p t d", p=P)


def column(ap):
    return ap.rearrange("(p o) -> p o", o=1)


def phase_a(nc, T, X, XN2T, LG, ident):
    NT = X.shape[1]
    G = NT // GT
    with ExitStack() as ctx:
        m = Space(nc, ctx, "a")
        w_cq, w_q, w_c = m.sb("w_cq", [P, 1]), m.sb("w_q", [P, 1]), m.sb("w_c", [P, 1])
        biases = m.sb("biases", [P, 3])
        bias_sum = m.sb("bias_sum", [P, 1])
        b_l = m.sb("b_l", [P, D])
        wl_rows = m.sb("wl_rows", [P, 4 * D])
        wl_t = m.sb("wl_t", [P, 4, D])
        gate_w, gate_b = m.sb("gate_w", [P, 8]), m.sb("gate_b", [P, 8])
        q_rows = [m.sb(f"q_rows{i}", [P, GT, D]) for i in range(2)]
        stats, mv = m.sb("stats", [P, GT, 6]), m.sb("mv", [P, GT, 2])
        var, rstd, minus_half = m.sb("var", [P, GT]), m.sb("rstd", [P, GT]), m.sb("minus_half", [P, GT])
        c_rows, xn_rows = m.sb("c_rows", [P, GT, D]), m.sb("xn_rows", [P, GT, D])
        c_t, cw_t, q_t = m.sb("c_t", [P, GW]), m.sb("cw_t", [P, GW]), m.sb("q_t", [P, GW])
        c2q_t, cc_t, cq_t = m.sb("c2q_t", [P, GW]), m.sb("cc_t", [P, GW]), m.sb("cq_t", [P, GW])
        xn_t = m.sb("xn_t", [P, GW])
        row_max, row_sum, row_rec = m.sb("row_max", [P, GT]), m.sb("row_sum", [P, GT]), m.sb("row_rec", [P, GT])
        s_max = m.sb("s_max", [P, GT])
        scores, weights = m.sb("scores", [P, GT, S]), m.sb("weights", [P, GT, S])
        a_diag = m.sb("a_diag", [P, GT, P])
        a_t = m.sb("a_t", [P, GW])
        bm, bsum, brec = m.sb("bm", [GT, NB]), m.sb("bsum", [GT, NB]), m.sb("brec", [GT, NB])
        b_shift, b_exp, b_att = m.sb("b_shift", [GT, P]), m.sb("b_exp", [GT, P]), m.sb("b_att", [GT, P])
        b_diag = m.sb("b_diag", [P, GT, NB])

        ps_c, ps_q, ps_s, ps_a = (m.ps(n, [P, 512]) for n in ("ps_c", "ps_q", "ps_s", "ps_a"))
        ps_c2q, ps_m, ps_z, ps_x = (m.ps(n, [P, 512]) for n in ("ps_c2q", "ps_m", "ps_z", "ps_x"))
        M_ROW, M_COL, M_Q2C, M_GATE = 0, 128, 136, 160

        w_loaded, masks_set, zeros_set = m.sem("w_loaded"), m.sem("masks_set"), m.sem("zeros_set")
        loaded = [m.sem(f"loaded{i}") for i in range(2)]
        wl_transposed, wl_copied = m.sem("wl_transposed"), m.sem("wl_copied")
        var_ready, rstd_ready, norm_ready = m.sem("var_ready"), m.sem("rstd_ready"), m.sem("norm_ready")
        ct_psum, ct_ready, cw_ready = m.sem("ct_psum"), m.sem("ct_ready"), m.sem("cw_ready")
        s_psum, s_shifted, s_exp, a_ready = m.sem("s_psum"), m.sem("s_shifted"), m.sem("s_exp"), m.sem("a_ready")
        at_psum, at_ready, c2q_psum, c2q_ready = m.sem("at_psum"), m.sem("at_ready"), m.sem("c2q_psum"), m.sem("c2q_ready")
        cc_ready, smax_ready, mrow_psum, b_shifted = m.sem("cc_ready"), m.sem("smax_ready"), m.sem("mrow_psum"), m.sem("b_shifted")
        b_exped, batt_ready, bcol_psum, bdiag_ready = m.sem("b_exped"), m.sem("batt_ready"), m.sem("bcol_psum"), m.sem("bdiag_ready")
        q2c_psum, cq_ready, z_psum = m.sem("q2c_psum"), m.sem("cq_ready"), m.sem("z_psum")
        xt_psum, xt_ready, gate_psum, group_done = m.sem("xt_psum"), m.sem("xt_ready"), m.sem("gate_psum"), m.sem("group_done")
        dve_order, dve_passed, pe_passed = m.sem("dve_order"), m.sem("dve_passed"), m.sem("pe_passed")
        DVE_STEPS = 19
        W_LOADS = 11

        x_dram, q_dram = rows(T["x"]), rows(T["ctx_1024"])

        block = ctx.enter_context(nc.Block())

        @block.sync
        def _(sp):
            def load(g, par):
                sp.dma_start(X[:, ds(GT * g, GT), :], x_dram[:, ds(GT * g, GT), :]).then_inc(loaded[par], 16)
                sp.dma_start(q_rows[par][:], q_dram[:, ds(GT * g, GT), :]).then_inc(loaded[par], 16)

            load(0, 0)
            sp.dma_start(w_cq[:], column(T["L0_xattn_w_cq"])).then_inc(w_loaded, 16)
            sp.dma_start(w_q[:], column(T["L0_xattn_w_q"])).then_inc(w_loaded, 16)
            sp.dma_start(w_c[:], column(T["L0_xattn_w_c"])).then_inc(w_loaded, 16)
            for n, name in enumerate(("L0_xattn_b_cq", "L0_xattn_b_c", "L0_xattn_b_q")):
                sp.dma_start(biases[:, n:n + 1], T[name].partition_broadcast(P)).then_inc(w_loaded, 16)
            sp.dma_start(b_l[:], T["L0_xattn_b_l"].partition_broadcast(P)).then_inc(w_loaded, 16)
            sp.dma_start(wl_rows[:], T["L0_xattn_W_l"]).then_inc(w_loaded, 16)
            sp.dma_start(gate_w[:], T["L0_ffn_gate_w"]).then_inc(w_loaded, 16)
            sp.dma_start(gate_b[:], T["L0_ffn_gate_b"].partition_broadcast(P)).then_inc(w_loaded, 16)
            load(1, 1)
            with sp.Fori(0, G // 2 - 1) as i:
                for par in range(2):
                    sp.wait_ge(c2q_psum, 2 * i + par + 1)
                    load(2 * i + 2 + par, par)

        @block.gpsimd
        def _(pool):
            pool.memset(ident[:], 0.0).then_inc(masks_set, 1)
            pool.wait_ge(masks_set, 1)
            pool.affine_select(out=ident[:], in_=ident[:], compare_op=ALU.not_equal, fill=1.0, base=0,
                               pattern=[[-1, P]], channel_multiplier=1).then_inc(masks_set, 1)
            pool.memset(minus_half[:], -0.5).then_inc(zeros_set, 1)
            pool.memset(a_diag[:], 0.0).then_inc(zeros_set, 1)
            pool.memset(b_diag[:], 0.0).then_inc(zeros_set, 1)
            pool.wait_ge(zeros_set, 3)
            with pool.Fori(0, 2 * G) as n:
                pool.wait_ge(var_ready, n + 1)
                pool.tensor_tensor(rstd[:], var[:], minus_half[:], ALU.pow).then_inc(rstd_ready, 1)

        @block.scalar
        def _(act):
            act.wait_ge(wl_transposed, 1)
            act.copy(wl_t[:].rearrange("p a b -> p (a b)"), ps_z[:]).then_inc(wl_copied, 1)
            with act.Fori(0, G) as g:
                act.wait_ge(ct_psum, 2 * g + 1)
                act.copy(c_t[:], ps_c[:]).then_inc(ct_ready, 1)
                act.wait_ge(ct_psum, 2 * g + 2)
                act.copy(q_t[:], ps_q[:]).then_inc(ct_ready, 1)
                act.wait_ge(s_shifted, g + 1)
                act.activation(weights[:], scores[:], ACT.Exp).then_inc(s_exp, 1)
                act.wait_ge(at_psum, g + 1)
                act.copy(a_t[:], ps_a[:]).then_inc(at_ready, 1)
                act.wait_ge(b_shifted, g + 1)
                act.activation(b_exp[:], b_shift[:], ACT.Exp).then_inc(b_exped, 1)
                act.wait_ge(c2q_psum, g + 1)
                act.copy(c2q_t[:], ps_c2q[:]).then_inc(c2q_ready, 1)
                act.wait_ge(xt_psum, g + 1)
                act.copy(xn_t[:], ps_x[:]).then_inc(xt_ready, 1)
                act.copy(XN2T[:, ds(GT * g, GT), :].rearrange("p a b -> p (a b)"), ps_x[:]).then_inc(xt_ready, 1)

        @block.vector
        def _(dve):
            dve.wait_ge(w_loaded, 16 * (W_LOADS - 1))
            dve.wait_ge(zeros_set, 3)
            dve.tensor_reduce(bias_sum[:], biases[:], AX.X, ALU.add).then_inc(dve_order, 1)

            def layernorm(step, x_of, out, n):
                for k in range(GT - 1):
                    dve.bn_stats(stats[:, k, :], x_of(k))
                step(dve.bn_stats(stats[:, GT - 1, :], x_of(GT - 1)), True)
                for k in range(GT - 1):
                    dve.bn_aggr(mv[:, k, :], stats[:, k, :])
                step(dve.bn_aggr(mv[:, GT - 1, :], stats[:, GT - 1, :]))
                dve.tensor_scalar(var[:], mv[:, :, 1], LN_EPS, None, ALU.add).then_inc(var_ready, 1)
                dve.wait_ge(rstd_ready, n)
                for k in range(GT):
                    dve.tensor_scalar(out[:, k, :], x_of(k), mv[:, k, 0:1], rstd[:, k:k + 1],
                                      ALU.subtract, ALU.mult).then_inc(norm_ready, 1)

            with dve.Fori(0, G // 2) as i:
                for par in range(2):
                    g = 2 * i + par
                    chain = Chain(dve, dve_order, g * DVE_STEPS + 1, dve_passed)

                    def x_of(k):
                        return X[:, ds(GT * g + k, 1), :].rearrange("p a b -> p (a b)")

                    wait_alone(dve, loaded[par], 32 * (i + 1), dve_passed)
                    layernorm(chain.step, x_of, c_rows, 2 * g + 1)
                    dve.wait_ge(ct_ready, 2 * g + 1)
                    dve.tensor_scalar(cw_t[:], c_t[:], w_cq[:, 0:1], w_q[:, 0:1], ALU.mult, ALU.add).then_inc(cw_ready, 1)
                    dve.wait_ge(s_psum, g + 1)
                    s_view = ps_s[:, 0:GT * S].rearrange("p (k q) -> p k q", q=S)
                    chain.step(dve.tensor_reduce(row_max[:], s_view, AX.X, ALU.max))
                    dve.scalar_tensor_tensor(s_max[:], ps_s[:, GT * S:GT * S + GT], bias_sum[:, 0:1], row_max[:],
                                             ALU.add, ALU.add).then_inc(smax_ready, 1)
                    dve.tensor_tensor(scores[:], s_view, row_max[:].unsqueeze(2).to_broadcast([P, GT, S]),
                                      ALU.subtract).then_inc(s_shifted, 1)
                    dve.wait_ge(mrow_psum, g + 1)
                    m_view = ps_m[0:GT, M_ROW:M_ROW + P].rearrange("p (b c) -> p b c", c=S)
                    chain.step(dve.tensor_reduce(bm[:], m_view, AX.X, ALU.max))
                    dve.tensor_tensor(b_shift[:].rearrange("p (b c) -> p b c", c=S), m_view,
                                      bm[:].unsqueeze(2).to_broadcast([GT, NB, S]), ALU.subtract).then_inc(b_shifted, 1)
                    dve.wait_ge(s_exp, g + 1)
                    chain.step(dve.tensor_reduce(row_sum[:], weights[:], AX.X, ALU.add))
                    chain.step(dve.reciprocal(row_rec[:], row_sum[:]))
                    for b in range(NB):
                        h = slice(b * S, b * S + S)
                        dve.tensor_tensor(a_diag[h, :, h], weights[h], row_rec[h].unsqueeze(2).to_broadcast([S, GT, S]),
                                          ALU.mult).then_inc(a_ready, 1)
                    dve.wait_ge(b_exped, g + 1)
                    b_view = b_exp[:].rearrange("p (b c) -> p b c", c=S)
                    chain.step(dve.tensor_reduce(bsum[:], b_view, AX.X, ALU.add))
                    chain.step(dve.reciprocal(brec[:], bsum[:]))
                    dve.tensor_tensor(b_att[:].rearrange("p (b c) -> p b c", c=S), b_view,
                                      brec[:].unsqueeze(2).to_broadcast([GT, NB, S]), ALU.mult).then_inc(batt_ready, 1)
                    dve.wait_ge(bcol_psum, g + 1)
                    for b in range(NB):
                        h = slice(b * S, b * S + S)
                        dve.tensor_copy(b_diag[h, :, b], ps_m[h, M_COL:M_COL + GT]).then_inc(bdiag_ready, 1)
                    dve.wait_ge(c2q_ready, g + 1)
                    dve.tensor_tensor(cc_t[:], c2q_t[:], c_t[:], ALU.mult).then_inc(cc_ready, 1)
                    dve.wait_ge(q2c_psum, g + 1)
                    dve.tensor_tensor(cq_t[:].rearrange("p (n c) -> p n c", c=S), c_t[:].rearrange("p (n c) -> p n c", c=S),
                                      ps_m[:, M_Q2C:M_Q2C + GT * NB].unsqueeze(2).to_broadcast([P, GT * NB, S]),
                                      ALU.mult).then_inc(cq_ready, 1)
                    dve.wait_ge(z_psum, g + 1)
                    x_g = X[:, ds(GT * g, GT), :]
                    chain.step(dve.tensor_tensor(x_g, ps_z[:].rearrange("p (k d) -> p k d", d=D), x_g, ALU.add))
                    chain.step(dve.tensor_tensor(x_g, x_g, b_l[:].unsqueeze(1).to_broadcast([P, GT, D]), ALU.add), True)
                    layernorm(chain.step, x_of, xn_rows, 2 * g + 2)
                    dve.wait_ge(gate_psum, g + 1)
                    chain.step(dve.tensor_tensor(LG[:, ds(GT * g, GT), :],
                                                 ps_m[:, M_GATE:M_GATE + GT * 8].rearrange("p (k e) -> p k e", e=8),
                                                 gate_b[:].unsqueeze(1).to_broadcast([P, GT, 8]), ALU.add))
                    while chain.n < DVE_STEPS:
                        chain.step(dve.tensor_copy(row_sum[:, 0:1], row_max[:, 0:1]))
                    assert chain.n == DVE_STEPS, chain.n

        @block.tensor
        def _(pe):
            pe.wait_ge(masks_set, 2)
            pe.wait_ge(w_loaded, 16 * (W_LOADS - 1))
            for j in range(4):
                last = pe.transpose(ps_z[:, j * P:(j + 1) * P], wl_rows[:, j * D:(j + 1) * D], ident[:])
            last.then_inc(wl_transposed, 1)
            pe.wait_ge(wl_copied, 1)
            with pe.Fori(0, G // 2) as i:
                for par in range(2):
                    g = 2 * i + par
                    for k in range(GT):
                        pe.wait_ge(norm_ready, 2 * GT * g + k + 1)
                        last = pe.transpose(ps_c[:, k * P:(k + 1) * P], c_rows[:, k, :], ident[:])
                    last.then_inc(ct_psum, 1)
                    pe.wait_ge(loaded[par], 32 * (i + 1))
                    for k in range(GT):
                        last = pe.transpose(ps_q[:, k * P:(k + 1) * P], q_rows[par][:, k, :], ident[:])
                    last.then_inc(ct_psum, 1)
                    pe.wait_ge(ct_ready, 2 * g + 2)
                    for k in range(GT):
                        last = pe.matmul(ps_s[:, GT * S + k:GT * S + k + 1], c_t[:, k * P:(k + 1) * P], w_c[:, 0:1],
                                         start=True, stop=True)
                    wait_alone(pe, cw_ready, g + 1, pe_passed)
                    for k in range(GT):
                        for b in range(NB):
                            o = k * P + b * S
                            last = pe.matmul(ps_s[b * S:b * S + S, k * S:(k + 1) * S], cw_t[:, o:o + S], q_t[:, o:o + S],
                                             start=True, stop=True)
                    last.then_inc(s_psum, 1)
                    pe.wait_ge(smax_ready, g + 1)
                    pe.transpose(ps_m[0:GT, M_ROW:M_ROW + P], s_max[:], ident[:]).then_inc(mrow_psum, 1)
                    pe.wait_ge(a_ready, NB * (g + 1))
                    for k in range(GT):
                        last = pe.transpose(ps_a[:, k * P:(k + 1) * P], a_diag[:, k, :], ident[:])
                    last.then_inc(at_psum, 1)
                    wait_alone(pe, batt_ready, g + 1, pe_passed)
                    pe.transpose(ps_m[:, M_COL:M_COL + GT], b_att[:], ident[0:GT, 0:GT]).then_inc(bcol_psum, 1)
                    pe.wait_ge(at_ready, g + 1)
                    for k in range(GT):
                        last = pe.matmul(ps_c2q[:, k * P:(k + 1) * P], q_rows[par][:, k, :], a_t[:, k * P:(k + 1) * P],
                                         start=True, stop=True)
                    last.then_inc(c2q_psum, 1)
                    pe.wait_ge(bdiag_ready, NB * (g + 1))
                    for k in range(GT):
                        last = pe.matmul(ps_m[:, M_Q2C + NB * k:M_Q2C + NB * (k + 1)], c_rows[:, k, :], b_diag[:, k, :],
                                         start=True, stop=True)
                    last.then_inc(q2c_psum, 1)
                    pe.wait_ge(c2q_ready, g + 1)
                    pe.wait_ge(cc_ready, g + 1)
                    pe.wait_ge(cq_ready, g + 1)
                    for k in range(GT):
                        for j, part in enumerate((c_t, c2q_t, cc_t, cq_t)):
                            last = pe.matmul(ps_z[:, k * D:(k + 1) * D], part[:, k * P:(k + 1) * P], wl_t[:, j, :],
                                             start=(j == 0), stop=(j == 3))
                    last.then_inc(z_psum, 1)
                    for k in range(GT):
                        pe.wait_ge(norm_ready, 2 * GT * g + GT + k + 1)
                        last = pe.transpose(ps_x[:, k * P:(k + 1) * P], xn_rows[:, k, :], ident[:])
                    last.then_inc(xt_psum, 1)
                    pe.wait_ge(xt_ready, 2 * g + 1)
                    for k in range(GT):
                        last = pe.matmul(ps_m[:, M_GATE + 8 * k:M_GATE + 8 * (k + 1)], xn_t[:, k * P:(k + 1) * P],
                                         gate_w[:], start=True, stop=True)
                    last.then_inc(gate_psum, 1)


def phase_r(nc, T, LG, COMB):
    NT, E = LG.shape[1], LG.shape[2]
    with ExitStack() as ctx:
        m = Space(nc, ctx, "r")
        above, ties = m.sb("above", [P, NT * E, E]), m.sb("ties", [P, NT * E, E])
        before = m.sb("before", [P, E, E])
        rank, first, second, tmp = (m.sb(n, [P, NT, E]) for n in ("rank", "first", "second", "tmp"))
        v1, v2, diff, ratio, w1, w2, den = (m.sb(n, [P, NT]) for n in ("v1", "v2", "diff", "ratio", "w1", "w2", "den"))
        before_set, diff_ready, ratio_ready, order = m.sem("before_set"), m.sem("diff_ready"), m.sem("ratio_ready"), m.sem("order")
        block = ctx.enter_context(nc.Block())

        @block.gpsimd
        def _(pool):
            pool.memset(before[:], 1.0).then_inc(before_set, 1)
            pool.wait_ge(before_set, 1)
            pool.affine_select(out=before[:], in_=before[:], compare_op=ALU.is_gt, fill=0.0, base=0,
                               pattern=[[1, E], [-1, E]], channel_multiplier=0).then_inc(before_set, 1)

        @block.scalar
        def _(act):
            act.wait_ge(diff_ready, 1)
            act.activation(ratio[:], diff[:], ACT.Exp).then_inc(ratio_ready, 1)

        @block.vector
        def _(dve):
            chain = Chain(dve, order, 0)
            lg_j = LG[:].unsqueeze(2).to_broadcast([P, NT, E, E])
            lg_e = LG[:].unsqueeze(3).to_broadcast([P, NT, E, E])
            a4 = above[:].rearrange("p (t e) j -> p t e j", e=E)
            t4 = ties[:].rearrange("p (t e) j -> p t e j", e=E)
            dve.tensor_tensor(a4, lg_j, lg_e, ALU.is_gt)
            chain.step(dve.tensor_tensor(t4, lg_j, lg_e, ALU.is_equal))
            dve.wait_ge(before_set, 2)
            chain.step(dve.tensor_tensor(t4, t4, before[:].unsqueeze(1).to_broadcast([P, NT, E, E]), ALU.mult))
            chain.step(dve.tensor_tensor(above[:], above[:], ties[:], ALU.add))
            chain.step(dve.tensor_reduce(rank[:].rearrange("p t e -> p (t e)"), above[:], AX.X, ALU.add))
            dve.tensor_scalar(first[:], rank[:], 0.0, None, ALU.is_equal)
            chain.step(dve.tensor_scalar(second[:], rank[:], 1.0, None, ALU.is_equal))
            chain.step(dve.tensor_tensor(tmp[:], first[:], LG[:], ALU.mult))
            chain.step(dve.tensor_reduce(v1[:], tmp[:], AX.X, ALU.add))
            chain.step(dve.tensor_tensor(tmp[:], second[:], LG[:], ALU.mult))
            chain.step(dve.tensor_reduce(v2[:], tmp[:], AX.X, ALU.add))
            dve.tensor_tensor(diff[:], v2[:], v1[:], ALU.subtract).then_inc(diff_ready, 1)
            dve.wait_ge(ratio_ready, 1)
            chain.step(dve.tensor_scalar(den[:], ratio[:], 1.0, None, ALU.add))
            chain.step(dve.reciprocal(w1[:], den[:]))
            chain.step(dve.tensor_tensor(w2[:], w1[:], ratio[:], ALU.mult))
            chain.step(dve.tensor_tensor(first[:], first[:], w1[:].unsqueeze(2).to_broadcast([P, NT, E]), ALU.mult))
            chain.step(dve.tensor_tensor(second[:], second[:], w2[:].unsqueeze(2).to_broadcast([P, NT, E]), ALU.mult))
            chain.step(dve.tensor_tensor(COMB[:], first[:], second[:], ALU.add))


def phase_b(nc, T, X, XN2T, COMB):
    NT = X.shape[1]
    G = NT // GT
    E = COMB.shape[2]
    H = 512
    HC = H // P
    with ExitStack() as ctx:
        m = Space(nc, ctx, "b")
        w1 = [m.sb(f"w1_{i}", [P, H]) for i in range(2)]
        w2 = [m.sb(f"w2_{i}", [P, HC, D]) for i in range(2)]
        b1 = [m.sb(f"b1_{i}", [P, HC]) for i in range(2)]
        b2 = [m.sb(f"b2_{i}", [P, D]) for i in range(2)]
        h_t = [m.sb(f"h_t{i}", [P, HC, GW]) for i in range(2)]
        y = [m.sb(f"y{i}", [P, GT, D]) for i in range(2)]
        ps_h = [m.ps(f"ps_h{j}", [P, GW]) for j in range(HC)]
        ps_y = [m.ps(f"ps_y{i}", [P, GW]) for i in range(2)]
        loaded = [m.sem(f"loaded{i}") for i in range(2)]
        h_psum, h_ready, y_psum, x_added, order = (m.sem(n) for n in ("h_psum", "h_ready", "y_psum", "x_added", "order"))
        ORDER = 2

        block = ctx.enter_context(nc.Block())

        @block.sync
        def _(sp):
            for e in range(E + 1):
                if e >= 2:
                    sp.wait_ge(x_added, G * (e - 1))
                q = e % 2
                a = (T["L0_ffn_w1"][e], T["L0_ffn_w2"][e], T["L0_ffn_b1"][e], T["L0_ffn_b2"][e]) if e < E else \
                    (T["L0_ffn_ws1"], T["L0_ffn_ws2"], T["L0_ffn_bs1"], T["L0_ffn_bs2"])
                sp.dma_start(w1[q][:], a[0]).then_inc(loaded[q], 16)
                sp.dma_start(w2[q][:], a[1].rearrange("(j p) d -> p j d", p=P)).then_inc(loaded[q], 16)
                with nc.allow_non_contiguous_dma("512 biases, one per partition"):
                    sp.dma_start(b1[q][:], a[2].rearrange("(j p) -> p j", p=P)).then_inc(loaded[q], 16)
                sp.dma_start(b2[q][:], a[3].partition_broadcast(P)).then_inc(loaded[q], 16)

        @block.tensor
        def _(pe):
            def up(e, g, n, first=False):
                for j in range(HC):
                    if not first:
                        pe.wait_ge(h_ready, HC * (n - 1) + j + 1)
                    pe.matmul(ps_h[j][:], w1[e % 2][:, j * P:(j + 1) * P],
                              XN2T[:, ds(GT * g, GT), :].rearrange("p a b -> p (a b)"), start=True, stop=True).then_inc(h_psum, 1)

            def down(e, n, par, first=False):
                pe.wait_ge(h_ready, HC * (n + 1))
                if not first:
                    pe.wait_ge(x_added, n - 1)
                for k in range(GT):
                    for j in range(HC):
                        last = pe.matmul(ps_y[par][:, k * D:(k + 1) * D], h_t[par][:, j, k * P:(k + 1) * P], w2[e % 2][:, j, :],
                                         start=(j == 0), stop=(j == HC - 1))
                last.then_inc(y_psum, 1)

            for e in range(E + 1):
                pe.wait_ge(loaded[e % 2], 64 * (e // 2 + 1))
                n0 = e * G
                up(e, 0, n0, e == 0)
                up(e, 1, n0 + 1)
                down(e, n0, 0, e == 0)

                def pair(i, first):
                    up(e, 2 * i + 2, n0 + 2 * i + 2)
                    down(e, n0 + 2 * i + 1, 1, first)
                    up(e, 2 * i + 3, n0 + 2 * i + 3)
                    down(e, n0 + 2 * i + 2, 0)

                pair(0, e == 0)
                with pe.Fori(1, G // 2 - 1) as i:
                    pair(i, False)
                down(e, n0 + G - 1, 1)

        @block.scalar
        def _(act):
            def gelu(e, n, par, first=False):
                if not first:
                    act.wait_ge(y_psum, n - 1)
                for j in range(HC):
                    act.wait_ge(h_psum, HC * n + j + 1)
                    act.activation(h_t[par][:, j, :], ps_h[j][:], ACT.Gelu, bias=b1[e % 2][:, j:j + 1]).then_inc(h_ready, 1)

            for e in range(E + 1):
                act.wait_ge(loaded[e % 2], 64 * (e // 2 + 1))
                n0 = e * G
                for g in range(2):
                    gelu(e, n0 + g, g, e == 0)
                with act.Fori(0, G // 2 - 1) as i:
                    for par in range(2):
                        gelu(e, n0 + 2 * i + 2 + par, par)

        @block.vector
        def _(dve):
            for e in range(E + 1):
                dve.wait_ge(loaded[e % 2], 64 * (e // 2 + 1))
                n0 = e * G
                with dve.Fori(0, G // 2) as i:
                    for par in range(2):
                        g = 2 * i + par
                        n = n0 + 2 * i + par
                        chain = Chain(dve, order, ORDER * n)
                        dve.wait_ge(y_psum, n + 1)
                        chain.step(dve.tensor_tensor(y[par][:], ps_y[par][:].rearrange("p (k d) -> p k d", d=D),
                                                     b2[e % 2][:].unsqueeze(1).to_broadcast([P, GT, D]), ALU.add))
                        x_g = X[:, ds(GT * g, GT), :]
                        if e < E:
                            chain.step(dve.tensor_tensor(y[par][:], y[par][:],
                                                         COMB[:, ds(GT * g, GT), e:e + 1].to_broadcast([P, GT, D]), ALU.mult))
                        else:
                            chain.n += 1
                            dve.sem_inc(order, 1)
                        dve.tensor_tensor(x_g, x_g, y[par][:], ALU.add).then_inc(x_added, 1)
                        dve.wait_ge(x_added, n + 1)


def phase_c(nc, T, X, ident, out):
    NT = X.shape[1]
    G = NT // GT
    N_HEADS, DH = T["L1_xattn_wq"].shape[1], T["L1_xattn_wq"].shape[2]
    J = N_HEADS // 2
    H = T["L1_ffn_w1"].shape[1]
    HC = H // P
    Q_SCALE = DH ** -0.5
    with ExitStack() as ctx:
        m = Space(nc, ctx, "c")
        wq, wk = m.sb("wq", [P, J, P]), m.sb("wk", [P, J, P])
        wv = m.sb("wv", [P, 2, J * DH])
        wo = m.sb("wo", [P, J, D])
        f1, f2 = m.sb("f1", [P, H]), m.sb("f2", [P, HC, D])
        fb1, fb2 = m.sb("fb1", [P, HC]), m.sb("fb2", [P, D])
        ctx_rows = [m.sb(f"ctx_rows{i}", [P, GT, D]) for i in range(2)]
        mask = [m.sb(f"mask{i}", [P, GT, S]) for i in range(2)]
        xn_rows, xn4_rows = m.sb("xn_rows", [P, GT, D]), m.sb("xn4_rows", [P, GT, D])
        xn_t, ctx_t, xn4_t = m.sb("xn_t", [P, GW]), m.sb("ctx_t", [P, GW]), m.sb("xn4_t", [P, GW])
        stats, mv = m.sb("stats", [P, GT, 6]), m.sb("mv", [P, GT, 2])
        var, rstd, minus_half = m.sb("var", [P, GT]), m.sb("rstd", [P, GT]), m.sb("minus_half", [P, GT])
        q_t = [m.sb(f"q_t{i}", [P, J, GW]) for i in range(2)]
        k_t = [m.sb(f"k_t{i}", [P, J, GW]) for i in range(2)]
        v_s = [m.sb(f"v_s{i}", [P, GT, NB, J * DH]) for i in range(2)]
        o_t = m.sb("o_t", [P, J, GW])
        shifted = m.sb("shifted", [P, 2, J * S])
        e_s = shifted
        probs = [m.sb(f"probs{i}", [P, J, 2, S]) for i in range(2)]
        r_max, r_sum, r_rec = (m.sb(n, [P, 2 * J]) for n in ("r_max", "r_sum", "r_rec"))
        p_t = [m.sb(f"p_t{i}", [P, J // 2 * P]) for i in range(2)]
        h_t = m.sb("h_t", [P, HC, GW])

        ps_s = m.ps("ps_s", [P, 2, J * S])
        ps_p = [m.ps(f"ps_p{i}", [P, 512]) for i in range(2)]
        ps_o = [m.ps(f"ps_o{i}", [P, 512]) for i in range(2)]
        ps_w = [m.ps(f"ps_w{i}", [P, 512]) for i in range(2)]

        w_loaded, half_set = m.sem("w_loaded"), m.sem("half_set")
        loaded = [m.sem(f"loaded{i}") for i in range(2)]
        var_ready, rstd_ready = m.sem("var_ready"), m.sem("rstd_ready")
        xn_ready, xn4_ready = m.sem("xn_ready"), m.sem("xn4_ready")
        work_full, work_free = m.sem("work_full"), [m.sem(f"work_free{i}") for i in range(2)]
        s_psum, s_taken, s_shifted, s_exp, probs_ready = (m.sem(n) for n in ("s_psum", "s_taken", "s_shifted", "s_exp", "probs_ready"))
        pt_psum, pt_ready, pv_psum, pv_taken = (m.sem(n) for n in ("pt_psum", "pt_ready", "pv_psum", "pv_taken"))
        order, y_ready, passed = m.sem("order"), m.sem("y_ready"), m.sem("passed")
        stored = [m.sem(f"stored{i}") for i in range(2)]

        x_out, q_dram = rows(out), rows(T["ctx_1024"])
        mask_dram = T["mask_Bx1xSxS2_ff0"].rearrange("b o f t -> (b o f) t").rearrange("(n p) t -> p n t", p=P)

        NQ = J
        USE = {"q": 0, "k": NQ, "o": 2 * NQ, "v": 2 * NQ + 1, "x4": 3 * NQ + 1, "xt": 3 * NQ + 2, "ct": 3 * NQ + 3,
               "up": 3 * NQ + 4, "down": 3 * NQ + 4 + HC}
        PER = 3 * NQ + 5 + HC
        FIRST = {"xt0": 0, "ct0": 1, "q": 2, "k": 2 + NQ, "v": 2 + 2 * NQ, "xt1": 2 + 3 * NQ, "ct1": 3 + 3 * NQ}
        N_FIRST = 4 + 3 * NQ
        G0 = {"q": 0, "k": NQ, "v": 2 * NQ, "xt": 3 * NQ, "ct": 3 * NQ + 1}
        N_G0 = 3 * NQ + 2
        BASE = N_FIRST + N_G0 - PER
        LASTG = {"o": 0, "x4": 1, "up": 2, "down": 2 + HC}
        N_BEFORE_LAST = PER - 2

        class Use:

            def __init__(self, i, n):
                self.bank = n % 2
                self.full = 2 * PER * i + n + 1
                self.before = PER * i + n // 2
                self.first = isinstance(self.before, int) and self.before == 0

        def use(i, c, name, j=0):
            if name in FIRST and c == "pro":
                return Use(0, FIRST[name] + j)
            g = 2 * i + c
            if isinstance(g, int) and g == 0:
                return Use(0, N_FIRST + G0[name] + j)
            if isinstance(g, int) and g == G - 1:
                return Use(0, BASE + PER * (G - 2) + PER + N_BEFORE_LAST - PER + LASTG[name] + j)
            if isinstance(g, int) and g == G:
                return Use(0, BASE + PER * (G - 2) + N_BEFORE_LAST + 3 + HC + LASTG[name] + j)
            n = USE[name] + j
            if isinstance(g, int) and g == G - 2 and name in ("up", "down"):
                n -= 2
            if isinstance(i, int):
                return Use(0, BASE + PER * g + n)
            return Use(i, BASE + PER * c + n)

        def groups(engine, body):
            body(0, 0)
            body(0, 1)
            with engine.Fori(0, (G - 4) // 2) as i:
                for c in (2, 3):
                    body(i, c)
            for c in (2, 3):
                body((G - 4) // 2, c)

        def is_g(i, c, g):
            return isinstance(i, int) and 2 * i + c == g

        def prev_use(i, c, name, j=0):
            if isinstance(i, int):
                return use(0, 2 * i + c - 1, name, j)
            return Use(i, BASE + PER * (c - 1) + USE[name] + j)

        def prev_xt(i, c, which):
            name = ("xt", "ct")[which]
            if is_g(i, c, 0):
                return use(0, "pro", name + "1")
            return prev_use(i, c, name)

        def norm_number(i, c, which):
            g = 2 * i + c
            if isinstance(g, int) and g == 0:
                return 3
            if isinstance(g, int) and g >= G - 1:
                return 3 + 2 * (G - 3) + 1 + (g - (G - 2))
            return 3 + 2 * (g - 1) + (1 if which == "x4" else 2)

        block = ctx.enter_context(nc.Block())

        @block.sync
        def _(sp):
            def load(g, par):
                sp.dma_start(ctx_rows[par][:], q_dram[:, ds(GT * g, GT), :]).then_inc(loaded[par], 16)
                sp.dma_start(mask[par][:], mask_dram[:, ds(GT * g, GT), :]).then_inc(loaded[par], 16)

            load(0, 0)
            sp.dma_start(wq[:], T["L1_xattn_wq"].rearrange("d n h -> d (n h)").rearrange("d (j f) -> d j f", f=P)).then_inc(w_loaded, 16)
            sp.dma_start(wk[:], T["L1_xattn_wk"].rearrange("d n h -> d (n h)").rearrange("d (j f) -> d j f", f=P)).then_inc(w_loaded, 16)
            for par in range(2):
                sp.dma_start(wv[:, par, :].rearrange("d (j h) -> d j h", h=DH),
                             T["L1_xattn_wv"].rearrange("d (j a) h -> d j a h", a=2)[:, :, par, :]).then_inc(w_loaded, 16)
            load(1, 1)
            sp.dma_start(wo[:], T["L1_xattn_wo"].rearrange("n h d -> (n h) d").rearrange("(j p) d -> p j d", p=P)).then_inc(w_loaded, 16)
            sp.dma_start(f1[:], T["L1_ffn_w1"]).then_inc(w_loaded, 16)
            sp.dma_start(f2[:], T["L1_ffn_w2"].rearrange("(j p) d -> p j d", p=P)).then_inc(w_loaded, 16)
            with nc.allow_non_contiguous_dma("512 biases, one per partition"):
                sp.dma_start(fb1[:], T["L1_ffn_b1"].rearrange("(j p) -> p j", p=P)).then_inc(w_loaded, 16)
            sp.dma_start(fb2[:], T["L1_ffn_b2"].partition_broadcast(P)).then_inc(w_loaded, 16)

            def store(g, par):
                sp.wait_ge(y_ready, g + 1)
                sp.dma_start(x_out[:, ds(GT * g, GT), :], X[:, ds(GT * g, GT), :]).then_inc(stored[par], 16)

            def body(i, c):
                g = 2 * i + c
                if not is_g(i, c, G - 1) and not is_g(i, c, G - 2):
                    sp.wait_ge(s_taken, GT * (g + 1))
                    load(g + 2, c % 2)
                if not is_g(i, c, 0):
                    store(g - 1, (c + 1) % 2)

            groups(sp, body)
            store(G - 1, 1)
            for par in range(2):
                sp.wait_ge(stored[par], 16 * G // 2)

        @block.gpsimd
        def _(pool):
            pool.memset(minus_half[:], -0.5).then_inc(half_set, 1)
            pool.wait_ge(half_set, 1)
            with pool.Fori(0, 2 * G) as n:
                pool.wait_ge(var_ready, n + 1)
                pool.tensor_tensor(rstd[:], var[:], minus_half[:], ALU.pow).then_inc(rstd_ready, 1)

        @block.tensor
        def _(pe):
            def begin(u):
                if not u.first:
                    pe.wait_ge(work_free[u.bank], u.before)
                return ps_w[u.bank]

            def transposes(u, source):
                w = begin(u)
                for k in range(GT):
                    last = pe.transpose(w[:, k * P:(k + 1) * P], source[:, k, :], ident[:])
                last.then_inc(work_full, 1)

            def prep_t(i, c, g, par, names=("xt", "ct")):
                pe.wait_ge(xn_ready, GT * (g + 1))
                transposes(use(i, c, names[0]), xn_rows)
                pe.wait_ge(loaded[par], 32 * (half_of(i, c, 2) + 1) if c != "pro" else 32)
                transposes(use(i, c, names[1]), ctx_rows[par])

            def half_of(i, c, more):
                return i + (c + more) // 2

            def project(i, c, name, weight, source, source_use):
                pe.wait_ge(work_free[source_use.bank], source_use.before + 1)
                for j in range(J):
                    u = use(i, c, name, j)
                    pe.matmul(begin(u)[:], weight[:, j, :], source[:], start=True, stop=True).then_inc(work_full, 1)

            def project_v(i, c, source_use):
                pe.wait_ge(work_free[source_use.bank], source_use.before + 1)
                for k in range(GT):
                    for par in range(2):
                        u = use(i, c, "v", 2 * k + par)
                        pe.matmul(begin(u)[:], ctx_t[:, k * P:(k + 1) * P], wv[:, par, :], start=True, stop=True).then_inc(work_full, 1)

            def scores(p, k, par, first):
                if not first:
                    wait_alone(pe, s_taken, p, passed)
                for j in range(J):
                    for b in range(NB):
                        for h in range(2):
                            r, o = slice(h * DH, h * DH + DH), k * P + b * S
                            last = pe.matmul(ps_s[b * S:b * S + S, h, j * S:(j + 1) * S], q_t[par][r, j, o:o + S],
                                             k_t[par][r, j, o:o + S], start=True, stop=True)
                last.then_inc(s_psum, 1)

            def transpose_probs(p, k):
                pe.wait_ge(probs_ready, p + 1)
                for half in range(2):
                    if not (isinstance(p, int) and p == 0):
                        pe.wait_ge(pt_ready, 2 * p + half - 1)
                    for jj in range(J // 2):
                        last = pe.transpose(ps_p[half][:, jj * P:(jj + 1) * P],
                                            probs[k % 2][:, half * (J // 2) + jj, :, :].rearrange("p a t -> p (a t)"), ident[:])
                    last.then_inc(pt_psum, 1)

            def values(p, k, par, phase):
                if phase == 0:
                    wait_alone(pe, pt_ready, 2 * (p + 1), passed)
                    if not (isinstance(p, int) and p == 0):
                        wait_alone(pe, pv_taken, 2 * p, passed)
                for jj in range(J // 2):
                    for b in range(NB):
                        for half in range(2):
                            h = (half + phase) % 2
                            j, r, o = half * (J // 2) + jj, slice(h * DH, h * DH + DH), jj * P + b * S
                            last = pe.matmul(ps_o[half][r, o:o + S], v_s[par][r, k, b, j * DH:(j + 1) * DH],
                                             p_t[half][r, o:o + S], start=True, stop=True)
                if phase == 1:
                    last.then_inc(pv_psum, 1)

            def out_projection(i, c, g):
                pe.wait_ge(pv_taken, 2 * GT * (g + 1))
                w = begin(use(i, c, "o"))
                for k in range(GT):
                    for j in range(J):
                        last = pe.matmul(w[:, k * D:(k + 1) * D], o_t[:, j, k * P:(k + 1) * P], wo[:, j, :],
                                         start=(j == 0), stop=(j == J - 1))
                last.then_inc(work_full, 1)

            def x4_transposes(i, c, g):
                pe.wait_ge(xn4_ready, GT * (g + 1))
                transposes(use(i, c, "x4"), xn4_rows)

            def feed_forward(i, c):
                u4 = use(i, c, "x4")
                pe.wait_ge(work_free[u4.bank], u4.before + 1)
                for j in range(HC):
                    pe.matmul(begin(use(i, c, "up", j))[:], f1[:, j * P:(j + 1) * P], xn4_t[:], start=True, stop=True).then_inc(work_full, 1)
                for j in (HC - 2, HC - 1):
                    u = use(i, c, "up", j)
                    pe.wait_ge(work_free[u.bank], u.before + 1)
                w = begin(use(i, c, "down"))
                for k in range(GT):
                    for j in range(HC):
                        last = pe.matmul(w[:, k * D:(k + 1) * D], h_t[:, j, k * P:(k + 1) * P], f2[:, j, :],
                                         start=(j == 0), stop=(j == HC - 1))
                last.then_inc(work_full, 1)

            pe.wait_ge(w_loaded, 16 * 9)
            prep_t(0, "pro", 0, 0, ("xt0", "ct0"))
            project(0, "pro", "q", wq, xn_t, use(0, "pro", "xt0"))
            project(0, "pro", "k", wk, ctx_t, use(0, "pro", "ct0"))
            project_v(0, "pro", use(0, "pro", "ct0"))
            prep_t(0, "pro", 1, 1, ("xt1", "ct1"))
            for u in (use(0, "pro", "v", 6), use(0, "pro", "v", 7)):
                pe.wait_ge(work_free[u.bank], u.before + 1)

            def body(i, c):
                g = 2 * i + c
                par = c % 2
                first, last_g = is_g(i, c, 0), is_g(i, c, G - 1)
                prep_next = not last_g
                for k in range(GT):
                    p = GT * g + k
                    if not (first and k == 0):
                        transpose_probs(p - 1, (k - 1) % GT)
                    if k == 0 and not first:
                        for n in (6, 7):
                            u = prev_use(i, c, "v", n)
                            pe.wait_ge(work_free[u.bank], u.before + 1)
                    scores(p, k, par, first and k == 0)
                    if not (first and k == 0):
                        values(p - 1, (k - 1) % GT, par if k else 1 - par, 0)
                    if k == 0 and prep_next:
                        project(i, c, "q", wq, xn_t, prev_xt(i, c, 0))
                    if k == 1 and prep_next:
                        project(i, c, "k", wk, ctx_t, prev_xt(i, c, 1))
                    if k == 1 and not first:
                        out_projection(i, c, g - 1)
                    if k == 2 and prep_next:
                        project_v(i, c, prev_xt(i, c, 1))
                    if k == 2 and not first:
                        x4_transposes(i, c, g - 1)
                    if k == 3 and prep_next and not is_g(i, c, G - 2):
                        prep_t(i, c, g + 2, par)
                    if k == 3 and not first:
                        feed_forward(i, c)
                    if not (first and k == 0):
                        values(p - 1, (k - 1) % GT, par if k else 1 - par, 1)

            groups(pe, body)
            transpose_probs(4 * G - 1, 3)
            values(4 * G - 1, 3, 1, 0)
            values(4 * G - 1, 3, 1, 1)
            out_projection(0, G, G - 1)
            x4_transposes(0, G, G - 1)
            feed_forward(0, G)

        @block.scalar
        def _(act):
            def take(u, instruction_of):
                act.wait_ge(work_full, u.full)
                instruction_of(ps_w[u.bank]).then_inc(work_free[u.bank], 1)

            def take_t(u, dest):
                take(u, lambda w: act.copy(dest[:], w[:]))

            def take_q(i, c, name, dest, scale, js):
                for j in js:
                    take(use(i, c, name, j), lambda w: act.mul(dest[:, j, :], w[:], scale) if scale != 1.0 else act.copy(dest[:, j, :], w[:]))

            def take_v(i, c, dest):
                for k in range(GT):
                    for h in range(2):
                        u = use(i, c, "v", 2 * k + h)
                        act.wait_ge(work_full, u.full)
                        for b in range(NB):
                            last = act.copy(dest[h * S:h * S + S, k, b, :], ps_w[u.bank][b * S:b * S + S, :])
                        last.then_inc(work_free[u.bank], 1)

            def take_probs(p):
                for half in range(2):
                    act.wait_ge(pt_psum, 2 * p + half + 1)
                    if not (isinstance(p, int) and p == 0):
                        act.wait_ge(pv_psum, p)
                    act.copy(p_t[half][:], ps_p[half][:]).then_inc(pt_ready, 1)

            def exponentials(p):
                act.wait_ge(s_shifted, p + 1)
                act.activation(e_s[:], shifted[:], ACT.Exp).then_inc(s_exp, 1)

            def take_values(p, k):
                act.wait_ge(pv_psum, p + 1)
                for half in range(2):
                    act.copy(o_t[:, half * (J // 2):(half + 1) * (J // 2), k * P:(k + 1) * P],
                             ps_o[half][:].rearrange("p (j c) -> p j c", c=P)).then_inc(pv_taken, 1)

            def take_hidden(i, c):
                for j in range(HC):
                    take(use(i, c, "up", j), lambda w: act.activation(h_t[:, j, :], w[:], ACT.Relu, bias=fb1[:, j:j + 1]))

            act.wait_ge(w_loaded, 16 * 9)
            take_t(use(0, "pro", "xt0"), xn_t)
            take_t(use(0, "pro", "ct0"), ctx_t)
            take_q(0, "pro", "q", q_t[0], Q_SCALE, range(J))
            take_q(0, "pro", "k", k_t[0], 1.0, range(J))
            take_v(0, "pro", v_s[0])
            take_t(use(0, "pro", "xt1"), xn_t)
            take_t(use(0, "pro", "ct1"), ctx_t)

            def body(i, c):
                g = 2 * i + c
                nxt = (c + 1) % 2
                first = is_g(i, c, 0)
                prep_next = not is_g(i, c, G - 1)
                for k in range(GT):
                    p = GT * g + k
                    if not (first and k == 0):
                        take_probs(p - 1)
                    if k == 0 and prep_next:
                        take_q(i, c, "q", q_t[nxt], Q_SCALE, range(0, 3))
                    if k == 1 and prep_next:
                        take_q(i, c, "k", k_t[nxt], 1.0, range(0, 3))
                    exponentials(p)
                    if k == 0 and prep_next:
                        take_q(i, c, "q", q_t[nxt], Q_SCALE, range(3, J))
                    if k == 1 and prep_next:
                        take_q(i, c, "k", k_t[nxt], 1.0, range(3, J))
                    if k == 2 and prep_next:
                        take_v(i, c, v_s[nxt])
                    if k == 2 and not first:
                        take_t(use(i, c, "x4"), xn4_t)
                    if k == 3 and prep_next and not is_g(i, c, G - 2):
                        take_t(use(i, c, "xt"), xn_t)
                        take_t(use(i, c, "ct"), ctx_t)
                    if k == 3 and not first:
                        take_hidden(i, c)
                    if not (first and k == 0):
                        take_values(p - 1, (k - 1) % GT)

            groups(act, body)
            take_probs(4 * G - 1)
            take_values(4 * G - 1, 3)
            take_t(use(0, G, "x4"), xn4_t)
            take_hidden(0, G)

        @block.vector
        def _(dve):
            state = {"order": 0}

            def step(ins, start, before_stats=False):
                state["order"] += 1
                ins.then_inc(order, 1)
                if before_stats:
                    wait_alone(dve, order, start + state["order"], passed)
                else:
                    dve.wait_ge(order, start + state["order"])

            def layernorm(start, g, dest, dest_ready, n):
                def x_of(k):
                    return X[:, ds(GT * g + k, 1), :].rearrange("p a b -> p (a b)")

                for k in range(GT - 1):
                    dve.bn_stats(stats[:, k, :], x_of(k))
                step(dve.bn_stats(stats[:, GT - 1, :], x_of(GT - 1)), start, True)
                for k in range(GT - 1):
                    dve.bn_aggr(mv[:, k, :], stats[:, k, :])
                step(dve.bn_aggr(mv[:, GT - 1, :], stats[:, GT - 1, :]), start)
                dve.tensor_scalar(var[:], mv[:, :, 1], LN_EPS, None, ALU.add).then_inc(var_ready, 1)
                dve.wait_ge(rstd_ready, n)
                for k in range(GT):
                    dve.tensor_scalar(dest[:, k, :], x_of(k), mv[:, k, 0:1], rstd[:, k:k + 1],
                                      ALU.subtract, ALU.mult).then_inc(dest_ready, 1)

            def shift(p, k, par, start):
                dve.wait_ge(s_psum, p + 1)
                s4 = shifted[:].rearrange("p h (j t) -> p h j t", t=S)
                msk = mask[par][:, k, :].unsqueeze(1).to_broadcast([P, 2 * J, S])
                flat = shifted[:].rearrange("p h (j t) -> p (h j) t", t=S)
                ins = dve.tensor_tensor(flat, ps_s[:].rearrange("p h (j t) -> p (h j) t", t=S), msk, ALU.add)
                ins.then_inc(s_taken, 1)
                dve.wait_ge(s_taken, p + 1)
                step(dve.tensor_reduce(r_max[:], flat, AX.X, ALU.max), start)
                dve.tensor_tensor(flat, flat, r_max[:].unsqueeze(2).to_broadcast([P, 2 * J, S]), ALU.subtract).then_inc(s_shifted, 1)

            def normalise(p, k, start):
                dve.wait_ge(s_exp, p + 1)
                e3 = e_s[:].rearrange("p h (j t) -> p (h j) t", t=S)
                step(dve.tensor_reduce(r_sum[:], e3, AX.X, ALU.add), start)
                step(dve.reciprocal(r_rec[:], r_sum[:]), start)
                if not (isinstance(p, int) and p < 2):
                    dve.wait_ge(pt_psum, 2 * (p - 1))
                for h in range(2):
                    ins = dve.tensor_tensor(probs[k % 2][:, :, h, :], e_s[:, h, :].rearrange("p (j t) -> p j t", t=S),
                                            r_rec[:, h * J:(h + 1) * J].unsqueeze(2).to_broadcast([P, J, S]), ALU.mult)
                ins.then_inc(probs_ready, 1)
                dve.wait_ge(probs_ready, p + 1)

            def add_attention(i, c, g, start):
                u = use(i, c, "o")
                dve.wait_ge(work_full, u.full)
                x_g = X[:, ds(GT * g, GT), :]
                dve.tensor_tensor(x_g, x_g, ps_w[u.bank][:].rearrange("p (k d) -> p k d", d=D), ALU.add).then_inc(work_free[u.bank], 1)
                dve.wait_ge(work_free[u.bank], u.before + 1)

            def finish(i, c, g, par, start):
                u = use(i, c, "down")
                dve.wait_ge(work_full, u.full)
                x_g = X[:, ds(GT * g, GT), :]
                dve.tensor_tensor(x_g, x_g, ps_w[u.bank][:].rearrange("p (k d) -> p k d", d=D),
                                  ALU.add).then_inc(work_free[u.bank], 1)
                dve.wait_ge(work_free[u.bank], u.before + 1)
                dve.tensor_tensor(x_g, x_g, fb2[:].unsqueeze(1).to_broadcast([P, GT, D]), ALU.add).then_inc(y_ready, 1)
                dve.wait_ge(y_ready, g + 1)

            PRO, O0, OG = 4, 3 * GT + 2, 3 * GT + 4
            dve.wait_ge(w_loaded, 16 * 9)
            layernorm(0, 0, xn_rows, xn_ready, 1)
            u = use(0, "pro", "xt0")
            dve.wait_ge(work_full, u.full)
            layernorm(0, 1, xn_rows, xn_ready, 2)

            def body(i, c):
                g = 2 * i + c
                first = is_g(i, c, 0)
                par = c % 2
                start = PRO if first else PRO + O0 + OG * (g - 1) - (2 if is_g(i, c, G - 1) else 0)
                state["order"] = 0
                dve.wait_ge(loaded[par], 32 * (i + c // 2 + 1))
                for k in range(GT):
                    p = GT * g + k
                    shift(p, k, par, start)
                    if k == 2 and not is_g(i, c, G - 1) and not is_g(i, c, G - 2):
                        u = prev_xt(i, c, 0)
                        wait_alone(dve, work_full, u.full, passed)
                        layernorm(start, g + 2, xn_rows, xn_ready, norm_number(i, c, "xn"))
                    normalise(p, k, start)
                    if k == 1 and not first:
                        add_attention(i, c, g - 1, start)
                        if not is_g(i, c, 1):
                            wait_alone(dve, work_full, prev_use(i, c, "x4").full, passed)
                        layernorm(start, g - 1, xn4_rows, xn4_ready, norm_number(i, c, "x4"))
                    if k == 3 and not first:
                        finish(i, c, g - 1, (c + 1) % 2, start)

            groups(dve, body)
            state["order"] = 0
            start = PRO + O0 + OG * (G - 2) - 2 + 3 * GT + 2
            add_attention(0, G, G - 1, start)
            dve.wait_ge(work_full, use(0, G - 1, "x4").full)
            layernorm(start, G - 1, xn4_rows, xn4_ready, 2 * G)
            finish(G // 2, 0, G - 1, 1, start)


def build(nc, T, out):
    NT = T["x"].shape[0] * T["x"].shape[1] // P
    E = T["L0_ffn_gate_w"].shape[1]
    with ExitStack() as ctx:
        m = Space(nc, ctx, "k")
        X, ident = m.sb("X", [P, NT, D]), m.sb("ident", [P, P])
        with ExitStack() as moe:
            m2 = Space(nc, moe, "e")
            XN2T, LG, COMB = m2.sb("XN2T", [P, NT, D]), m2.sb("LG", [P, NT, E]), m2.sb("COMB", [P, NT, E])
            phase_a(nc, T, X, XN2T, LG, ident)
            phase_r(nc, T, LG, COMB)
            phase_b(nc, T, X, XN2T, COMB)
        phase_c(nc, T, X, ident, out)


def kernel(**inputs):
    import numpy as _np
    import concourse.bacc as _bacc
    from concourse import mybir as _mybir
    from concourse.bass_utils import run_bass_kernel_spmd as _run

    nc = _bacc.Bacc("TRN2", target_bir_lowering=False, num_devices=1)
    arrays, tensors = {}, {}
    for name in inputs:
        a = _np.ascontiguousarray(inputs[name])
        arrays[f"in_{name}"] = a
        tensors[name] = nc.dram_tensor(f"in_{name}", a.shape, _mybir.dt.from_np(a.dtype), kind="ExternalInput").ap()
    out = nc.dram_tensor("out", inputs["x"].shape, _mybir.dt.float32, kind="ExternalOutput").ap()
    build(nc, tensors, out)
    r = _run(nc, [arrays], core_ids=[0])
    return r.results[0]["out"]
```

```python
from contextlib import ExitStack

import concourse.bass as bass
from concourse import mybir

ALU = mybir.AluOpType
ACT = mybir.ActivationFunctionType
AX = mybir.AxisListType
F32 = mybir.dt.float32

P = 128
D = 128
S = 64
NB = P // S
GT = 4
GW = GT * P
LN_EPS = 1e-5


def ds(start, size):
    return bass.ds(start, size)


def wait_alone(engine, semaphore, value, passed):
    engine.wait_ge(semaphore, value)
    engine.sem_inc(passed, 1)


class Chain:

    def __init__(self, engine, semaphore, start, passed=None):
        self.engine, self.semaphore, self.start, self.passed, self.n = engine, semaphore, start, passed, 0

    def step(self, instruction, before_stats=False):
        self.n += 1
        instruction.then_inc(self.semaphore, 1)
        if before_stats:
            wait_alone(self.engine, self.semaphore, self.start + self.n, self.passed)
        else:
            self.engine.wait_ge(self.semaphore, self.start + self.n)


class Space:

    def __init__(self, nc, ctx, tag):
        self.nc, self.ctx, self.tag = nc, ctx, tag

    def sb(self, name, shape, dtype=F32):
        return self.ctx.enter_context(self.nc.sbuf_tensor(f"{self.tag}_{name}", shape, dtype))

    def ps(self, name, shape):
        return self.ctx.enter_context(self.nc.psum_tensor(f"{self.tag}_{name}", shape, F32))

    def sem(self, name):
        return self.ctx.enter_context(self.nc.semaphore(f"{self.tag}_{name}"))


def rows(ap):
    return ap.rearrange("b s d -> (b s) d").rearrange("(t p) d -> p t d", p=P)


def column(ap):
    return ap.rearrange("(p o) -> p o", o=1)


def phase_a(nc, T, X, XN2, XN2T, LG, experts, sorted_x, ident):
    NT = X.shape[1]
    G = NT // GT
    with ExitStack() as ctx:
        m = Space(nc, ctx, "a")
        w_cq, w_q, w_c = m.sb("w_cq", [P, 1]), m.sb("w_q", [P, 1]), m.sb("w_c", [P, 1])
        biases = m.sb("biases", [P, 3])
        bias_sum = m.sb("bias_sum", [P, 1])
        b_l = m.sb("b_l", [P, D])
        wl_rows = m.sb("wl_rows", [P, 4 * D])
        wl_t = m.sb("wl_t", [P, 4, D])
        gate_w, gate_b = m.sb("gate_w", [P, 8]), m.sb("gate_b", [P, 8])
        q_rows = [m.sb(f"q_rows{i}", [P, GT, D]) for i in range(2)]
        stats, mv = m.sb("stats", [P, GT, 6]), m.sb("mv", [P, GT, 2])
        var1, rstd1, var2, rstd2, minus_half = (m.sb(n, [P, GT]) for n in ("var1", "rstd1", "var2", "rstd2", "minus_half"))
        c_rows = [m.sb(f"c_rows{i}", [P, GT, D]) for i in range(2)]
        xn_rows = m.sb("xn_rows", [P, GT, D])
        c_t = [m.sb(f"c_t{i}", [P, GW]) for i in range(2)]
        cw_t, q_t = m.sb("cw_t", [P, GW]), m.sb("q_t", [P, GW])
        c2q_t, cc_t, cq_t = m.sb("c2q_t", [P, GW]), m.sb("cc_t", [P, GW]), m.sb("cq_t", [P, GW])
        xn_t = m.sb("xn_t", [P, GW])
        row_max, row_sum, row_rec = m.sb("row_max", [P, GT]), m.sb("row_sum", [P, GT]), m.sb("row_rec", [P, GT])
        s_max = m.sb("s_max", [P, GT])
        scores, weights = m.sb("scores", [P, GT, S]), m.sb("weights", [P, GT, S])
        a_diag = m.sb("a_diag", [P, GT, P])
        a_t = m.sb("a_t", [P, GW])
        bm, bsum, brec = m.sb("bm", [GT, NB]), m.sb("bsum", [GT, NB]), m.sb("brec", [GT, NB])
        b_shift, b_exp, b_att = m.sb("b_shift", [GT, P]), m.sb("b_exp", [GT, P]), m.sb("b_att", [GT, P])
        b_diag = m.sb("b_diag", [P, GT, NB])

        zeros = m.sb("zeros", [P, 1136])

        ps_c, ps_q, ps_s, ps_a = (m.ps(n, [P, 512]) for n in ("ps_c", "ps_q", "ps_s", "ps_a"))
        ps_c2q, ps_m, ps_z, ps_x = (m.ps(n, [P, 512]) for n in ("ps_c2q", "ps_m", "ps_z", "ps_x"))
        M_ROW, M_COL, M_Q2C, M_GATE = 0, 128, 136, 160

        w_loaded, masks_set, zeros_set = m.sem("w_loaded"), m.sem("masks_set"), m.sem("zeros_set")
        loaded = [m.sem(f"loaded{i}") for i in range(2)]
        wl_transposed, wl_copied = m.sem("wl_transposed"), m.sem("wl_copied")
        var1_ready, rstd1_ready, cnorm_ready = m.sem("var1_ready"), m.sem("rstd1_ready"), m.sem("cnorm_ready")
        var2_ready, rstd2_ready, xnorm_ready = m.sem("var2_ready"), m.sem("rstd2_ready"), m.sem("xnorm_ready")
        ct_psum, ct_ready, cw_ready = m.sem("ct_psum"), m.sem("ct_ready"), m.sem("cw_ready")
        s_psum, s_shifted, s_exp, a_ready = m.sem("s_psum"), m.sem("s_shifted"), m.sem("s_exp"), m.sem("a_ready")
        at_psum, at_ready, c2q_psum, c2q_ready = m.sem("at_psum"), m.sem("at_ready"), m.sem("c2q_psum"), m.sem("c2q_ready")
        cc_ready, smax_ready, mrow_psum, b_shifted = m.sem("cc_ready"), m.sem("smax_ready"), m.sem("mrow_psum"), m.sem("b_shifted")
        b_exped, batt_ready, bcol_psum, bdiag_ready = m.sem("b_exped"), m.sem("batt_ready"), m.sem("bcol_psum"), m.sem("bdiag_ready")
        q2c_psum, cq_ready, z_psum = m.sem("q2c_psum"), m.sem("cq_ready"), m.sem("z_psum")
        xt_psum, xt_ready, gate_psum, kept = m.sem("xt_psum"), m.sem("xt_ready"), m.sem("gate_psum"), m.sem("kept")
        experts_loaded, cleared, pool_passed = m.sem("experts_loaded"), m.sem("cleared"), m.sem("pool_passed")
        dve_order, dve_passed, pe_passed = m.sem("dve_order"), m.sem("dve_passed"), m.sem("pe_passed")
        W_LOADS = 11

        x_dram, q_dram = rows(T["x"]), rows(T["ctx_1024"])

        block = ctx.enter_context(nc.Block())

        @block.sync
        def _(sp):
            def load(g, par):
                sp.dma_start(X[:, ds(GT * g, GT), :], x_dram[:, ds(GT * g, GT), :]).then_inc(loaded[par], 16)
                sp.dma_start(q_rows[par][:], q_dram[:, ds(GT * g, GT), :]).then_inc(loaded[par], 16)

            load(0, 0)
            sp.dma_start(w_cq[:], column(T["L0_xattn_w_cq"])).then_inc(w_loaded, 16)
            sp.dma_start(w_q[:], column(T["L0_xattn_w_q"])).then_inc(w_loaded, 16)
            sp.dma_start(w_c[:], column(T["L0_xattn_w_c"])).then_inc(w_loaded, 16)
            for n, name in enumerate(("L0_xattn_b_cq", "L0_xattn_b_c", "L0_xattn_b_q")):
                sp.dma_start(biases[:, n:n + 1], T[name].partition_broadcast(P)).then_inc(w_loaded, 16)
            sp.dma_start(b_l[:], T["L0_xattn_b_l"].partition_broadcast(P)).then_inc(w_loaded, 16)
            sp.dma_start(wl_rows[:], T["L0_xattn_W_l"]).then_inc(w_loaded, 16)
            sp.dma_start(gate_w[:], T["L0_ffn_gate_w"]).then_inc(w_loaded, 16)
            sp.dma_start(gate_b[:], T["L0_ffn_gate_b"].partition_broadcast(P)).then_inc(w_loaded, 16)
            load(1, 1)
            with sp.Fori(0, G // 2 - 1) as i:
                for par in range(2):
                    sp.wait_ge(c2q_psum, 2 * i + par + 1)
                    load(2 * i + 2 + par, par)
            w1_all, w2_all = experts
            E = w1_all.shape[1]
            HC = T["L0_ffn_w1"].shape[2] // P
            sp.dma_start(w1_all[:, :, 0:HC * P], T["L0_ffn_w1"].rearrange("e d h -> d e h")).then_inc(experts_loaded, 16)
            sp.dma_start(w2_all[:], T["L0_ffn_w2"].rearrange("e (j p) d -> p (e j) d", p=P)).then_inc(experts_loaded, 16)
            with nc.allow_non_contiguous_dma("biases, one per partition"):
                for e in range(E):
                    sp.dma_start(w1_all[:, e, HC * P:HC * P + HC], T["L0_ffn_b1"][e].rearrange("(j p) -> p j", p=P)).then_inc(experts_loaded, 16)
            sp.dma_start(w1_all[:, :, HC * P + HC:], T["L0_ffn_b2"].partition_broadcast(P)).then_inc(experts_loaded, 16)
            sp.wait_ge(zeros_set, 4)
            rest = sorted_x.rearrange("(p n) d -> p (n d)", p=P)
            for n in range(rest.shape[1] // 1136):
                sp.dma_start(rest[:, n * 1136:(n + 1) * 1136], zeros[:]).then_inc(cleared, 16)
            sp.wait_ge(experts_loaded, 16 * (3 + E))
            sp.wait_ge(cleared, 16 * (rest.shape[1] // 1136))

        def turns(engine, body):
            body(0, -2, True, False, False)
            body(0, -1, True, True, False)
            with engine.Fori(0, G // 2 - 1) as i:
                body(i, 0, True, True, True)
                body(i, 1, True, True, True)
            body(0, G - 2, False, True, True)
            body(0, G - 1, False, False, True)

        @block.gpsimd
        def _(pool):
            pool.memset(ident[:], 0.0).then_inc(masks_set, 1)
            pool.wait_ge(masks_set, 1)
            pool.affine_select(out=ident[:], in_=ident[:], compare_op=ALU.not_equal, fill=1.0, base=0,
                               pattern=[[-1, P]], channel_multiplier=1).then_inc(masks_set, 1)
            pool.memset(minus_half[:], -0.5).then_inc(zeros_set, 1)
            pool.memset(a_diag[:], 0.0).then_inc(zeros_set, 1)
            pool.memset(b_diag[:], 0.0).then_inc(zeros_set, 1)
            pool.wait_ge(zeros_set, 3)

            def body(i, c, s1, s2, s3):
                n = 2 * i + c
                if s1:
                    pool.wait_ge(var1_ready, n + 3)
                    pool.tensor_tensor(rstd1[:], var1[:], minus_half[:], ALU.pow).then_inc(rstd1_ready, 1)
                    if isinstance(n, int) and n == -2:
                        pool.memset(zeros[:], 0.0).then_inc(zeros_set, 1)
                if s3:
                    pool.wait_ge(var2_ready, n + 1)
                    pool.tensor_tensor(rstd2[:], var2[:], minus_half[:], ALU.pow).then_inc(rstd2_ready, 1)
                    wait_alone(pool, xnorm_ready, GT * (n + 1), pool_passed)
                    pool.tensor_copy(XN2[:, ds(GT * n, GT), :], xn_rows[:]).then_inc(kept, 1)

            turns(pool, body)

        @block.scalar
        def _(act):
            act.wait_ge(wl_transposed, 1)
            act.copy(wl_t[:].rearrange("p a b -> p (a b)"), ps_z[:]).then_inc(wl_copied, 1)

            def body(i, c, s1, s2, s3):
                n = 2 * i + c
                if s2:
                    act.wait_ge(s_shifted, n + 2)
                    act.activation(weights[:], scores[:], ACT.Exp).then_inc(s_exp, 1)
                    act.wait_ge(b_shifted, n + 2)
                    act.activation(b_exp[:], b_shift[:], ACT.Exp).then_inc(b_exped, 1)
                if s1:
                    act.wait_ge(ct_psum, 2 * (n + 2) + 1)
                    act.copy(c_t[c % 2][:], ps_c[:]).then_inc(ct_ready, 1)
                    act.wait_ge(ct_psum, 2 * (n + 2) + 2)
                    act.copy(q_t[:], ps_q[:]).then_inc(ct_ready, 1)
                if s2:
                    act.wait_ge(at_psum, n + 2)
                    act.copy(a_t[:], ps_a[:]).then_inc(at_ready, 1)
                    act.wait_ge(c2q_psum, n + 2)
                    act.copy(c2q_t[:], ps_c2q[:]).then_inc(c2q_ready, 1)
                if s3:
                    act.wait_ge(xt_psum, n + 1)
                    act.copy(xn_t[:], ps_x[:]).then_inc(xt_ready, 1)
                    act.copy(XN2T[:, ds(GT * n, GT), :].rearrange("p a b -> p (a b)"), ps_x[:]).then_inc(xt_ready, 1)

            turns(act, body)

        @block.vector
        def _(dve):
            dve.wait_ge(w_loaded, 16 * (W_LOADS - 1))
            dve.wait_ge(zeros_set, 3)
            dve.tensor_reduce(bias_sum[:], biases[:], AX.X, ALU.add).then_inc(dve_order, 1)

            def statistics(step, x_of, var, var_ready):
                for k in range(GT - 1):
                    dve.bn_stats(stats[:, k, :], x_of(k))
                step(dve.bn_stats(stats[:, GT - 1, :], x_of(GT - 1)), True)
                for k in range(GT - 1):
                    dve.bn_aggr(mv[:, k, :], stats[:, k, :])
                step(dve.bn_aggr(mv[:, GT - 1, :], stats[:, GT - 1, :]))
                dve.tensor_scalar(var[:], mv[:, :, 1], LN_EPS, None, ALU.add).then_inc(var_ready, 1)

            def normalise(x_of, rstd, out, norm_ready):
                for k in range(GT):
                    dve.tensor_scalar(out[:, k, :], x_of(k), mv[:, k, 0:1], rstd[:, k:k + 1],
                                      ALU.subtract, ALU.mult).then_inc(norm_ready, 1)

            STEPS1, STEPS2, STEPS3 = 2, 6, 5

            def body(i, c, s1, s2, s3):
                n = 2 * i + c
                par = c % 2
                start = 1 + (n + 2) * STEPS1 + (n + 1) * STEPS2 + n * STEPS3
                if isinstance(n, int):
                    start = 1 + min(n + 2, G) * STEPS1 + max(n + 1, 0) * STEPS2 + max(n, 0) * STEPS3
                chain = Chain(dve, dve_order, start, dve_passed)

                def x_of(group):
                    return lambda k: X[:, ds(GT * group + k, 1), :].rearrange("p a b -> p (a b)")

                if s3:
                    dve.wait_ge(c2q_ready, n + 1)
                    dve.tensor_tensor(cc_t[:], c2q_t[:], c_t[par][:], ALU.mult).then_inc(cc_ready, 1)
                    dve.wait_ge(q2c_psum, n + 1)
                    dve.tensor_tensor(cq_t[:].rearrange("p (n c) -> p n c", c=S), c_t[par][:].rearrange("p (n c) -> p n c", c=S),
                                      ps_m[:, M_Q2C:M_Q2C + GT * NB].unsqueeze(2).to_broadcast([P, GT * NB, S]),
                                      ALU.mult).then_inc(cq_ready, 1)
                if s2:
                    dve.wait_ge(s_psum, n + 2)
                    s_view = ps_s[:, 0:GT * S].rearrange("p (k q) -> p k q", q=S)
                    chain.step(dve.tensor_reduce(row_max[:], s_view, AX.X, ALU.max))
                    dve.scalar_tensor_tensor(s_max[:], ps_s[:, GT * S:GT * S + GT], bias_sum[:, 0:1], row_max[:],
                                             ALU.add, ALU.add).then_inc(smax_ready, 1)
                    dve.tensor_tensor(scores[:], s_view, row_max[:].unsqueeze(2).to_broadcast([P, GT, S]),
                                      ALU.subtract).then_inc(s_shifted, 1)
                if s1:
                    wait_alone(dve, loaded[par], 32 * (i + (c + 2) // 2 + 1), dve_passed)
                    statistics(chain.step, x_of(n + 2), var1, var1_ready)
                if s2:
                    dve.wait_ge(mrow_psum, n + 2)
                    m_view = ps_m[0:GT, M_ROW:M_ROW + P].rearrange("p (b c) -> p b c", c=S)
                    chain.step(dve.tensor_reduce(bm[:], m_view, AX.X, ALU.max))
                    dve.tensor_tensor(b_shift[:].rearrange("p (b c) -> p b c", c=S), m_view,
                                      bm[:].unsqueeze(2).to_broadcast([GT, NB, S]), ALU.subtract).then_inc(b_shifted, 1)
                if s1:
                    dve.wait_ge(rstd1_ready, n + 3)
                    normalise(x_of(n + 2), rstd1, c_rows[par], cnorm_ready)
                if s2:
                    dve.wait_ge(s_exp, n + 2)
                    chain.step(dve.tensor_reduce(row_sum[:], weights[:], AX.X, ALU.add))
                    chain.step(dve.reciprocal(row_rec[:], row_sum[:]))
                    for b in range(NB):
                        h = slice(b * S, b * S + S)
                        dve.tensor_tensor(a_diag[h, :, h], weights[h], row_rec[h].unsqueeze(2).to_broadcast([S, GT, S]),
                                          ALU.mult).then_inc(a_ready, 1)
                if s3:
                    dve.wait_ge(z_psum, n + 1)
                    x_g = X[:, ds(GT * n, GT), :]
                    chain.step(dve.tensor_tensor(x_g, ps_z[:].rearrange("p (k d) -> p k d", d=D), x_g, ALU.add))
                    chain.step(dve.tensor_tensor(x_g, x_g, b_l[:].unsqueeze(1).to_broadcast([P, GT, D]), ALU.add), True)
                    statistics(chain.step, x_of(n), var2, var2_ready)
                if s2:
                    dve.wait_ge(b_exped, n + 2)
                    b_view = b_exp[:].rearrange("p (b c) -> p b c", c=S)
                    chain.step(dve.tensor_reduce(bsum[:], b_view, AX.X, ALU.add))
                    chain.step(dve.reciprocal(brec[:], bsum[:]))
                    dve.tensor_tensor(b_att[:].rearrange("p (b c) -> p b c", c=S), b_view,
                                      brec[:].unsqueeze(2).to_broadcast([GT, NB, S]), ALU.mult).then_inc(batt_ready, 1)
                if s3:
                    dve.wait_ge(rstd2_ready, n + 1)
                    normalise(x_of(n), rstd2, xn_rows, xnorm_ready)
                if s1:
                    dve.wait_ge(ct_ready, 2 * (n + 2) + 1)
                    dve.tensor_scalar(cw_t[:], c_t[par][:], w_cq[:, 0:1], w_q[:, 0:1], ALU.mult, ALU.add).then_inc(cw_ready, 1)
                if s2:
                    dve.wait_ge(bcol_psum, n + 2)
                    for b in range(NB):
                        h = slice(b * S, b * S + S)
                        dve.tensor_copy(b_diag[h, :, b], ps_m[h, M_COL:M_COL + GT]).then_inc(bdiag_ready, 1)
                if s3:
                    dve.wait_ge(gate_psum, n + 1)
                    chain.step(dve.tensor_tensor(LG[:, ds(GT * n, GT), :],
                                                 ps_m[:, M_GATE:M_GATE + GT * 8].rearrange("p (k e) -> p k e", e=8),
                                                 gate_b[:].unsqueeze(1).to_broadcast([P, GT, 8]), ALU.add))
                assert chain.n == STEPS1 * s1 + STEPS2 * s2 + STEPS3 * s3, chain.n

            turns(dve, body)

        @block.tensor
        def _(pe):
            pe.wait_ge(masks_set, 2)
            pe.wait_ge(w_loaded, 16 * (W_LOADS - 1))
            for j in range(4):
                last = pe.transpose(ps_z[:, j * P:(j + 1) * P], wl_rows[:, j * D:(j + 1) * D], ident[:])
            last.then_inc(wl_transposed, 1)
            pe.wait_ge(wl_copied, 1)

            def body(i, c, s1, s2, s3):
                n = 2 * i + c
                par = c % 2
                if s2:
                    pe.wait_ge(smax_ready, n + 2)
                    pe.transpose(ps_m[0:GT, M_ROW:M_ROW + P], s_max[:], ident[:]).then_inc(mrow_psum, 1)
                if s3:
                    pe.wait_ge(c2q_ready, n + 1)
                    pe.wait_ge(cc_ready, n + 1)
                    pe.wait_ge(cq_ready, n + 1)
                    for k in range(GT):
                        for j, part in enumerate((c_t[par], c2q_t, cc_t, cq_t)):
                            last = pe.matmul(ps_z[:, k * D:(k + 1) * D], part[:, k * P:(k + 1) * P], wl_t[:, j, :],
                                             start=(j == 0), stop=(j == 3))
                    last.then_inc(z_psum, 1)
                if s1:
                    pe.wait_ge(loaded[par], 32 * (i + (c + 2) // 2 + 1))
                    for k in range(GT):
                        pe.wait_ge(cnorm_ready, GT * (n + 2) + k + 1)
                        last = pe.transpose(ps_c[:, k * P:(k + 1) * P], c_rows[par][:, k, :], ident[:])
                    last.then_inc(ct_psum, 1)
                    for k in range(GT):
                        last = pe.transpose(ps_q[:, k * P:(k + 1) * P], q_rows[par][:, k, :], ident[:])
                    last.then_inc(ct_psum, 1)
                if s2:
                    pe.wait_ge(a_ready, NB * (n + 2))
                    for k in range(GT):
                        last = pe.transpose(ps_a[:, k * P:(k + 1) * P], a_diag[:, k, :], ident[:])
                    last.then_inc(at_psum, 1)
                    wait_alone(pe, batt_ready, n + 2, pe_passed)
                    pe.transpose(ps_m[:, M_COL:M_COL + GT], b_att[:], ident[0:GT, 0:GT]).then_inc(bcol_psum, 1)
                    pe.wait_ge(at_ready, n + 2)
                    for k in range(GT):
                        last = pe.matmul(ps_c2q[:, k * P:(k + 1) * P], q_rows[1 - par][:, k, :], a_t[:, k * P:(k + 1) * P],
                                         start=True, stop=True)
                    last.then_inc(c2q_psum, 1)
                if s3:
                    for k in range(GT):
                        pe.wait_ge(xnorm_ready, GT * n + k + 1)
                        last = pe.transpose(ps_x[:, k * P:(k + 1) * P], xn_rows[:, k, :], ident[:])
                    last.then_inc(xt_psum, 1)
                if s1:
                    pe.wait_ge(ct_ready, 2 * (n + 2) + 2)
                    for k in range(GT):
                        last = pe.matmul(ps_s[:, GT * S + k:GT * S + k + 1], c_t[par][:, k * P:(k + 1) * P], w_c[:, 0:1],
                                         start=True, stop=True)
                    wait_alone(pe, cw_ready, n + 3, pe_passed)
                    for k in range(GT):
                        for b in range(NB):
                            o = k * P + b * S
                            last = pe.matmul(ps_s[b * S:b * S + S, k * S:(k + 1) * S], cw_t[:, o:o + S], q_t[:, o:o + S],
                                             start=True, stop=True)
                    last.then_inc(s_psum, 1)
                if s2:
                    pe.wait_ge(bdiag_ready, NB * (n + 2))
                    for k in range(GT):
                        last = pe.matmul(ps_m[:, M_Q2C + NB * k:M_Q2C + NB * (k + 1)], c_rows[1 - par][:, k, :], b_diag[:, k, :],
                                         start=True, stop=True)
                    last.then_inc(q2c_psum, 1)
                if s3:
                    pe.wait_ge(xt_ready, 2 * n + 2)
                    for k in range(GT):
                        last = pe.matmul(ps_m[:, M_GATE + 8 * k:M_GATE + 8 * (k + 1)], xn_t[:, k * P:(k + 1) * P],
                                         gate_w[:], start=True, stop=True)
                    last.then_inc(gate_psum, 1)

            turns(pe, body)


def phase_r(nc, T, X, XN2, XN2T, LG, w_first, w_second, slot_of, expert_of, sorted_x, SLOTS, N_SORTED):
    NT, E = LG.shape[1], LG.shape[2]
    G = NT // GT
    H = 512
    HC = H // P
    MAX_TILES = NT * P // SLOTS
    with ExitStack() as ctx:
        m = Space(nc, ctx, "r")
        above, ties = m.sb("above", [P, NT * E, E]), m.sb("ties", [P, NT * E, E])
        before = m.sb("before", [P, E, E])
        rank, first, second = (m.sb(n, [P, NT, E]) for n in ("rank", "first", "second"))
        tmp = above[:, 0:NT, :]
        passed_ends = above[:, NT:NT + N_SORTED, :]
        running = ties[:, 0:NT, :].rearrange("p t e -> p (t e)").rearrange("p (e t) -> p e t", e=E)
        v1, v2, diff, ratio, den = (m.sb(n, [P, NT]) for n in ("v1", "v2", "diff", "ratio", "den"))
        chosen, going_on = (m.sb(n, [P, E, NT]) for n in ("chosen", "going_on"))
        lower, ones = m.sb("lower", [P, P]), m.sb("ones", [P, P])
        counts = m.sb("counts", [P, E])
        limits, more = m.sb("limits", [P, MAX_TILES]), m.sb("more", [P, E, MAX_TILES])
        tiles, ends, base = m.sb("tiles", [P, E]), m.sb("ends", [P, E]), m.sb("base", [P, E])
        numbers = m.sb("numbers", [P, N_SORTED])
        owner, slot = m.sb("owner", [P, N_SORTED]), m.sb("slot", [P, 2, NT])
        w1, w2 = m.sb("w1", [P, H]), m.sb("w2", [P, HC, D])
        b1, b2 = m.sb("b1", [P, HC]), m.sb("b2", [P, D])
        h_t = [m.sb(f"h_t{i}", [P, HC, GW]) for i in range(2)]
        ps_h = [m.ps(f"ps_h{j}", [P, GW]) for j in range(HC)]
        ps_y = [m.ps(f"ps_y{i}", [P, GW]) for i in range(2)]
        ps_r = m.ps("ps_r", [P, 512])

        constants, diff_ready, ratio_ready, order = m.sem("constants"), m.sem("diff_ready"), m.sem("ratio_ready"), m.sem("order")
        counts_ready, sums_psum, slots_ready, scattered = m.sem("counts_ready"), m.sem("sums_psum"), m.sem("slots_ready"), m.sem("scattered")
        w_loaded, h_psum, h_ready, y_psum, x_added = (m.sem(n) for n in ("w_loaded", "h_psum", "h_ready", "y_psum", "x_added"))
        x_order = m.sem("x_order")
        block = ctx.enter_context(nc.Block())

        @block.sync
        def _(sp):
            sp.dma_start(w1[:], T["L0_ffn_ws1"]).then_inc(w_loaded, 16)
            sp.dma_start(w2[:], T["L0_ffn_ws2"].rearrange("(j p) d -> p j d", p=P)).then_inc(w_loaded, 16)
            with nc.allow_non_contiguous_dma("512 biases, one per partition"):
                sp.dma_start(b1[:], T["L0_ffn_bs1"].rearrange("(j p) -> p j", p=P)).then_inc(w_loaded, 16)
            sp.dma_start(b2[:], T["L0_ffn_bs2"].partition_broadcast(P)).then_inc(w_loaded, 16)

        @block.gpsimd
        def _(pool):
            pool.memset(before[:], 1.0).then_inc(constants, 1)
            pool.memset(lower[:], 1.0).then_inc(constants, 1)
            pool.memset(ones[:], 1.0).then_inc(constants, 1)
            pool.memset(going_on[:], 1.0).then_inc(constants, 1)
            pool.wait_ge(constants, 4)
            pool.affine_select(out=before[:], in_=before[:], compare_op=ALU.is_gt, fill=0.0, base=0,
                               pattern=[[1, E], [-1, E]], channel_multiplier=0).then_inc(constants, 1)
            pool.affine_select(out=lower[:], in_=lower[:], compare_op=ALU.is_gt, fill=0.0, base=0,
                               pattern=[[1, P]], channel_multiplier=-1).then_inc(constants, 1)
            pool.memset(going_on[:, :, 0:1], 0.0).then_inc(constants, 1)
            pool.iota(limits[:], pattern=[[SLOTS, MAX_TILES]], base=0, channel_multiplier=0,
                      allow_small_or_imprecise_dtypes=True).then_inc(constants, 1)
            pool.iota(numbers[:], pattern=[[1, N_SORTED]], base=0, channel_multiplier=0,
                      allow_small_or_imprecise_dtypes=True).then_inc(constants, 1)
            pool.wait_ge(slots_ready, 1)
            for t in range(NT):
                for choice in range(2):
                    pool.indirect_dma_start(out=sorted_x, out_offset=bass.IndirectOffsetOnAxis(ap=slot_of[:, choice, t:t + 1], axis=0),
                                            in_=XN2[:, t, :], in_offset=None).then_inc(scattered, 16)
            pool.wait_ge(scattered, 16 * 2 * NT)

        def shared(engine, body):
            for g in range(2):
                body(g, g)

        @block.tensor
        def _(pe):
            def up(g, first=False):
                for j in range(HC):
                    if not first:
                        pe.wait_ge(h_ready, HC * (g - 1) + j + 1)
                    pe.matmul(ps_h[j][:], w1[:, j * P:(j + 1) * P],
                              XN2T[:, ds(GT * g, GT), :].rearrange("p a b -> p (a b)"), start=True, stop=True).then_inc(h_psum, 1)

            def down(g, par, first=False):
                pe.wait_ge(h_ready, HC * (g + 1))
                if not first:
                    pe.wait_ge(x_added, g - 1)
                for k in range(GT):
                    for j in range(HC):
                        last = pe.matmul(ps_y[par][:, k * D:(k + 1) * D], h_t[par][:, j, k * P:(k + 1) * P], w2[:, j, :],
                                         start=(j == 0), stop=(j == HC - 1))
                last.then_inc(y_psum, 1)

            pe.wait_ge(w_loaded, 64)
            up(0, True)
            up(1)
            down(0, 0, True)
            up(2)
            down(1, 1, True)
            pe.wait_ge(constants, 6)
            pe.wait_ge(counts_ready, 1)
            pe.matmul(ps_r[:, 0:E], lower[:], counts[:], start=True, stop=True)
            pe.matmul(ps_r[:, E:2 * E], ones[:], counts[:], start=True, stop=True).then_inc(sums_psum, 1)
            with pe.Fori(1, G // 2 - 1) as i:
                up(2 * i + 1)
                down(2 * i, 0)
                up(2 * i + 2)
                down(2 * i + 1, 1)
            up(G - 1)
            down(G - 2, 0)
            down(G - 1, 1)

        @block.scalar
        def _(act):
            def gelu(g, par, first=False):
                if not first:
                    act.wait_ge(y_psum, g - 1)
                for j in range(HC):
                    act.wait_ge(h_psum, HC * g + j + 1)
                    act.activation(h_t[par][:, j, :], ps_h[j][:], ACT.Gelu, bias=b1[:, j:j + 1]).then_inc(h_ready, 1)

            act.wait_ge(w_loaded, 64)
            gelu(0, 0, True)
            gelu(1, 1, True)
            gelu(2, 0)
            with act.Fori(1, G // 2 - 1) as i:
                gelu(2 * i + 1, 1)
                gelu(2 * i + 2, 0)
            gelu(G - 1, 1)
            act.wait_ge(diff_ready, 1)
            act.activation(ratio[:], diff[:], ACT.Exp).then_inc(ratio_ready, 1)

        @block.vector
        def _(dve):
            chain = Chain(dve, order, 0)
            step = chain.step
            lg_j = LG[:].unsqueeze(2).to_broadcast([P, NT, E, E])
            lg_e = LG[:].unsqueeze(3).to_broadcast([P, NT, E, E])
            a4 = above[:].rearrange("p (t e) j -> p t e j", e=E)
            t4 = ties[:].rearrange("p (t e) j -> p t e j", e=E)

            def add(g, par):
                dve.wait_ge(y_psum, g + 1)
                x_g = X[:, ds(GT * g, GT), :]
                dve.tensor_tensor(x_g, x_g, ps_y[par][:].rearrange("p (k d) -> p k d", d=D), ALU.add).then_inc(x_added, 1)
                dve.wait_ge(x_added, g + 1)
                dve.tensor_tensor(x_g, x_g, b2[:].unsqueeze(1).to_broadcast([P, GT, D]), ALU.add).then_inc(x_order, 1)

            dve.wait_ge(constants, 9)
            dve.tensor_tensor(a4, lg_j, lg_e, ALU.is_gt)
            step(dve.tensor_tensor(t4, lg_j, lg_e, ALU.is_equal))
            step(dve.tensor_tensor(t4, t4, before[:].unsqueeze(1).to_broadcast([P, NT, E, E]), ALU.mult))
            step(dve.tensor_tensor(above[:], above[:], ties[:], ALU.add))
            step(dve.tensor_reduce(rank[:].rearrange("p t e -> p (t e)"), above[:], AX.X, ALU.add))
            step(dve.tensor_scalar(chosen[:].rearrange("p e t -> p t e"), rank[:], 2.0, None, ALU.is_lt))
            dve.tensor_reduce(counts[:], chosen[:], AX.X, ALU.add).then_inc(counts_ready, 1)
            dve.wait_ge(w_loaded, 64)
            add(0, 0)
            add(1, 1)
            step(dve.tensor_tensor_scan(running.rearrange("p e t -> p (e t)"), going_on[:].rearrange("p e t -> p (e t)"),
                                        chosen[:].rearrange("p e t -> p (e t)"), 0.0, ALU.mult, ALU.add))
            dve.wait_ge(sums_psum, 1)
            step(dve.tensor_tensor(more[:], ps_r[:, E:2 * E].unsqueeze(2).to_broadcast([P, E, MAX_TILES]),
                                   limits[:].unsqueeze(1).to_broadcast([P, E, MAX_TILES]), ALU.is_gt))
            step(dve.tensor_reduce(tiles[:], more[:], AX.X, ALU.add))
            step(dve.tensor_tensor_scan(ends[:], ones[:, 0:E], tiles[:], 0.0, ALU.mult, ALU.add))
            step(dve.tensor_tensor(base[:], ends[:], tiles[:], ALU.subtract))
            step(dve.tensor_scalar(base[:], base[:], float(SLOTS), -1.0, ALU.mult, ALU.add))
            step(dve.tensor_tensor(base[:], base[:], ps_r[:, 0:E], ALU.add))
            step(dve.tensor_tensor(running, running, base[:].unsqueeze(2).to_broadcast([P, E, NT]), ALU.add))
            for choice, mask in enumerate((first, second)):
                step(dve.tensor_scalar(mask[:], rank[:], float(choice), None, ALU.is_equal))
                step(dve.tensor_tensor(tmp, mask[:], running.rearrange("p e t -> p t e"), ALU.mult))
                step(dve.tensor_reduce(slot[:, choice, :], tmp, AX.X, ALU.add))
            dve.tensor_copy(slot_of[:], slot[:]).then_inc(slots_ready, 1)
            step(dve.tensor_tensor(passed_ends, ends[:].unsqueeze(1).to_broadcast([P, N_SORTED, E]),
                                   numbers[:].unsqueeze(2).to_broadcast([P, N_SORTED, E]), ALU.is_le))
            step(dve.tensor_reduce(owner[:], passed_ends, AX.X, ALU.add))
            step(dve.tensor_scalar(expert_of[:], owner[:], float(E - 1), None, ALU.min))
            for value, mask in ((v1, first), (v2, second)):
                step(dve.tensor_tensor(tmp, mask[:], LG[:], ALU.mult))
                step(dve.tensor_reduce(value[:], tmp, AX.X, ALU.add))
            dve.tensor_tensor(diff[:], v2[:], v1[:], ALU.subtract).then_inc(diff_ready, 1)
            with dve.Fori(1, G // 2) as i:
                for par in range(2):
                    add(2 * i + par, par)
            dve.wait_ge(ratio_ready, 1)
            step(dve.tensor_scalar(den[:], ratio[:], 1.0, None, ALU.add))
            step(dve.reciprocal(w_first[:], den[:]))
            step(dve.tensor_tensor(w_second[:], w_first[:], ratio[:], ALU.mult))


def phase_d(nc, T, experts, expert_of, sorted_x, sorted_y, ident, SLOTS, N_SORTED):
    w1_all, w2_all = experts
    E = w1_all.shape[1]
    HC = w2_all.shape[1] // E
    W1 = w1_all.shape[2]
    K = SLOTS // P
    RX, RY, RW = 4, 4, 4
    with ExitStack() as ctx:
        m = Space(nc, ctx, "d")
        x_rows = [m.sb(f"x_rows{i}", [P, K, D]) for i in range(RX)]
        y_rows = [m.sb(f"y_rows{i}", [P, K, D]) for i in range(RY)]
        x_t = [m.sb(f"x_t{i}", [P, SLOTS]) for i in range(2)]
        w1 = [m.sb(f"w1_{i}", [P, W1]) for i in range(RW)]
        h_t = [m.sb(f"h_t{i}", [P, HC, SLOTS]) for i in range(2)]
        ps_h = [m.ps(f"ps_h{j}", [P, 512]) for j in range(HC)]
        ps_y = [m.ps(f"ps_y{i}", [P, 512]) for i in range(2)]
        ps_x = [m.ps(f"ps_x{i}", [P, 512]) for i in range(2)]
        loaded = [m.sem(f"loaded{i}") for i in range(RX)]
        stored = [m.sem(f"stored{i}") for i in range(RY)]
        xt_psum, xt_ready, w1_ready = m.sem("xt_psum"), m.sem("xt_ready"), m.sem("w1_ready")
        h_psum, h_ready, y_psum, y_ready = m.sem("h_psum"), m.sem("h_ready"), m.sem("y_psum"), m.sem("y_ready")
        U = 4
        PEEL = 2 * U - (-N_SORTED) % U if N_SORTED % U else U
        PEEL = U + N_SORTED % U
        TURNS = (N_SORTED - PEEL) // U
        x_dram = sorted_x.rearrange("(n k p) d -> n p k d", k=K, p=P)
        y_dram = sorted_y.rearrange("(n k p) d -> n p k d", k=K, p=P)

        def tiles(engine, body):
            for n in range(PEEL):
                body(0, n)
            with engine.Fori(0, TURNS) as i:
                for c in range(U):
                    body(i, PEEL + c)

        block = ctx.enter_context(nc.Block())

        @block.sync
        def _(sp):
            def load(i, c):
                n = U * i + c
                sp.dma_start(x_rows[c % RX][:], x_dram[ds(n, 1)].rearrange("n p k d -> p (n k) d")).then_inc(loaded[c % RX], 16)

            def body(i, c):
                n = U * i + c
                sp.wait_ge(y_ready, n + 1)
                sp.dma_start(y_dram[ds(n, 1)].rearrange("n p k d -> p (n k) d"), y_rows[c % RY][:]).then_inc(stored[c % RY], 16)

            AHEAD = 3
            for n in range(AHEAD):
                load(0, n)
            for n in range(PEEL - AHEAD):
                if n + AHEAD >= RX:
                    sp.wait_ge(xt_psum, n + AHEAD - RX + 1)
                load(0, n + AHEAD)
                body(0, n)
            with sp.Fori(0, TURNS) as i:
                for c in range(U):
                    sp.wait_ge(xt_psum, U * i + PEEL + c - RX + 1)
                    load(i, PEEL + c)
                    body(i, PEEL + c - AHEAD)
            for c in range(U - AHEAD, U):
                body(TURNS - 1, PEEL + c)
            for q in range(RY):
                sp.wait_ge(stored[q], 16 * len([n for n in range(N_SORTED) if n % RY == q]))

        @block.vector
        def _(dve):
            def copy_w1(i, c):
                n = U * i + c
                if not (isinstance(n, int) and n < RW):
                    dve.wait_ge(y_ready, n - RW + 1)
                e = dve.value_load(expert_of[0:1, ds(n, 1)], min_val=0, max_val=E - 1)
                dve.tensor_copy(w1[c % RW][:], w1_all[:, ds(e, 1), :].rearrange("p a b -> p (a b)")).then_inc(w1_ready, 1)

            def take_y(i, c):
                n = U * i + c
                dve.wait_ge(y_psum, n + 1)
                if not (isinstance(n, int) and n < RY):
                    dve.wait_ge(stored[c % RY], 16 * (i + c // RY))
                dve.tensor_tensor(y_rows[c % RY][:], ps_y[c % 2][:, 0:SLOTS].rearrange("p (k d) -> p k d", d=D),
                                  w1[c % RW][:, HC * P + HC:].unsqueeze(1).to_broadcast([P, K, D]), ALU.add).then_inc(y_ready, 1)

            copy_w1(0, 0)
            copy_w1(0, 1)
            for n in range(PEEL - 2):
                copy_w1(0, n + 2)
                take_y(0, n)
            with dve.Fori(0, TURNS) as i:
                for c in range(U):
                    copy_w1(i, PEEL + c)
                    take_y(i, PEEL + c - 2)
            take_y(TURNS - 1, PEEL + U - 2)
            take_y(TURNS - 1, PEEL + U - 1)

        @block.scalar
        def _(act):
            def take_x(i, c):
                n = U * i + c
                act.wait_ge(xt_psum, n + 1)
                act.copy(x_t[c % 2][:], ps_x[c % 2][:, 0:SLOTS]).then_inc(xt_ready, 1)

            def gelu(i, c):
                n = U * i + c
                if not (isinstance(n, int) and n < 2):
                    act.wait_ge(y_psum, n - 1)
                for j in range(HC):
                    act.wait_ge(h_psum, HC * n + j + 1)
                    act.activation(h_t[c % 2][:, j, :], ps_h[j][:, 0:SLOTS], ACT.Gelu,
                                   bias=w1[c % RW][:, HC * P + j:HC * P + j + 1]).then_inc(h_ready, 1)

            take_x(0, 0)
            for n in range(PEEL - 1):
                take_x(0, n + 1)
                gelu(0, n)
            with act.Fori(0, TURNS) as i:
                for c in range(U):
                    take_x(i, PEEL + c)
                    gelu(i, PEEL + c - 1)
            gelu(TURNS - 1, PEEL + U - 1)

        @block.tensor
        def _(pe):
            def transposes(i, c):
                n = U * i + c
                pe.wait_ge(loaded[c % RX], 16 * (i + c // RX + 1))
                if not (isinstance(n, int) and n < 2):
                    pe.wait_ge(xt_ready, n - 1)
                for k in range(K):
                    last = pe.transpose(ps_x[c % 2][:, k * P:(k + 1) * P], x_rows[c % RX][:, k, :], ident[:])
                last.then_inc(xt_psum, 1)

            def up(i, c):
                n = U * i + c
                pe.wait_ge(xt_ready, n + 1)
                pe.wait_ge(w1_ready, n + 1)
                for j in range(HC):
                    if not (isinstance(n, int) and n == 0):
                        pe.wait_ge(h_ready, HC * (n - 1) + j + 1)
                    pe.matmul(ps_h[j][:, 0:SLOTS], w1[c % RW][:, j * P:(j + 1) * P], x_t[c % 2][:], start=True, stop=True).then_inc(h_psum, 1)

            def down(i, c):
                n = U * i + c
                e = pe.value_load(expert_of[0:1, ds(n, 1)], min_val=0, max_val=E - 1)
                pe.wait_ge(h_ready, HC * (n + 1))
                if not (isinstance(n, int) and n < 2):
                    pe.wait_ge(y_ready, n - 1)
                for k in range(K):
                    for j in range(HC):
                        last = pe.matmul(ps_y[c % 2][:, k * D:(k + 1) * D], h_t[c % 2][:, j, k * P:(k + 1) * P],
                                         w2_all[:, ds(e * HC + j, 1), :].rearrange("p a b -> p (a b)"), start=(j == 0), stop=(j == HC - 1))
                last.then_inc(y_psum, 1)

            transposes(0, 0)
            up(0, 0)
            transposes(0, 1)
            for n in range(PEEL - 2):
                transposes(0, n + 2)
                up(0, n + 1)
                down(0, n)
            with pe.Fori(0, TURNS) as i:
                for c in range(U):
                    transposes(i, PEEL + c)
                    up(i, PEEL + c - 1)
                    down(i, PEEL + c - 2)
            up(TURNS - 1, PEEL + U - 1)
            down(TURNS - 1, PEEL + U - 2)
            down(TURNS - 1, PEEL + U - 1)


def phase_c(nc, T, X, w_first, w_second, slot_of, sorted_y, ident, out):
    NT = X.shape[1]
    G = NT // GT
    N_HEADS, DH = T["L1_xattn_wq"].shape[1], T["L1_xattn_wq"].shape[2]
    J = N_HEADS // 2
    H = T["L1_ffn_w1"].shape[1]
    HC = H // P
    Q_SCALE = DH ** -0.5
    with ExitStack() as ctx:
        m = Space(nc, ctx, "c")
        wq, wk = m.sb("wq", [P, J, P]), m.sb("wk", [P, J, P])
        wv = m.sb("wv", [P, 2, J * DH])
        wo = m.sb("wo", [P, J, D])
        f1, f2 = m.sb("f1", [P, H]), m.sb("f2", [P, HC, D])
        fb1, fb2 = m.sb("fb1", [P, HC]), m.sb("fb2", [P, D])
        ctx_rows = m.sb("ctx_rows", [P, GT, D])
        mask = [m.sb(f"mask{i}", [P, GT, S]) for i in range(2)]
        xn_rows, xn4_rows = m.sb("xn_rows", [P, GT, D]), m.sb("xn4_rows", [P, GT, D])
        xn_t, ctx_t = m.sb("xn_t", [P, GW]), m.sb("ctx_t", [P, GW])
        xn4_t = xn_t
        stats, mv = m.sb("stats", [P, GT, 6]), m.sb("mv", [P, GT, 2])
        var, rstd, minus_half = m.sb("var", [P, GT]), m.sb("rstd", [P, GT]), m.sb("minus_half", [P, GT])
        q_t = [m.sb(f"q_t{i}", [P, J, GW]) for i in range(2)]
        k_t = [m.sb(f"k_t{i}", [P, J, GW]) for i in range(2)]
        v_s = [m.sb(f"v_s{i}", [P, GT, NB, J * DH]) for i in range(2)]
        o_t = m.sb("o_t", [P, J, GW])
        shifted = m.sb("shifted", [P, 2, J * S])
        e_s = shifted
        probs = [m.sb(f"probs{i}", [P, J, 2, S]) for i in range(2)]
        r_max, r_sum, r_rec = (m.sb(n, [P, 2 * J]) for n in ("r_max", "r_sum", "r_rec"))
        p_t = [m.sb(f"p_t{i}", [P, J // 2 * P]) for i in range(2)]
        h_t = m.sb("h_t", [P, HC, GW])
        back = m.sb("back", [P, 2, GT, D])

        ps_s = m.ps("ps_s", [P, 2, J * S])
        ps_p = [m.ps(f"ps_p{i}", [P, 512]) for i in range(2)]
        ps_o = [m.ps(f"ps_o{i}", [P, 512]) for i in range(2)]
        ps_w = [m.ps(f"ps_w{i}", [P, 512]) for i in range(2)]

        w_loaded, half_set = m.sem("w_loaded"), m.sem("half_set")
        loaded, mask_loaded = m.sem("loaded"), [m.sem(f"mask_loaded{i}") for i in range(2)]
        var_ready, rstd_ready = m.sem("var_ready"), m.sem("rstd_ready")
        xn_ready, xn4_ready = m.sem("xn_ready"), m.sem("xn4_ready")
        work_full, work_free = m.sem("work_full"), [m.sem(f"work_free{i}") for i in range(2)]
        s_psum, s_taken, s_shifted, s_exp, probs_ready = (m.sem(n) for n in ("s_psum", "s_taken", "s_shifted", "s_exp", "probs_ready"))
        pt_psum, pt_ready, pv_psum, pv_taken = (m.sem(n) for n in ("pt_psum", "pt_ready", "pv_psum", "pv_taken"))
        order, y_ready, passed = m.sem("order"), m.sem("y_ready"), m.sem("passed")
        gathered, added = m.sem("gathered"), m.sem("added")
        stored = [m.sem(f"stored{i}") for i in range(2)]

        x_out, q_dram = rows(out), rows(T["ctx_1024"])
        mask_dram = T["mask_Bx1xSxS2_ff0"].rearrange("b o f t -> (b o f) t").rearrange("(n p) t -> p n t", p=P)

        NQ = J
        USE = {"q": 0, "k": NQ, "o": 2 * NQ, "v": 2 * NQ + 1, "x4": 3 * NQ + 1, "up": 3 * NQ + 2,
               "down": 3 * NQ + 2 + HC, "xt": 3 * NQ + 3 + HC, "ct": 3 * NQ + 4 + HC}
        PER = 3 * NQ + 5 + HC
        FIRST = {"xt0": 0, "ct0": 1, "q": 2, "k": 2 + NQ, "v": 2 + 2 * NQ, "xt1": 2 + 3 * NQ, "ct1": 3 + 3 * NQ}
        N_FIRST = 4 + 3 * NQ
        G0 = {"q": 0, "k": NQ, "v": 2 * NQ, "xt": 3 * NQ, "ct": 3 * NQ + 1}
        N_G0 = 3 * NQ + 2
        BASE = N_FIRST + N_G0 - PER
        LASTG = {"o": 0, "x4": 1, "up": 2, "down": 2 + HC}
        N_BEFORE_LAST = PER - 2

        class Use:

            def __init__(self, i, n):
                self.bank = n % 2
                self.full = 2 * PER * i + n + 1
                self.before = PER * i + n // 2
                self.first = isinstance(self.before, int) and self.before == 0

        def use(i, c, name, j=0):
            if name in FIRST and c == "pro":
                return Use(0, FIRST[name] + j)
            g = 2 * i + c
            if isinstance(g, int) and g == 0:
                return Use(0, N_FIRST + G0[name] + j)
            if isinstance(g, int) and g == G - 1:
                return Use(0, BASE + PER * (G - 2) + PER + N_BEFORE_LAST - PER + LASTG[name] + j)
            if isinstance(g, int) and g == G:
                return Use(0, BASE + PER * (G - 2) + N_BEFORE_LAST + 3 + HC + LASTG[name] + j)
            n = USE[name] + j
            if isinstance(i, int):
                return Use(0, BASE + PER * g + n)
            return Use(i, BASE + PER * c + n)

        def groups(engine, body):
            body(0, 0)
            body(0, 1)
            with engine.Fori(0, (G - 4) // 2) as i:
                for c in (2, 3):
                    body(i, c)
            for c in (2, 3):
                body((G - 4) // 2, c)

        def is_g(i, c, g):
            return isinstance(i, int) and 2 * i + c == g

        def prev_use(i, c, name, j=0):
            if isinstance(i, int):
                return use(0, 2 * i + c - 1, name, j)
            return Use(i, BASE + PER * (c - 1) + USE[name] + j)

        def prev_xt(i, c, which):
            name = ("xt", "ct")[which]
            if is_g(i, c, 0):
                return use(0, "pro", name + "1")
            return prev_use(i, c, name)

        def norm_number(i, c, which):
            g = 2 * i + c
            if isinstance(g, int) and g == 0:
                return 3
            if isinstance(g, int) and g >= G - 2:
                return 3 + 2 * (G - 3) + 1 + (g - (G - 2))
            return 3 + 2 * (g - 1) + (2 if which == "x4" else 1)

        block = ctx.enter_context(nc.Block())

        @block.sync
        def _(sp):
            def load_ctx(g):
                sp.dma_start(ctx_rows[:], q_dram[:, ds(GT * g, GT), :]).then_inc(loaded, 16)

            def load_mask(g, par):
                sp.dma_start(mask[par][:], mask_dram[:, ds(GT * g, GT), :]).then_inc(mask_loaded[par], 16)

            load_ctx(0)
            sp.dma_start(wq[:], T["L1_xattn_wq"].rearrange("d n h -> d (n h)").rearrange("d (j f) -> d j f", f=P)).then_inc(w_loaded, 16)
            sp.dma_start(wk[:], T["L1_xattn_wk"].rearrange("d n h -> d (n h)").rearrange("d (j f) -> d j f", f=P)).then_inc(w_loaded, 16)
            for par in range(2):
                sp.dma_start(wv[:, par, :].rearrange("d (j h) -> d j h", h=DH),
                             T["L1_xattn_wv"].rearrange("d (j a) h -> d j a h", a=2)[:, :, par, :]).then_inc(w_loaded, 16)
            load_mask(0, 0)
            load_mask(1, 1)
            sp.dma_start(wo[:], T["L1_xattn_wo"].rearrange("n h d -> (n h) d").rearrange("(j p) d -> p j d", p=P)).then_inc(w_loaded, 16)
            sp.dma_start(f1[:], T["L1_ffn_w1"]).then_inc(w_loaded, 16)
            sp.dma_start(f2[:], T["L1_ffn_w2"].rearrange("(j p) d -> p j d", p=P)).then_inc(w_loaded, 16)
            with nc.allow_non_contiguous_dma("512 biases, one per partition"):
                sp.dma_start(fb1[:], T["L1_ffn_b1"].rearrange("(j p) -> p j", p=P)).then_inc(w_loaded, 16)
            sp.dma_start(fb2[:], T["L1_ffn_b2"].partition_broadcast(P)).then_inc(w_loaded, 16)

            def store(g, par):
                sp.wait_ge(y_ready, g + 1)
                sp.dma_start(x_out[:, ds(GT * g, GT), :], X[:, ds(GT * g, GT), :]).then_inc(stored[par], 16)

            def body(i, c):
                g = 2 * i + c
                if not is_g(i, c, G - 1) and not is_g(i, c, G - 2):
                    sp.wait_ge(work_full, prev_xt(i, c, 1).full)
                    load_ctx(g + 2)
                    sp.wait_ge(s_taken, GT * (g + 1))
                    load_mask(g + 2, c % 2)
                if not is_g(i, c, 0):
                    store(g - 1, (c + 1) % 2)

            sp.wait_ge(work_full, use(0, "pro", "ct0").full)
            load_ctx(1)
            groups(sp, body)
            store(G - 1, 1)
            for par in range(2):
                sp.wait_ge(stored[par], 16 * G // 2)

        @block.gpsimd
        def _(pool):
            pool.memset(minus_half[:], -0.5).then_inc(half_set, 1)

            def gather(g):
                if g > 0:
                    pool.wait_ge(added, g)
                for k in range(GT):
                    for choice in range(2):
                        pool.indirect_dma_start(out=back[:, choice, k, :], out_offset=None, in_=sorted_y,
                                                in_offset=bass.IndirectOffsetOnAxis(ap=slot_of[:, choice, GT * g + k:GT * g + k + 1], axis=0)
                                                ).then_inc(gathered, 16)

            def root(n):
                pool.wait_ge(var_ready, n)
                pool.tensor_tensor(rstd[:], var[:], minus_half[:], ALU.pow).then_inc(rstd_ready, 1)

            gather(0)
            pool.wait_ge(half_set, 1)
            root(1)
            gather(1)
            root(2)
            gather(2)
            root(3)
            gather(3)
            n = 3
            for g in range(1, G + 1):
                if g + 2 < G:
                    n += 1
                    root(n)
                if g + 3 < G:
                    gather(g + 3)
                n += 1
                root(n)

        @block.tensor
        def _(pe):
            def begin(u):
                if not u.first:
                    pe.wait_ge(work_free[u.bank], u.before)
                return ps_w[u.bank]

            def transposes(u, source):
                w = begin(u)
                for k in range(GT):
                    last = pe.transpose(w[:, k * P:(k + 1) * P], source[:, k, :], ident[:])
                last.then_inc(work_full, 1)

            def prep_t(i, c, g, par, names=("xt", "ct")):
                pe.wait_ge(xn_ready, GT * (g + 1))
                transposes(use(i, c, names[0]), xn_rows)
                pe.wait_ge(loaded, 16 * (g + 1))
                transposes(use(i, c, names[1]), ctx_rows)

            def project(i, c, name, weight, source, source_use):
                pe.wait_ge(work_free[source_use.bank], source_use.before + 1)
                for j in range(J):
                    u = use(i, c, name, j)
                    pe.matmul(begin(u)[:], weight[:, j, :], source[:], start=True, stop=True).then_inc(work_full, 1)

            def project_v(i, c, source_use):
                pe.wait_ge(work_free[source_use.bank], source_use.before + 1)
                for k in range(GT):
                    for par in range(2):
                        u = use(i, c, "v", 2 * k + par)
                        pe.matmul(begin(u)[:], ctx_t[:, k * P:(k + 1) * P], wv[:, par, :], start=True, stop=True).then_inc(work_full, 1)

            def scores(p, k, par, first):
                if not first:
                    wait_alone(pe, s_taken, p, passed)
                for j in range(J):
                    for b in range(NB):
                        for h in range(2):
                            r, o = slice(h * DH, h * DH + DH), k * P + b * S
                            last = pe.matmul(ps_s[b * S:b * S + S, h, j * S:(j + 1) * S], q_t[par][r, j, o:o + S],
                                             k_t[par][r, j, o:o + S], start=True, stop=True)
                last.then_inc(s_psum, 1)

            def transpose_probs(p, k):
                pe.wait_ge(probs_ready, p + 1)
                for half in range(2):
                    if not (isinstance(p, int) and p == 0):
                        pe.wait_ge(pt_ready, 2 * p + half - 1)
                    for jj in range(J // 2):
                        last = pe.transpose(ps_p[half][:, jj * P:(jj + 1) * P],
                                            probs[k % 2][:, half * (J // 2) + jj, :, :].rearrange("p a t -> p (a t)"), ident[:])
                    last.then_inc(pt_psum, 1)

            def values(p, k, par, phase):
                if phase == 0:
                    wait_alone(pe, pt_ready, 2 * (p + 1), passed)
                    if not (isinstance(p, int) and p == 0):
                        wait_alone(pe, pv_taken, 2 * p, passed)
                for jj in range(J // 2):
                    for b in range(NB):
                        for half in range(2):
                            h = (half + phase) % 2
                            j, r, o = half * (J // 2) + jj, slice(h * DH, h * DH + DH), jj * P + b * S
                            last = pe.matmul(ps_o[half][r, o:o + S], v_s[par][r, k, b, j * DH:(j + 1) * DH],
                                             p_t[half][r, o:o + S], start=True, stop=True)
                if phase == 1:
                    last.then_inc(pv_psum, 1)

            def out_projection(i, c, g):
                pe.wait_ge(pv_taken, 2 * GT * (g + 1))
                w = begin(use(i, c, "o"))
                for k in range(GT):
                    for j in range(J):
                        last = pe.matmul(w[:, k * D:(k + 1) * D], o_t[:, j, k * P:(k + 1) * P], wo[:, j, :],
                                         start=(j == 0), stop=(j == J - 1))
                last.then_inc(work_full, 1)

            def x4_transposes(i, c, g):
                pe.wait_ge(xn4_ready, GT * (g + 1))
                transposes(use(i, c, "x4"), xn4_rows)

            def feed_up(i, c):
                u4 = use(i, c, "x4")
                pe.wait_ge(work_free[u4.bank], u4.before + 1)
                for j in range(HC):
                    pe.matmul(begin(use(i, c, "up", j))[:], f1[:, j * P:(j + 1) * P], xn4_t[:], start=True, stop=True).then_inc(work_full, 1)

            def feed_down(i, c):
                for j in (HC - 2, HC - 1):
                    u = use(i, c, "up", j)
                    pe.wait_ge(work_free[u.bank], u.before + 1)
                w = begin(use(i, c, "down"))
                for k in range(GT):
                    for j in range(HC):
                        last = pe.matmul(w[:, k * D:(k + 1) * D], h_t[:, j, k * P:(k + 1) * P], f2[:, j, :],
                                         start=(j == 0), stop=(j == HC - 1))
                last.then_inc(work_full, 1)

            pe.wait_ge(w_loaded, 16 * 9)
            prep_t(0, "pro", 0, 0, ("xt0", "ct0"))
            project(0, "pro", "q", wq, xn_t, use(0, "pro", "xt0"))
            project(0, "pro", "k", wk, ctx_t, use(0, "pro", "ct0"))
            project_v(0, "pro", use(0, "pro", "ct0"))
            prep_t(0, "pro", 1, 1, ("xt1", "ct1"))
            for u in (use(0, "pro", "v", 6), use(0, "pro", "v", 7)):
                pe.wait_ge(work_free[u.bank], u.before + 1)

            def body(i, c):
                g = 2 * i + c
                par = c % 2
                first, last_g = is_g(i, c, 0), is_g(i, c, G - 1)
                prep_next = not last_g
                for k in range(GT):
                    p = GT * g + k
                    if not (first and k == 0):
                        transpose_probs(p - 1, (k - 1) % GT)
                    if k == 0 and not first:
                        for n in (6, 7):
                            u = prev_use(i, c, "v", n)
                            pe.wait_ge(work_free[u.bank], u.before + 1)
                    scores(p, k, par, first and k == 0)
                    if not (first and k == 0):
                        values(p - 1, (k - 1) % GT, par if k else 1 - par, 0)
                    if k == 0 and prep_next:
                        project(i, c, "q", wq, xn_t, prev_xt(i, c, 0))
                    if k == 1 and prep_next:
                        project(i, c, "k", wk, ctx_t, prev_xt(i, c, 1))
                    if k == 1 and not first:
                        out_projection(i, c, g - 1)
                    if k == 2 and prep_next:
                        project_v(i, c, prev_xt(i, c, 1))
                    if k == 2 and not first:
                        x4_transposes(i, c, g - 1)
                    if k == 3 and not first:
                        feed_up(i, c)
                    if not (first and k == 0):
                        values(p - 1, (k - 1) % GT, par if k else 1 - par, 1)
                    if k == 3 and not first:
                        feed_down(i, c)
                    if k == 3 and prep_next and not is_g(i, c, G - 2):
                        prep_t(i, c, g + 2, par)

            groups(pe, body)
            transpose_probs(4 * G - 1, 3)
            values(4 * G - 1, 3, 1, 0)
            values(4 * G - 1, 3, 1, 1)
            out_projection(0, G, G - 1)
            x4_transposes(0, G, G - 1)
            feed_up(0, G)
            feed_down(0, G)

        @block.scalar
        def _(act):
            def take(u, instruction_of):
                act.wait_ge(work_full, u.full)
                instruction_of(ps_w[u.bank]).then_inc(work_free[u.bank], 1)

            def take_t(u, dest):
                take(u, lambda w: act.copy(dest[:], w[:]))

            def take_q(i, c, name, dest, scale, js):
                for j in js:
                    take(use(i, c, name, j), lambda w: act.mul(dest[:, j, :], w[:], scale) if scale != 1.0 else act.copy(dest[:, j, :], w[:]))

            def take_v(i, c, dest, ks=range(GT)):
                for k in ks:
                    for h in range(2):
                        u = use(i, c, "v", 2 * k + h)
                        act.wait_ge(work_full, u.full)
                        for b in range(NB):
                            last = act.copy(dest[h * S:h * S + S, k, b, :], ps_w[u.bank][b * S:b * S + S, :])
                        last.then_inc(work_free[u.bank], 1)

            def take_probs(p):
                for half in range(2):
                    act.wait_ge(pt_psum, 2 * p + half + 1)
                    if not (isinstance(p, int) and p == 0):
                        act.wait_ge(pv_psum, p)
                    act.copy(p_t[half][:], ps_p[half][:]).then_inc(pt_ready, 1)

            def exponentials(p):
                act.wait_ge(s_shifted, p + 1)
                act.activation(e_s[:], shifted[:], ACT.Exp).then_inc(s_exp, 1)

            def take_values(p, k):
                act.wait_ge(pv_psum, p + 1)
                for half in range(2):
                    act.copy(o_t[:, half * (J // 2):(half + 1) * (J // 2), k * P:(k + 1) * P],
                             ps_o[half][:].rearrange("p (j c) -> p j c", c=P)).then_inc(pv_taken, 1)

            def take_hidden(i, c, js=range(HC)):
                for j in js:
                    take(use(i, c, "up", j), lambda w: act.activation(h_t[:, j, :], w[:], ACT.Relu, bias=fb1[:, j:j + 1]))

            act.wait_ge(w_loaded, 16 * 9)
            take_t(use(0, "pro", "xt0"), xn_t)
            take_t(use(0, "pro", "ct0"), ctx_t)
            take_q(0, "pro", "q", q_t[0], Q_SCALE, range(J))
            take_q(0, "pro", "k", k_t[0], 1.0, range(J))
            take_v(0, "pro", v_s[0])
            take_t(use(0, "pro", "xt1"), xn_t)
            take_t(use(0, "pro", "ct1"), ctx_t)

            def body(i, c):
                g = 2 * i + c
                nxt = (c + 1) % 2
                first = is_g(i, c, 0)
                prep_next = not is_g(i, c, G - 1)
                for k in range(GT):
                    p = GT * g + k
                    if not (first and k == 0):
                        take_probs(p - 1)
                    if k == 0 and prep_next:
                        take_q(i, c, "q", q_t[nxt], Q_SCALE, range(0, 3))
                    if k == 1 and prep_next:
                        take_q(i, c, "k", k_t[nxt], 1.0, range(0, 3))
                    if k == 2 and prep_next:
                        take_v(i, c, v_s[nxt], range(0, 1))
                    if k == 3 and not first:
                        take_hidden(i, c, range(0, 2))
                    exponentials(p)
                    if k == 0 and prep_next:
                        take_q(i, c, "q", q_t[nxt], Q_SCALE, range(3, J))
                    if k == 1 and prep_next:
                        take_q(i, c, "k", k_t[nxt], 1.0, range(3, J))
                    if k == 2 and prep_next:
                        take_v(i, c, v_s[nxt], range(2, GT))
                    if k == 2 and not first:
                        take_t(use(i, c, "x4"), xn4_t)
                    if k == 3 and not first:
                        take_hidden(i, c, range(2, HC))
                    if not (first and k == 0):
                        take_values(p - 1, (k - 1) % GT)
                    if k == 3 and prep_next and not is_g(i, c, G - 2):
                        take_t(use(i, c, "xt"), xn_t)
                        take_t(use(i, c, "ct"), ctx_t)

            groups(act, body)
            take_probs(4 * G - 1)
            take_values(4 * G - 1, 3)
            take_t(use(0, G, "x4"), xn4_t)
            take_hidden(0, G)

        @block.vector
        def _(dve):
            state = {"order": 0}

            def step(ins, start, before_stats=False):
                state["order"] += 1
                ins.then_inc(order, 1)
                if before_stats:
                    wait_alone(dve, order, start + state["order"], passed)
                else:
                    dve.wait_ge(order, start + state["order"])

            def add_experts(g, start):
                dve.wait_ge(gathered, 16 * 2 * GT * (g + 1))
                x_g = X[:, ds(GT * g, GT), :]
                for choice, w in enumerate((w_first, w_second)):
                    b = back[:, choice, :, :]
                    step(dve.tensor_tensor(b, b, w[:, ds(GT * g, GT)].unsqueeze(2).to_broadcast([P, GT, D]), ALU.mult), start)
                    ins = dve.tensor_tensor(x_g, x_g, b, ALU.add)
                    if choice == 0:
                        step(ins, start)
                ins.then_inc(added, 1)
                wait_alone(dve, added, g + 1, passed)

            def layernorm(start, g, dest, dest_ready, n):
                def x_of(k):
                    return X[:, ds(GT * g + k, 1), :].rearrange("p a b -> p (a b)")

                for k in range(GT - 1):
                    dve.bn_stats(stats[:, k, :], x_of(k))
                step(dve.bn_stats(stats[:, GT - 1, :], x_of(GT - 1)), start, True)
                for k in range(GT - 1):
                    dve.bn_aggr(mv[:, k, :], stats[:, k, :])
                step(dve.bn_aggr(mv[:, GT - 1, :], stats[:, GT - 1, :]), start)
                dve.tensor_scalar(var[:], mv[:, :, 1], LN_EPS, None, ALU.add).then_inc(var_ready, 1)
                dve.wait_ge(rstd_ready, n)
                for k in range(GT):
                    dve.tensor_scalar(dest[:, k, :], x_of(k), mv[:, k, 0:1], rstd[:, k:k + 1],
                                      ALU.subtract, ALU.mult).then_inc(dest_ready, 1)

            def shift(p, k, par, start):
                dve.wait_ge(s_psum, p + 1)
                s4 = shifted[:].rearrange("p h (j t) -> p h j t", t=S)
                msk = mask[par][:, k, :].unsqueeze(1).to_broadcast([P, 2 * J, S])
                flat = shifted[:].rearrange("p h (j t) -> p (h j) t", t=S)
                ins = dve.tensor_tensor(flat, ps_s[:].rearrange("p h (j t) -> p (h j) t", t=S), msk, ALU.add)
                ins.then_inc(s_taken, 1)
                dve.wait_ge(s_taken, p + 1)
                step(dve.tensor_reduce(r_max[:], flat, AX.X, ALU.max), start)
                dve.tensor_tensor(flat, flat, r_max[:].unsqueeze(2).to_broadcast([P, 2 * J, S]), ALU.subtract).then_inc(s_shifted, 1)

            def normalise(p, k, start):
                dve.wait_ge(s_exp, p + 1)
                e3 = e_s[:].rearrange("p h (j t) -> p (h j) t", t=S)
                step(dve.tensor_reduce(r_sum[:], e3, AX.X, ALU.add), start)
                step(dve.reciprocal(r_rec[:], r_sum[:]), start)
                if not (isinstance(p, int) and p < 2):
                    dve.wait_ge(pt_psum, 2 * (p - 1))
                for h in range(2):
                    ins = dve.tensor_tensor(probs[k % 2][:, :, h, :], e_s[:, h, :].rearrange("p (j t) -> p j t", t=S),
                                            r_rec[:, h * J:(h + 1) * J].unsqueeze(2).to_broadcast([P, J, S]), ALU.mult)
                ins.then_inc(probs_ready, 1)
                dve.wait_ge(probs_ready, p + 1)

            def take_v(i, c, dest, k):
                for h in range(2):
                    u = use(i, c, "v", 2 * k + h)
                    dve.wait_ge(work_full, u.full)
                    for b in range(NB):
                        last = dve.tensor_copy(dest[h * S:h * S + S, k, b, :], ps_w[u.bank][b * S:b * S + S, :])
                    last.then_inc(work_free[u.bank], 1)

            def add_attention(i, c, g, start):
                u = use(i, c, "o")
                dve.wait_ge(work_full, u.full)
                x_g = X[:, ds(GT * g, GT), :]
                dve.tensor_tensor(x_g, x_g, ps_w[u.bank][:].rearrange("p (k d) -> p k d", d=D), ALU.add).then_inc(work_free[u.bank], 1)
                dve.wait_ge(work_free[u.bank], u.before + 1)

            def finish(i, c, g, par, start):
                u = use(i, c, "down")
                dve.wait_ge(work_full, u.full)
                x_g = X[:, ds(GT * g, GT), :]
                dve.tensor_tensor(x_g, x_g, ps_w[u.bank][:].rearrange("p (k d) -> p k d", d=D),
                                  ALU.add).then_inc(work_free[u.bank], 1)
                dve.wait_ge(work_free[u.bank], u.before + 1)
                dve.tensor_tensor(x_g, x_g, fb2[:].unsqueeze(1).to_broadcast([P, GT, D]), ALU.add).then_inc(y_ready, 1)
                dve.wait_ge(y_ready, g + 1)

            ADD = 3
            PRO, O0, OG = 4 + 2 * ADD, 3 * GT + 2 + ADD, 3 * GT + 4 + ADD
            add_experts(0, 0)
            layernorm(0, 0, xn_rows, xn_ready, 1)
            add_experts(1, 0)
            dve.wait_ge(w_loaded, 16 * 9)
            u = use(0, "pro", "xt0")
            dve.wait_ge(work_full, u.full)
            layernorm(0, 1, xn_rows, xn_ready, 2)

            def body(i, c):
                g = 2 * i + c
                first = is_g(i, c, 0)
                par = c % 2
                start = PRO if first else PRO + O0 + OG * (g - 1) - (2 + ADD if is_g(i, c, G - 1) else 0)
                state["order"] = 0
                dve.wait_ge(mask_loaded[par], 16 * (i + c // 2 + 1))
                for k in range(GT):
                    p = GT * g + k
                    shift(p, k, par, start)
                    if k == 2 and not is_g(i, c, G - 1):
                        take_v(i, c, v_s[(c + 1) % 2], 1)
                    normalise(p, k, start)
                    if k == 0 and not is_g(i, c, G - 1) and not is_g(i, c, G - 2):
                        u = prev_xt(i, c, 0)
                        wait_alone(dve, work_full, u.full, passed)
                        add_experts(g + 2, start)
                        layernorm(start, g + 2, xn_rows, xn_ready, norm_number(i, c, "xn"))
                    if k == 1 and not first:
                        add_attention(i, c, g - 1, start)
                        if not is_g(i, c, 1):
                            wait_alone(dve, work_full, prev_use(i, c, "x4").full, passed)
                        layernorm(start, g - 1, xn4_rows, xn4_ready, norm_number(i, c, "x4"))
                    if k == 3 and not first:
                        finish(i, c, g - 1, (c + 1) % 2, start)

            groups(dve, body)
            state["order"] = 0
            start = PRO + O0 + OG * (G - 2) - 2 - ADD + 3 * GT + 2
            add_attention(0, G, G - 1, start)
            dve.wait_ge(work_full, use(0, G - 1, "x4").full)
            layernorm(start, G - 1, xn4_rows, xn4_ready, 2 * G)
            finish(G // 2, 0, G - 1, 1, start)


def build(nc, T, out):
    NT = T["x"].shape[0] * T["x"].shape[1] // P
    E = T["L0_ffn_gate_w"].shape[1]
    HC = T["L0_ffn_w1"].shape[2] // P
    SLOTS = 2 * P
    N_SORTED = (2 * NT * P + E * (SLOTS - 1)) // SLOTS
    sorted_x = nc.dram_tensor("sorted_x", [N_SORTED * SLOTS, D], F32, kind="Internal").ap()
    sorted_y = nc.dram_tensor("sorted_y", [N_SORTED * SLOTS, D], F32, kind="Internal").ap()
    with ExitStack() as ctx:
        m = Space(nc, ctx, "k")
        X, ident = m.sb("X", [P, NT, D]), m.sb("ident", [P, P])
        w_first, w_second = m.sb("w_first", [P, NT]), m.sb("w_second", [P, NT])
        slot_of = m.sb("slot_of", [P, 2, NT], mybir.dt.uint32)
        with ExitStack() as moe:
            m2 = Space(nc, moe, "e")
            expert_of = m2.sb("expert_of", [P, N_SORTED], mybir.dt.int32)
            experts = (m2.sb("w1_all", [P, E, HC * P + HC + D]), m2.sb("w2_all", [P, E * HC, D]))
            with ExitStack() as rest:
                m3 = Space(nc, rest, "f")
                XN2, XN2T, LG = m3.sb("XN2", [P, NT, D]), m3.sb("XN2T", [P, NT, D]), m3.sb("LG", [P, NT, E])
                phase_a(nc, T, X, XN2, XN2T, LG, experts, sorted_x, ident)
                phase_r(nc, T, X, XN2, XN2T, LG, w_first, w_second, slot_of, expert_of, sorted_x, SLOTS, N_SORTED)
            phase_d(nc, T, experts, expert_of, sorted_x, sorted_y, ident, SLOTS, N_SORTED)
        phase_c(nc, T, X, w_first, w_second, slot_of, sorted_y, ident, out)


def kernel(**inputs):
    import numpy as _np
    import concourse.bacc as _bacc
    from concourse import mybir as _mybir
    from concourse.bass_utils import run_bass_kernel_spmd as _run

    nc = _bacc.Bacc("TRN2", target_bir_lowering=False, num_devices=1)
    arrays, tensors = {}, {}
    for name in inputs:
        a = _np.ascontiguousarray(inputs[name])
        arrays[f"in_{name}"] = a
        tensors[name] = nc.dram_tensor(f"in_{name}", a.shape, _mybir.dt.from_np(a.dtype), kind="ExternalInput").ap()
    out = nc.dram_tensor("out", inputs["x"].shape, _mybir.dt.float32, kind="ExternalOutput").ap()
    build(nc, tensors, out)
    r = _run(nc, [arrays], core_ids=[0])
    return r.results[0]["out"]
```

```python
from contextlib import ExitStack

import concourse.bass as bass
from concourse import mybir

ALU = mybir.AluOpType
ACT = mybir.ActivationFunctionType
AX = mybir.AxisListType
F32 = mybir.dt.float32
F32R = mybir.dt.float32r

P = 128
D = 128
S = 64
NB = P // S
GT = 4
GW = GT * P
LN_EPS = 1e-5


def ds(start, size):
    return bass.ds(start, size)


def wait_alone(engine, semaphore, value, passed):
    engine.wait_ge(semaphore, value)
    engine.sem_inc(passed, 1)


class Chain:

    def __init__(self, engine, semaphore, start, passed=None):
        self.engine, self.semaphore, self.start, self.passed, self.n = engine, semaphore, start, passed, 0

    def step(self, instruction, before_stats=False):
        self.n += 1
        instruction.then_inc(self.semaphore, 1)
        if before_stats:
            wait_alone(self.engine, self.semaphore, self.start + self.n, self.passed)
        else:
            self.engine.wait_ge(self.semaphore, self.start + self.n)


class Space:

    def __init__(self, nc, ctx, tag):
        self.nc, self.ctx, self.tag = nc, ctx, tag

    def sb(self, name, shape, dtype=F32):
        return self.ctx.enter_context(self.nc.sbuf_tensor(f"{self.tag}_{name}", shape, dtype))

    def ps(self, name, shape):
        return self.ctx.enter_context(self.nc.psum_tensor(f"{self.tag}_{name}", shape, F32))

    def sem(self, name):
        return self.ctx.enter_context(self.nc.semaphore(f"{self.tag}_{name}"))


def rows(ap):
    return ap.rearrange("b s d -> (b s) d").rearrange("(t p) d -> p t d", p=P)


def column(ap):
    return ap.rearrange("(p o) -> p o", o=1)


class Split:

    def __init__(self, space, name, shape):
        self.high, self.low = (space.sb(f"{name}_{part}", shape, F32R) for part in ("high", "low"))


def split_matmul(pe, out, left, right, left_at, right_at):
    parts = ((left.high, right.high), (left.high, right.low), (left.low, right.high))
    for n, (a, b) in enumerate(parts):
        last = pe.matmul(out, left_at(a), right_at(b), start=(n == 0), stop=(n == len(parts) - 1))
    return last


def scatter_rows(pool, XN2, slot_of, sorted_x, scattered, g, first, last):
    for n in range(first, last):
        t, choice = GT * g + n // 2, n % 2
        pool.indirect_dma_start(out=sorted_x, out_offset=bass.IndirectOffsetOnAxis(ap=slot_of[:, choice, t:t + 1], axis=0),
                                in_=XN2[:, t, :], in_offset=None).then_inc(scattered, 16)


def phase_a(nc, T, X, XN2, LG, routing, experts, sorted_x, ident):
    rank_all, slot_of, cum, ones, zeros, scattered, SLOTS, REGION, N_SORTED = routing
    NT = X.shape[1]
    G = NT // GT
    with ExitStack() as ctx:
        m = Space(nc, ctx, "a")
        w_cq, w_q, w_c = m.sb("w_cq", [P, 1]), m.sb("w_q", [P, 1]), m.sb("w_c", [P, 1])
        biases = m.sb("biases", [P, 3])
        bias_sum = m.sb("bias_sum", [P, 1])
        b_l = m.sb("b_l", [P, D])
        wl_rows = m.sb("wl_rows", [P, 4 * D])
        wl_t = m.sb("wl_t", [P, 4, D])
        gate_w, gate_b = m.sb("gate_w", [P, 8]), m.sb("gate_b", [P, 8])
        q_rows = [m.sb(f"q_rows{i}", [P, GT, D]) for i in range(2)]
        stats, mv = m.sb("stats", [P, GT, 6]), m.sb("mv", [P, GT, 2])
        var1, rstd1, var2, rstd2, minus_half = (m.sb(n, [P, GT]) for n in ("var1", "rstd1", "var2", "rstd2", "minus_half"))
        c_rows = [m.sb(f"c_rows{i}", [P, GT, D]) for i in range(2)]
        xn_rows = m.sb("xn_rows", [P, GT, D])
        c_t = [m.sb(f"c_t{i}", [P, GW]) for i in range(2)]
        cw_t, q_t = m.sb("cw_t", [P, GW]), m.sb("q_t", [P, GW])
        c2q_t, cc_t, cq_t = m.sb("c2q_t", [P, GW]), m.sb("cc_t", [P, GW]), m.sb("cq_t", [P, GW])
        xn_t = m.sb("xn_t", [P, GW])
        row_max, row_sum, row_rec = m.sb("row_max", [P, GT]), m.sb("row_sum", [P, GT]), m.sb("row_rec", [P, GT])
        s_max = m.sb("s_max", [P, GT])
        scores, weights = m.sb("scores", [P, GT, S]), m.sb("weights", [P, GT, S])
        a_diag = m.sb("a_diag", [P, GT, P])
        a_t = m.sb("a_t", [P, GW])
        bm, bsum, brec = m.sb("bm", [GT, NB]), m.sb("bsum", [GT, NB]), m.sb("brec", [GT, NB])
        b_shift, b_exp, b_att = m.sb("b_shift", [GT, P]), m.sb("b_exp", [GT, P]), m.sb("b_att", [GT, P])
        b_diag = m.sb("b_diag", [P, GT, NB])

        SC = T["L0_ffn_ws1"].shape[1] // P
        ws1, ws2 = m.sb("ws1", [P, SC * P]), m.sb("ws2", [P, SC, D])
        bs1, bs2 = m.sb("bs1", [P, SC]), m.sb("bs2", [P, D])
        h_t = m.sb("h_t", [P, SC, GW])

        E = LG.shape[2]
        above, ties = m.sb("above", [P, GT * E, E]), m.sb("ties", [P, GT * E, E])
        before = m.sb("before", [P, E, E])
        lower = m.sb("lower", [P, P])
        chosen, going_on, running = (m.sb(n, [P, E, GT]) for n in ("chosen", "going_on", "running"))
        counts = [m.sb(f"counts{i}", [P, E]) for i in range(2)]
        region_start, base = m.sb("region_start", [P, E]), m.sb("base", [P, E])
        choices, picked = m.sb("choices", [P, 2, GT, E]), m.sb("picked", [P, 2, GT, E])
        slot = m.sb("slot", [P, 2, GT])

        ps_c, ps_q, ps_s, ps_c2q, ps_m, ps_z = (m.ps(n, [P, 512]) for n in ("ps_c", "ps_q", "ps_s", "ps_c2q", "ps_m", "ps_z"))
        ps_a, ps_x = ps_c, ps_q
        ps_h = [m.ps(f"ps_h{i}", [P, GW]) for i in range(2)]
        M_ROW, M_COL, M_Q2C, M_GATE = 0, 128, 136, 160

        w_loaded, masks_set, zeros_set = m.sem("w_loaded"), m.sem("masks_set"), m.sem("zeros_set")
        loaded = [m.sem(f"loaded{i}") for i in range(2)]
        wl_transposed, wl_copied = m.sem("wl_transposed"), m.sem("wl_copied")
        var1_ready, rstd1_ready, cnorm_ready = m.sem("var1_ready"), m.sem("rstd1_ready"), m.sem("cnorm_ready")
        var2_ready, rstd2_ready, xnorm_ready = m.sem("var2_ready"), m.sem("rstd2_ready"), m.sem("xnorm_ready")
        ct_psum, ct_ready, cw_ready = m.sem("ct_psum"), m.sem("ct_ready"), m.sem("cw_ready")
        s_psum, s_shifted, s_exp, a_ready = m.sem("s_psum"), m.sem("s_shifted"), m.sem("s_exp"), m.sem("a_ready")
        at_psum, at_ready, c2q_psum, c2q_ready = m.sem("at_psum"), m.sem("at_ready"), m.sem("c2q_psum"), m.sem("c2q_ready")
        cc_ready, smax_ready, mrow_psum, b_shifted = m.sem("cc_ready"), m.sem("smax_ready"), m.sem("mrow_psum"), m.sem("b_shifted")
        b_exped, batt_ready, bcol_psum, bdiag_ready = m.sem("b_exped"), m.sem("batt_ready"), m.sem("bcol_psum"), m.sem("bdiag_ready")
        q2c_psum, cq_ready, z_psum = m.sem("q2c_psum"), m.sem("cq_ready"), m.sem("z_psum")
        xt_psum, xt_ready, gate_psum, kept = m.sem("xt_psum"), m.sem("xt_ready"), m.sem("gate_psum"), m.sem("kept")
        experts_loaded, cleared = m.sem("experts_loaded"), m.sem("cleared")
        dve_order, dve_passed, pe_passed = m.sem("dve_order"), m.sem("dve_passed"), m.sem("pe_passed")
        route_constants, counts_ready, slots_ready = m.sem("route_constants"), m.sem("counts_ready"), m.sem("slots_ready")
        sums_psum, x_biased = m.sem("sums_psum"), m.sem("x_biased")
        shared_loaded, h_psum, h_ready, y_psum, x_added = (m.sem(n) for n in ("shared_loaded", "h_psum", "h_ready", "y_psum", "x_added"))
        W_LOADS = 11

        x_dram, q_dram = rows(T["x"]), rows(T["ctx_1024"])

        block = ctx.enter_context(nc.Block())

        @block.sync
        def _(sp):
            def load(g, par):
                sp.dma_start(X[:, ds(GT * g, GT), :], x_dram[:, ds(GT * g, GT), :]).then_inc(loaded[par], 16)
                sp.dma_start(q_rows[par][:], q_dram[:, ds(GT * g, GT), :]).then_inc(loaded[par], 16)

            load(0, 0)
            sp.dma_start(w_cq[:], column(T["L0_xattn_w_cq"])).then_inc(w_loaded, 16)
            sp.dma_start(w_q[:], column(T["L0_xattn_w_q"])).then_inc(w_loaded, 16)
            sp.dma_start(w_c[:], column(T["L0_xattn_w_c"])).then_inc(w_loaded, 16)
            for n, name in enumerate(("L0_xattn_b_cq", "L0_xattn_b_c", "L0_xattn_b_q")):
                sp.dma_start(biases[:, n:n + 1], T[name].partition_broadcast(P)).then_inc(w_loaded, 16)
            sp.dma_start(b_l[:], T["L0_xattn_b_l"].partition_broadcast(P)).then_inc(w_loaded, 16)
            sp.dma_start(wl_rows[:], T["L0_xattn_W_l"]).then_inc(w_loaded, 16)
            sp.dma_start(gate_w[:], T["L0_ffn_gate_w"]).then_inc(w_loaded, 16)
            sp.dma_start(gate_b[:], T["L0_ffn_gate_b"].partition_broadcast(P)).then_inc(w_loaded, 16)
            load(1, 1)
            sp.dma_start(ws1[:], T["L0_ffn_ws1"]).then_inc(shared_loaded, 16)
            sp.dma_start(ws2[:], T["L0_ffn_ws2"].rearrange("(j p) d -> p j d", p=P)).then_inc(shared_loaded, 16)
            with nc.allow_non_contiguous_dma("512 biases, one per partition"):
                sp.dma_start(bs1[:], T["L0_ffn_bs1"].rearrange("(j p) -> p j", p=P)).then_inc(shared_loaded, 16)
            sp.dma_start(bs2[:], T["L0_ffn_bs2"].partition_broadcast(P)).then_inc(shared_loaded, 16)
            with sp.Fori(0, G // 2 - 1) as i:
                for par in range(2):
                    sp.wait_ge(c2q_psum, 2 * i + par + 1)
                    load(2 * i + 2 + par, par)
            w1_all, w2_all = experts
            HC = T["L0_ffn_w1"].shape[2] // P
            sp.dma_start(w1_all[:, :, 0:HC * P], T["L0_ffn_w1"].rearrange("e d h -> d e h")).then_inc(experts_loaded, 16)
            sp.dma_start(w2_all[:], T["L0_ffn_w2"].rearrange("e (j p) d -> p (e j) d", p=P)).then_inc(experts_loaded, 16)
            with nc.allow_non_contiguous_dma("biases, one per partition"):
                for e in range(E):
                    sp.dma_start(w1_all[:, e, HC * P:HC * P + HC], T["L0_ffn_b1"][e].rearrange("(j p) -> p j", p=P)).then_inc(experts_loaded, 16)
            sp.dma_start(w1_all[:, :, HC * P + HC:], T["L0_ffn_b2"].partition_broadcast(P)).then_inc(experts_loaded, 16)
            sp.wait_ge(zeros_set, 4)
            for t in range(E * REGION, sorted_x.shape[0] // SLOTS):
                sp.dma_start(sorted_x[t * SLOTS:(t + 1) * SLOTS, :].rearrange("(p a) d -> p (a d)", p=P), zeros[:]).then_inc(cleared, 16)
            sp.wait_ge(experts_loaded, 16 * (3 + E))
            sp.wait_ge(cleared, 16 * (sorted_x.shape[0] // SLOTS - E * REGION))

        def turns(engine, body):
            body(0, -2, True, False, False, False, False)
            body(0, -1, True, True, False, False, False)
            body(0, 0, True, True, True, False, False)
            body(0, 1, True, True, True, True, False)
            with engine.Fori(1, G // 2 - 1) as i:
                body(i, 0, True, True, True, True, True)
                body(i, 1, True, True, True, True, True)
            body(0, G - 2, False, True, True, True, True)
            body(0, G - 1, False, False, True, True, True)
            body(0, G, False, False, False, True, True)
            body(0, G + 1, False, False, False, False, True)

        @block.gpsimd
        def _(pool):
            pool.memset(ident[:], 0.0).then_inc(masks_set, 1)
            pool.wait_ge(masks_set, 1)
            pool.affine_select(out=ident[:], in_=ident[:], compare_op=ALU.not_equal, fill=1.0, base=0,
                               pattern=[[-1, P]], channel_multiplier=1).then_inc(masks_set, 1)
            pool.memset(minus_half[:], -0.5).then_inc(zeros_set, 1)
            pool.memset(a_diag[:], 0.0).then_inc(zeros_set, 1)
            pool.memset(b_diag[:], 0.0).then_inc(zeros_set, 1)
            pool.wait_ge(zeros_set, 3)

            def set_route_constants():
                pool.memset(zeros[:], 0.0).then_inc(zeros_set, 1)
                pool.memset(before[:], 1.0).then_inc(route_constants, 1)
                pool.memset(lower[:], 1.0).then_inc(route_constants, 1)
                pool.memset(going_on[:], 1.0).then_inc(route_constants, 1)
                pool.wait_ge(route_constants, 3)
                pool.affine_select(out=before[:], in_=before[:], compare_op=ALU.is_gt, fill=0.0, base=0,
                                   pattern=[[1, E], [-1, E]], channel_multiplier=0).then_inc(route_constants, 1)
                pool.affine_select(out=lower[:], in_=lower[:], compare_op=ALU.is_gt, fill=0.0, base=0,
                                   pattern=[[1, P]], channel_multiplier=-1).then_inc(route_constants, 1)
                pool.memset(going_on[:, :, 0:1], 0.0).then_inc(route_constants, 1)
                pool.iota(region_start[:], pattern=[[REGION * SLOTS, E]], base=-1, channel_multiplier=0,
                          allow_small_or_imprecise_dtypes=True).then_inc(route_constants, 1)
                pool.memset(ones[:], 1.0).then_inc(route_constants, 1)
                pool.memset(cum[1][:], 0.0).then_inc(route_constants, 1)
                for choice in range(2):
                    pool.memset(choices[:, choice, :, :], float(choice)).then_inc(route_constants, 1)

            def scatter(g, first, last):
                pool.wait_ge(kept, g + 1)
                pool.wait_ge(slots_ready, g + 1)
                scatter_rows(pool, XN2, slot_of, sorted_x, scattered, g, first, last)

            pool.wait_ge(shared_loaded, 64)
            for n in range(-2, G + 2):
                if n + 2 < G:
                    pool.wait_ge(var1_ready, n + 3)
                    pool.tensor_tensor(rstd1[:], var1[:], minus_half[:], ALU.pow).then_inc(rstd1_ready, 1)
                if n == -2:
                    set_route_constants()
                if n >= 2:
                    pool.wait_ge(x_added, n - 1)
                    x_g = X[:, GT * (n - 2):GT * (n - 1), :]
                    pool.tensor_tensor(x_g, x_g, bs2[:].unsqueeze(1).to_broadcast([P, GT, D]), ALU.add).then_inc(x_biased, 1)
                if n >= 3:
                    scatter(n - 3, 0, 3)
                if 0 <= n < G:
                    pool.wait_ge(var2_ready, n + 1)
                    pool.tensor_tensor(rstd2[:], var2[:], minus_half[:], ALU.pow).then_inc(rstd2_ready, 1)
                    pool.wait_ge(xnorm_ready, GT * (n + 1))
                    pool.tensor_copy(XN2[:, GT * n:GT * (n + 1), :], xn_rows[:]).then_inc(kept, 1)
                if n >= 3:
                    scatter(n - 3, 3, 2 * GT)

        @block.scalar
        def _(act):
            act.wait_ge(wl_transposed, 1)
            act.copy(wl_t[:].rearrange("p a b -> p (a b)"), ps_z[:]).then_inc(wl_copied, 1)

            def body(i, c, s1, s2, s3, s4, s5):
                n = 2 * i + c
                if s2:
                    act.wait_ge(s_shifted, n + 2)
                    act.activation(weights[:], scores[:], ACT.Exp).then_inc(s_exp, 1)
                    act.wait_ge(b_shifted, n + 2)
                    act.activation(b_exp[:], b_shift[:], ACT.Exp).then_inc(b_exped, 1)
                if s1:
                    act.wait_ge(ct_psum, 2 * (n + 2) + 1)
                    act.copy(c_t[c % 2][:], ps_c[:]).then_inc(ct_ready, 1)
                    act.wait_ge(ct_psum, 2 * (n + 2) + 2)
                    act.copy(q_t[:], ps_q[:]).then_inc(ct_ready, 1)
                if s2:
                    act.wait_ge(at_psum, n + 2)
                    act.copy(a_t[:], ps_a[:]).then_inc(at_ready, 1)
                if s4:
                    if isinstance(n, int) and n == 1:
                        act.wait_ge(shared_loaded, 64)
                    for j in range(SC):
                        act.wait_ge(h_psum, SC * (n - 1) + j + 1)
                        act.activation(h_t[:, j, :], ps_h[j % 2][:], ACT.Gelu, bias=bs1[:, j:j + 1]).then_inc(h_ready, 1)
                if s2:
                    act.wait_ge(c2q_psum, n + 2)
                    act.copy(c2q_t[:], ps_c2q[:]).then_inc(c2q_ready, 1)
                if s3:
                    act.wait_ge(xt_psum, n + 1)
                    act.copy(xn_t[:], ps_x[:]).then_inc(xt_ready, 1)

            turns(act, body)

        @block.vector
        def _(dve):
            dve.wait_ge(w_loaded, 16 * (W_LOADS - 1))
            dve.wait_ge(zeros_set, 3)
            dve.tensor_reduce(bias_sum[:], biases[:], AX.X, ALU.add).then_inc(dve_order, 1)

            def statistics(step, x_of, var, var_ready):
                for k in range(GT - 1):
                    dve.bn_stats(stats[:, k, :], x_of(k))
                step(dve.bn_stats(stats[:, GT - 1, :], x_of(GT - 1)), True)
                for k in range(GT - 1):
                    dve.bn_aggr(mv[:, k, :], stats[:, k, :])
                step(dve.bn_aggr(mv[:, GT - 1, :], stats[:, GT - 1, :]))
                dve.tensor_scalar(var[:], mv[:, :, 1], LN_EPS, None, ALU.add).then_inc(var_ready, 1)

            def normalise(x_of, rstd, out, norm_ready):
                for k in range(GT):
                    dve.tensor_scalar(out[:, k, :], x_of(k), mv[:, k, 0:1], rstd[:, k:k + 1],
                                      ALU.subtract, ALU.mult).then_inc(norm_ready, 1)

            def ranks(step, g, par):
                if isinstance(g, int) and g == 0:
                    dve.wait_ge(route_constants, 11)
                lg, rank = LG[:, ds(GT * g, GT), :], rank_all[:, ds(GT * g, GT), :]
                lg_j = lg.unsqueeze(2).to_broadcast([P, GT, E, E])
                lg_e = lg.unsqueeze(3).to_broadcast([P, GT, E, E])
                a4 = above[:].rearrange("p (t e) j -> p t e j", e=E)
                t4 = ties[:].rearrange("p (t e) j -> p t e j", e=E)
                dve.tensor_tensor(a4, lg_j, lg_e, ALU.is_gt)
                step(dve.tensor_tensor(t4, lg_j, lg_e, ALU.is_equal))
                step(dve.tensor_tensor(t4, t4, before[:].unsqueeze(1).to_broadcast([P, GT, E, E]), ALU.mult))
                step(dve.tensor_tensor(above[:], above[:], ties[:], ALU.add))
                step(dve.tensor_reduce(rank.rearrange("p t e -> p (t e)"), above[:], AX.X, ALU.add))
                step(dve.tensor_scalar(chosen[:].rearrange("p e t -> p t e"), rank, 2.0, None, ALU.is_lt))
                step(dve.tensor_reduce(counts[par][:], chosen[:], AX.X, ALU.add))
                step(dve.tensor_tensor(cum[par][:], cum[1 - par][:], counts[par][:], ALU.add))
                ins = dve.tensor_tensor_scan(running[:].rearrange("p e t -> p (e t)"), going_on[:].rearrange("p e t -> p (e t)"),
                                             chosen[:].rearrange("p e t -> p (e t)"), 0.0, ALU.mult, ALU.add)
                step(ins)
                dve.sem_inc(counts_ready, 1)

            def slots(step, g):
                step(dve.tensor_tensor(running[:], running[:], base[:].unsqueeze(2).to_broadcast([P, E, GT]), ALU.add))
                rank = rank_all[:, ds(GT * g, GT), :].unsqueeze(1).to_broadcast([P, 2, GT, E])
                step(dve.tensor_tensor(picked[:], rank, choices[:], ALU.is_equal))
                step(dve.tensor_tensor(picked[:], picked[:],
                                       running[:].rearrange("p e t -> p t e").unsqueeze(1).to_broadcast([P, 2, GT, E]), ALU.mult))
                step(dve.tensor_reduce(slot[:], picked[:], AX.X, ALU.add))
                dve.tensor_copy(slot_of[:, :, ds(GT * g, GT)], slot[:]).then_inc(slots_ready, 1)

            STEPS1, STEPS2, STEPS3, STEPS4, STEPS5 = 2, 6, 5, 8, 5

            def body(i, c, s1, s2, s3, s4, s5):
                n = 2 * i + c
                par = c % 2
                start = 1 + (n + 2) * STEPS1 + (n + 1) * STEPS2 + n * STEPS3 + (n - 1) * STEPS4 + (n - 2) * STEPS5
                if isinstance(n, int):
                    start = 1 + sum(steps * min(max(n + 2 - k, 0), G)
                                    for k, steps in enumerate((STEPS1, STEPS2, STEPS3, STEPS4, STEPS5)))
                chain = Chain(dve, dve_order, start, dve_passed)

                def x_of(group):
                    return lambda k: X[:, ds(GT * group + k, 1), :].rearrange("p a b -> p (a b)")

                if s3:
                    dve.wait_ge(c2q_ready, n + 1)
                    dve.tensor_tensor(cc_t[:], c2q_t[:], c_t[par][:], ALU.mult).then_inc(cc_ready, 1)
                    dve.wait_ge(q2c_psum, n + 1)
                    dve.tensor_tensor(cq_t[:].rearrange("p (n c) -> p n c", c=S), c_t[par][:].rearrange("p (n c) -> p n c", c=S),
                                      ps_m[:, M_Q2C:M_Q2C + GT * NB].unsqueeze(2).to_broadcast([P, GT * NB, S]),
                                      ALU.mult).then_inc(cq_ready, 1)
                if s2:
                    dve.wait_ge(s_psum, n + 2)
                    s_view = ps_s[:, 0:GT * S].rearrange("p (k q) -> p k q", q=S)
                    chain.step(dve.tensor_reduce(row_max[:], s_view, AX.X, ALU.max))
                    dve.scalar_tensor_tensor(s_max[:], ps_s[:, GT * S:GT * S + GT], bias_sum[:, 0:1], row_max[:],
                                             ALU.add, ALU.add).then_inc(smax_ready, 1)
                    dve.tensor_tensor(scores[:], s_view, row_max[:].unsqueeze(2).to_broadcast([P, GT, S]),
                                      ALU.subtract).then_inc(s_shifted, 1)
                if s5:
                    dve.wait_ge(y_psum, n - 1)
                    x_s = X[:, ds(GT * (n - 2), GT), :]
                    dve.tensor_tensor(x_s, x_s, ps_h[0][:].rearrange("p (k d) -> p k d", d=D), ALU.add).then_inc(x_added, 1)
                if s1:
                    wait_alone(dve, loaded[par], 32 * (i + (c + 2) // 2 + 1), dve_passed)
                    statistics(chain.step, x_of(n + 2), var1, var1_ready)
                if s2:
                    dve.wait_ge(mrow_psum, n + 2)
                    m_view = ps_m[0:GT, M_ROW:M_ROW + P].rearrange("p (b c) -> p b c", c=S)
                    chain.step(dve.tensor_reduce(bm[:], m_view, AX.X, ALU.max))
                    dve.tensor_tensor(b_shift[:].rearrange("p (b c) -> p b c", c=S), m_view,
                                      bm[:].unsqueeze(2).to_broadcast([GT, NB, S]), ALU.subtract).then_inc(b_shifted, 1)
                if s5:
                    wait_alone(dve, sums_psum, n - 1, dve_passed)
                    chain.step(dve.tensor_tensor(base[:], ps_x[:, 0:E], region_start[:], ALU.add))
                if s1:
                    dve.wait_ge(rstd1_ready, n + 3)
                    normalise(x_of(n + 2), rstd1, c_rows[par], cnorm_ready)
                if s2:
                    dve.wait_ge(s_exp, n + 2)
                    chain.step(dve.tensor_reduce(row_sum[:], weights[:], AX.X, ALU.add))
                    chain.step(dve.reciprocal(row_rec[:], row_sum[:]))
                    for b in range(NB):
                        h = slice(b * S, b * S + S)
                        dve.tensor_tensor(a_diag[h, :, h], weights[h], row_rec[h].unsqueeze(2).to_broadcast([S, GT, S]),
                                          ALU.mult).then_inc(a_ready, 1)
                if s3:
                    dve.wait_ge(z_psum, n + 1)
                    x_g = X[:, ds(GT * n, GT), :]
                    chain.step(dve.tensor_tensor(x_g, ps_z[:].rearrange("p (k d) -> p k d", d=D), x_g, ALU.add))
                    chain.step(dve.tensor_tensor(x_g, x_g, b_l[:].unsqueeze(1).to_broadcast([P, GT, D]), ALU.add), True)
                    statistics(chain.step, x_of(n), var2, var2_ready)
                if s2:
                    dve.wait_ge(b_exped, n + 2)
                    b_view = b_exp[:].rearrange("p (b c) -> p b c", c=S)
                    chain.step(dve.tensor_reduce(bsum[:], b_view, AX.X, ALU.add))
                    chain.step(dve.reciprocal(brec[:], bsum[:]))
                    dve.tensor_tensor(b_att[:].rearrange("p (b c) -> p b c", c=S), b_view,
                                      brec[:].unsqueeze(2).to_broadcast([GT, NB, S]), ALU.mult).then_inc(batt_ready, 1)
                if s3:
                    dve.wait_ge(rstd2_ready, n + 1)
                    normalise(x_of(n), rstd2, xn_rows, xnorm_ready)
                if s1:
                    dve.wait_ge(ct_ready, 2 * (n + 2) + 1)
                    dve.tensor_scalar(cw_t[:], c_t[par][:], w_cq[:, 0:1], w_q[:, 0:1], ALU.mult, ALU.add).then_inc(cw_ready, 1)
                if s2:
                    dve.wait_ge(bcol_psum, n + 2)
                    for b in range(NB):
                        h = slice(b * S, b * S + S)
                        dve.tensor_copy(b_diag[h, :, b], ps_m[h, M_COL:M_COL + GT]).then_inc(bdiag_ready, 1)
                if s5:
                    slots(chain.step, n - 2)
                if s4:
                    ranks(chain.step, n - 1, (c + 1) % 2)
                if s3:
                    dve.wait_ge(gate_psum, n + 1)
                    chain.step(dve.tensor_tensor(LG[:, ds(GT * n, GT), :],
                                                 ps_m[:, M_GATE:M_GATE + GT * 8].rearrange("p (k e) -> p k e", e=8),
                                                 gate_b[:].unsqueeze(1).to_broadcast([P, GT, 8]), ALU.add))
                assert chain.n == STEPS1 * s1 + STEPS2 * s2 + STEPS3 * s3 + STEPS4 * s4 + STEPS5 * s5, chain.n

            turns(dve, body)

        @block.tensor
        def _(pe):
            pe.wait_ge(masks_set, 2)
            pe.wait_ge(w_loaded, 16 * (W_LOADS - 1))
            for j in range(4):
                last = pe.transpose(ps_z[:, j * P:(j + 1) * P], wl_rows[:, j * D:(j + 1) * D], ident[:])
            last.then_inc(wl_transposed, 1)
            pe.wait_ge(wl_copied, 1)

            def body(i, c, s1, s2, s3, s4, s5):
                n = 2 * i + c
                par = c % 2
                if s2:
                    pe.wait_ge(smax_ready, n + 2)
                    pe.transpose(ps_m[0:GT, M_ROW:M_ROW + P], s_max[:], ident[:]).then_inc(mrow_psum, 1)
                if s3:
                    pe.wait_ge(c2q_ready, n + 1)
                    pe.wait_ge(cc_ready, n + 1)
                    pe.wait_ge(cq_ready, n + 1)
                    for k in range(GT):
                        for j, part in enumerate((c_t[par], c2q_t, cc_t, cq_t)):
                            last = pe.matmul(ps_z[:, k * D:(k + 1) * D], part[:, k * P:(k + 1) * P], wl_t[:, j, :],
                                             start=(j == 0), stop=(j == 3))
                    last.then_inc(z_psum, 1)
                if s1:
                    pe.wait_ge(loaded[par], 32 * (i + (c + 2) // 2 + 1))
                    for k in range(GT):
                        pe.wait_ge(cnorm_ready, GT * (n + 2) + k + 1)
                        last = pe.transpose(ps_c[:, k * P:(k + 1) * P], c_rows[par][:, k, :], ident[:])
                    last.then_inc(ct_psum, 1)
                    for k in range(GT):
                        last = pe.transpose(ps_q[:, k * P:(k + 1) * P], q_rows[par][:, k, :], ident[:])
                    last.then_inc(ct_psum, 1)
                if s2:
                    if s1:
                        wait_alone(pe, ct_ready, 2 * (n + 2) + 1, pe_passed)
                    pe.wait_ge(a_ready, NB * (n + 2))
                    for k in range(GT):
                        last = pe.transpose(ps_a[:, k * P:(k + 1) * P], a_diag[:, k, :], ident[:])
                    last.then_inc(at_psum, 1)
                if s4:
                    if isinstance(n, int) and n == 1:
                        pe.wait_ge(shared_loaded, 64)
                    for j in range(SC):
                        if j >= 2:
                            pe.wait_ge(h_ready, SC * (n - 1) + j - 1)
                        elif j == 0 and not (isinstance(n, int) and n == 1):
                            pe.wait_ge(x_added, n - 1)
                        pe.matmul(ps_h[j % 2][:], ws1[:, j * P:(j + 1) * P], xn_t[:], start=True, stop=True).then_inc(h_psum, 1)
                if s2:
                    wait_alone(pe, batt_ready, n + 2, pe_passed)
                    pe.transpose(ps_m[:, M_COL:M_COL + GT], b_att[:], ident[0:GT, 0:GT]).then_inc(bcol_psum, 1)
                    pe.wait_ge(at_ready, n + 2)
                    for k in range(GT):
                        last = pe.matmul(ps_c2q[:, k * P:(k + 1) * P], q_rows[1 - par][:, k, :], a_t[:, k * P:(k + 1) * P],
                                         start=True, stop=True)
                    last.then_inc(c2q_psum, 1)
                if s3:
                    if s1:
                        wait_alone(pe, ct_ready, 2 * (n + 2) + 2, pe_passed)
                    for k in range(GT):
                        pe.wait_ge(xnorm_ready, GT * n + k + 1)
                        last = pe.transpose(ps_x[:, k * P:(k + 1) * P], xn_rows[:, k, :], ident[:])
                    last.then_inc(xt_psum, 1)
                if s1:
                    pe.wait_ge(ct_ready, 2 * (n + 2) + 2)
                    for k in range(GT):
                        last = pe.matmul(ps_s[:, GT * S + k:GT * S + k + 1], c_t[par][:, k * P:(k + 1) * P], w_c[:, 0:1],
                                         start=True, stop=True)
                    wait_alone(pe, cw_ready, n + 3, pe_passed)
                    for k in range(GT):
                        for b in range(NB):
                            o = k * P + b * S
                            last = pe.matmul(ps_s[b * S:b * S + S, k * S:(k + 1) * S], cw_t[:, o:o + S], q_t[:, o:o + S],
                                             start=True, stop=True)
                    last.then_inc(s_psum, 1)
                if s2:
                    pe.wait_ge(bdiag_ready, NB * (n + 2))
                    for k in range(GT):
                        last = pe.matmul(ps_m[:, M_Q2C + NB * k:M_Q2C + NB * (k + 1)], c_rows[1 - par][:, k, :], b_diag[:, k, :],
                                         start=True, stop=True)
                    last.then_inc(q2c_psum, 1)
                if s3:
                    pe.wait_ge(xt_ready, n + 1)
                    for k in range(GT):
                        last = pe.matmul(ps_m[:, M_GATE + 8 * k:M_GATE + 8 * (k + 1)], xn_t[:, k * P:(k + 1) * P],
                                         gate_w[:], start=True, stop=True)
                    last.then_inc(gate_psum, 1)
                if s4:
                    pe.wait_ge(h_ready, SC * n)
                    for k in range(GT):
                        for j in range(SC):
                            last = pe.matmul(ps_h[0][:, k * D:(k + 1) * D], h_t[:, j, k * P:(k + 1) * P], ws2[:, j, :],
                                             start=(j == 0), stop=(j == SC - 1))
                    last.then_inc(y_psum, 1)
                    wait_alone(pe, counts_ready, n, pe_passed)
                    pe.matmul(ps_x[:, 0:E], ones[:], cum[c % 2][:], start=True, stop=False)
                    pe.matmul(ps_x[:, 0:E], lower[:], counts[(c + 1) % 2][:], start=False, stop=True).then_inc(sums_psum, 1)

            turns(pe, body)


def phase_r(nc, XN2, LG, w_first, w_second, y_row_of, expert_of, tile_of, routing, sorted_x):
    rank_all, slot_of, cum, ones, zeros, scattered, SLOTS, REGION, N_SORTED = routing
    NT, E = LG.shape[1], LG.shape[2]
    G = NT // GT
    MAX_TILES = NT * P // SLOTS
    with ExitStack() as ctx:
        m = Space(nc, ctx, "r")
        mask, tmp = m.sb("mask", [P, NT, E]), m.sb("tmp", [P, NT, E])
        moved, y_row = m.sb("moved", [P, E]), m.sb("y_row", [P, 2, NT])
        v1, v2, diff, ratio, den = (m.sb(n, [P, NT]) for n in ("v1", "v2", "diff", "ratio", "den"))
        limits, more = m.sb("limits", [P, MAX_TILES]), m.sb("more", [P, E, MAX_TILES])
        tiles, ends, spare = m.sb("tiles", [P, E]), m.sb("ends", [P, E]), m.sb("spare", [P, E])
        region_start, tail, tail_row = m.sb("region_start", [P, E]), m.sb("tail", [P, E]), m.sb("tail_row", [P, E], mybir.dt.int32)
        numbers, passed_ends = m.sb("numbers", [P, N_SORTED]), m.sb("passed_ends", [P, N_SORTED, E])
        owner, place = m.sb("owner", [P, N_SORTED]), m.sb("place", [P, N_SORTED])
        ps_r = m.ps("ps_r", [P, 512])

        constants, diff_ready, ratio_ready, order = m.sem("constants"), m.sem("diff_ready"), m.sem("ratio_ready"), m.sem("order")
        sums_psum, tails_ready, tails_filled = m.sem("sums_psum"), m.sem("tails_ready"), m.sem("tails_filled")
        block = ctx.enter_context(nc.Block())

        @block.sync
        def _(sp):
            sp.wait_ge(tails_ready, 1)
            sp.wait_ge(scattered, 16 * 2 * NT)
            for e in range(E):
                row = sp.value_load(tail_row[0:1, e:e + 1], min_val=e * REGION * SLOTS, max_val=((e + 1) * REGION - 1) * SLOTS)
                sp.dma_start(sorted_x[ds(row, SLOTS), :].rearrange("(p a) d -> p (a d)", p=P), zeros[:]).then_inc(tails_filled, 16)
            sp.wait_ge(tails_filled, 16 * E)

        @block.gpsimd
        def _(pool):
            pool.iota(limits[:], pattern=[[SLOTS, MAX_TILES]], base=0, channel_multiplier=0,
                      allow_small_or_imprecise_dtypes=True).then_inc(constants, 1)
            pool.iota(numbers[:], pattern=[[1, N_SORTED]], base=0, channel_multiplier=0,
                      allow_small_or_imprecise_dtypes=True).then_inc(constants, 1)
            pool.iota(region_start[:], pattern=[[REGION * SLOTS, E]], base=0, channel_multiplier=0,
                      allow_small_or_imprecise_dtypes=True).then_inc(constants, 1)
            scatter_rows(pool, XN2, slot_of, sorted_x, scattered, G - 1, 0, 2 * GT)
            pool.wait_ge(scattered, 16 * 2 * NT)

        @block.tensor
        def _(pe):
            pe.matmul(ps_r[:, 0:E], ones[:], cum[(G - 1) % 2][:], start=True, stop=True).then_inc(sums_psum, 1)

        @block.scalar
        def _(act):
            act.wait_ge(diff_ready, 1)
            act.activation(ratio[:], diff[:], ACT.Exp).then_inc(ratio_ready, 1)

        @block.vector
        def _(dve):
            chain = Chain(dve, order, 0)
            step = chain.step
            dve.wait_ge(constants, 3)
            dve.wait_ge(sums_psum, 1)
            step(dve.tensor_tensor(tail[:], ps_r[:, 0:E], region_start[:], ALU.add))
            dve.tensor_copy(tail_row[:], tail[:]).then_inc(tails_ready, 1)
            step(dve.tensor_tensor(more[:], ps_r[:, 0:E].unsqueeze(2).to_broadcast([P, E, MAX_TILES]),
                                   limits[:].unsqueeze(1).to_broadcast([P, E, MAX_TILES]), ALU.is_gt))
            step(dve.tensor_reduce(tiles[:], more[:], AX.X, ALU.add))
            step(dve.tensor_tensor_scan(ends[:], ones[:, 0:E], tiles[:], 0.0, ALU.mult, ALU.add))
            step(dve.tensor_tensor(passed_ends[:], ends[:].unsqueeze(1).to_broadcast([P, N_SORTED, E]),
                                   numbers[:].unsqueeze(2).to_broadcast([P, N_SORTED, E]), ALU.is_le))
            step(dve.tensor_reduce(owner[:], passed_ends[:], AX.X, ALU.add))
            step(dve.tensor_scalar(expert_of[:], owner[:], float(E - 1), None, ALU.min))
            step(dve.tensor_scalar(spare[:], tiles[:], -1.0, float(REGION), ALU.mult, ALU.add))
            step(dve.tensor_tensor(passed_ends[:], passed_ends[:], spare[:].unsqueeze(1).to_broadcast([P, N_SORTED, E]), ALU.mult))
            step(dve.tensor_reduce(place[:], passed_ends[:], AX.X, ALU.add))
            step(dve.tensor_tensor(place[:], place[:], numbers[:], ALU.add))
            step(dve.tensor_copy(tile_of[:], place[:]))
            step(dve.tensor_tensor(moved[:], ends[:], tiles[:], ALU.subtract))
            step(dve.tensor_scalar(moved[:], moved[:], float(SLOTS), None, ALU.mult))
            step(dve.tensor_tensor(moved[:], moved[:], region_start[:], ALU.subtract))
            step(dve.tensor_copy(y_row[:], slot_of[:]))
            for choice, value in enumerate((v1, v2)):
                step(dve.tensor_scalar(mask[:], rank_all[:], float(choice), None, ALU.is_equal))
                step(dve.tensor_tensor(tmp[:], mask[:], moved[:].unsqueeze(1).to_broadcast([P, NT, E]), ALU.mult))
                step(dve.tensor_reduce(value[:], tmp[:], AX.X, ALU.add))
                step(dve.tensor_tensor(y_row[:, choice, :], y_row[:, choice, :], value[:], ALU.add))
                step(dve.tensor_tensor(tmp[:], mask[:], LG[:], ALU.mult))
                step(dve.tensor_reduce(value[:], tmp[:], AX.X, ALU.add))
            step(dve.tensor_copy(y_row_of[:], y_row[:]))
            dve.tensor_tensor(diff[:], v2[:], v1[:], ALU.subtract).then_inc(diff_ready, 1)
            dve.wait_ge(ratio_ready, 1)
            step(dve.tensor_scalar(den[:], ratio[:], 1.0, None, ALU.add))
            step(dve.reciprocal(w_first[:], den[:]))
            step(dve.tensor_tensor(w_second[:], w_first[:], ratio[:], ALU.mult))


def phase_d(nc, T, layer1, experts, expert_of, tile_of, sorted_x, sorted_y, ident, SLOTS, N_SORTED):
    w1_all, w2_all = experts
    E = w1_all.shape[1]
    HC = w2_all.shape[1] // E
    W1 = w1_all.shape[2]
    DH = T["L1_xattn_wv"].shape[2]
    K = SLOTS // P
    RX, RY, RW = 4, 4, 4
    with ExitStack() as ctx:
        m = Space(nc, ctx, "d")
        x_rows = [m.sb(f"x_rows{i}", [P, K, D]) for i in range(RX)]
        y_rows = [m.sb(f"y_rows{i}", [P, K, D]) for i in range(RY)]
        x_t = [Split(m, f"x_t{i}", [P, SLOTS]) for i in range(2)]
        w1 = [Split(m, f"w1_{i}", [P, HC * P]) for i in range(RW)]
        biases = [m.sb(f"biases_{i}", [P, W1 - HC * P]) for i in range(RW)]
        h_t = [m.sb(f"h_t{i}", [P, HC, SLOTS]) for i in range(2)]
        ps_h = [m.ps(f"ps_h{j}", [P, 512]) for j in range(HC)]
        ps_y = [m.ps(f"ps_y{i}", [P, 512]) for i in range(2)]
        ps_x = [m.ps(f"ps_x{i}", [P, 512]) for i in range(2)]
        loaded = [m.sem(f"loaded{i}") for i in range(RX)]
        stored = [m.sem(f"stored{i}") for i in range(RY)]
        xt_psum, xt_ready, w1_ready = m.sem("xt_psum"), m.sem("xt_ready"), m.sem("w1_ready")
        high_made, x_high = m.sem("high_made"), m.sem("x_high")
        h_psum, h_ready, y_psum, y_ready = m.sem("h_psum"), m.sem("h_ready"), m.sem("y_psum"), m.sem("y_ready")
        U = 4
        PEEL = U + N_SORTED % U
        TURNS = (N_SORTED - PEEL) // U
        loading = [m.sb(f"loading{i}", [P, w.high.shape[1]]) for i, w in enumerate(layer1)]
        layer1_loaded, layer1_high, layer1_low = m.sem("layer1_loaded"), m.sem("layer1_high"), m.sem("layer1_low")
        N_LOADS = 5

        x_dram = sorted_x.rearrange("(n k p) d -> n p k d", k=K, p=P)
        y_dram = sorted_y.rearrange("(n k p) d -> n p k d", k=K, p=P)

        def tiles(engine, body):
            for n in range(PEEL):
                body(0, n)
            with engine.Fori(0, TURNS) as i:
                for c in range(U):
                    body(i, PEEL + c)

        block = ctx.enter_context(nc.Block())

        @block.sync
        def _(sp):
            def tile_number(n):
                return sp.value_load(tile_of[0:1, ds(n, 1)], min_val=0, max_val=x_dram.shape[0] - 1)

            def load(i, c):
                t = tile_number(U * i + c)
                if not (isinstance(i, int) and i == 0 and c < RX):
                    sp.wait_ge(xt_psum, U * i + c - RX + 1)
                sp.dma_start(x_rows[c % RX][:], x_dram[ds(t, 1)].rearrange("n p k d -> p (n k) d")).then_inc(loaded[c % RX], 16)

            for n in range(PEEL):
                load(0, n)
                if n == 2:
                    for w, name in zip(loading, ("wq", "wk")):
                        sp.dma_start(w[:], T[f"L1_xattn_{name}"].rearrange("d n h -> d (n h)")).then_inc(layer1_loaded, 16)
                    for parity in range(2):
                        sp.dma_start(loading[2][:].rearrange("d (a j h) -> d a j h", a=2, h=DH)[:, parity],
                                     T["L1_xattn_wv"].rearrange("d (j a) h -> d j a h", a=2)[:, :, parity, :]).then_inc(layer1_loaded, 16)
                    sp.dma_start(loading[3][:], T["L1_ffn_w1"]).then_inc(layer1_loaded, 16)
            with sp.Fori(0, TURNS) as i:
                for c in range(U):
                    load(i, PEEL + c)

        @block.gpsimd
        def _(pool):
            def store(i, c):
                n = U * i + c
                pool.wait_ge(y_ready, n + 1)
                pool.dma_start(y_dram[ds(n, 1)].rearrange("n p k d -> p (n k) d"), y_rows[c % RY][:]).then_inc(stored[c % RY], 16)

            tiles(pool, store)
            for q in range(RY):
                pool.wait_ge(stored[q], 16 * len([n for n in range(N_SORTED) if n % RY == q]))

        @block.vector
        def _(dve):
            def copy_w1(i, c):
                n = U * i + c
                if not (isinstance(n, int) and n < RW):
                    dve.wait_ge(y_ready, n - RW + 1)
                e = dve.value_load(expert_of[0:1, ds(n, 1)], min_val=0, max_val=E - 1)
                weights = w1_all[:, ds(e, 1), 0:HC * P].rearrange("p a b -> p (a b)")
                dve.tensor_copy(w1[c % RW].high[:], weights).then_inc(high_made, 1)
                dve.tensor_copy(biases[c % RW][:], w1_all[:, ds(e, 1), HC * P:].rearrange("p a b -> p (a b)"))
                dve.wait_ge(high_made, n + 1)
                dve.tensor_tensor(w1[c % RW].low[:], weights, w1[c % RW].high[:], ALU.subtract).then_inc(w1_ready, 1)

            def low_x(i, c):
                n = U * i + c
                dve.wait_ge(x_high, n + 1)
                dve.tensor_tensor(x_t[c % 2].low[:], ps_x[c % 2][:, 0:SLOTS], x_t[c % 2].high[:], ALU.subtract).then_inc(xt_ready, 1)

            def take_y(i, c):
                n = U * i + c
                dve.wait_ge(y_psum, n + 1)
                if not (isinstance(n, int) and n < RY):
                    dve.wait_ge(stored[c % RY], 16 * (i + c // RY))
                dve.tensor_tensor(y_rows[c % RY][:], ps_y[c % 2][:, 0:SLOTS].rearrange("p (k d) -> p k d", d=D),
                                  biases[c % RW][:, HC:].unsqueeze(1).to_broadcast([P, K, D]), ALU.add).then_inc(y_ready, 1)

            copy_w1(0, 0)
            low_x(0, 0)
            copy_w1(0, 1)
            low_x(0, 1)
            for n in range(PEEL - 2):
                copy_w1(0, n + 2)
                low_x(0, n + 2)
                take_y(0, n)
            for n, (w, source) in enumerate(zip(layer1, loading)):
                dve.wait_ge(layer1_high, n + 1)
                dve.tensor_tensor(w.low[:], source[:], w.high[:], ALU.subtract).then_inc(layer1_low, 1)
            with dve.Fori(0, TURNS) as i:
                for c in range(U):
                    copy_w1(i, PEEL + c)
                    low_x(i, PEEL + c)
                    take_y(i, PEEL + c - 2)
            take_y(TURNS - 1, PEEL + U - 2)
            take_y(TURNS - 1, PEEL + U - 1)

        @block.scalar
        def _(act):
            def take_x(i, c):
                n = U * i + c
                act.wait_ge(xt_psum, n + 1)
                if not (isinstance(n, int) and n < 2):
                    act.wait_ge(h_psum, HC * (n - 1))
                act.copy(x_t[c % 2].high[:], ps_x[c % 2][:, 0:SLOTS]).then_inc(x_high, 1)

            def gelu(i, c):
                n = U * i + c
                if not (isinstance(n, int) and n < 2):
                    act.wait_ge(y_psum, n - 1)
                for j in range(HC):
                    act.wait_ge(h_psum, HC * n + j + 1)
                    act.activation(h_t[c % 2][:, j, :], ps_h[j][:, 0:SLOTS], ACT.Gelu,
                                   bias=biases[c % RW][:, j:j + 1]).then_inc(h_ready, 1)

            take_x(0, 0)
            for n in range(PEEL - 1):
                take_x(0, n + 1)
                gelu(0, n)
                if n == 2:
                    act.wait_ge(layer1_loaded, 16 * N_LOADS)
                if 2 <= n < 2 + len(layer1):
                    act.copy(layer1[n - 2].high[:], loading[n - 2][:]).then_inc(layer1_high, 1)
            with act.Fori(0, TURNS) as i:
                for c in range(U):
                    take_x(i, PEEL + c)
                    gelu(i, PEEL + c - 1)
            gelu(TURNS - 1, PEEL + U - 1)

        @block.tensor
        def _(pe):
            def transposes(i, c):
                n = U * i + c
                pe.wait_ge(loaded[c % RX], 16 * (i + c // RX + 1))
                if not (isinstance(n, int) and n < 2):
                    pe.wait_ge(xt_ready, n - 1)
                for k in range(K):
                    last = pe.transpose(ps_x[c % 2][:, k * P:(k + 1) * P], x_rows[c % RX][:, k, :], ident[:])
                last.then_inc(xt_psum, 1)

            def up(i, c):
                n = U * i + c
                pe.wait_ge(xt_ready, n + 1)
                pe.wait_ge(w1_ready, n + 1)
                for j in range(HC):
                    if not (isinstance(n, int) and n == 0):
                        pe.wait_ge(h_ready, HC * (n - 1) + j + 1)
                    split_matmul(pe, ps_h[j][:, 0:SLOTS], w1[c % RW], x_t[c % 2], lambda w: w[:, j * P:(j + 1) * P],
                                 lambda x: x[:]).then_inc(h_psum, 1)

            def down(i, c):
                n = U * i + c
                e = pe.value_load(expert_of[0:1, ds(n, 1)], min_val=0, max_val=E - 1)
                pe.wait_ge(h_ready, HC * (n + 1))
                if not (isinstance(n, int) and n < 2):
                    pe.wait_ge(y_ready, n - 1)
                for k in range(K):
                    for j in range(HC):
                        last = pe.matmul(ps_y[c % 2][:, k * D:(k + 1) * D], h_t[c % 2][:, j, k * P:(k + 1) * P],
                                         w2_all[:, ds(e * HC + j, 1), :].rearrange("p a b -> p (a b)"), start=(j == 0), stop=(j == HC - 1))
                last.then_inc(y_psum, 1)

            transposes(0, 0)
            up(0, 0)
            transposes(0, 1)
            for n in range(PEEL - 2):
                transposes(0, n + 2)
                up(0, n + 1)
                down(0, n)
            with pe.Fori(0, TURNS) as i:
                for c in range(U):
                    transposes(i, PEEL + c)
                    up(i, PEEL + c - 1)
                    down(i, PEEL + c - 2)
            up(TURNS - 1, PEEL + U - 1)
            down(TURNS - 1, PEEL + U - 2)
            down(TURNS - 1, PEEL + U - 1)


def phase_c(nc, T, X, layer1, w_first, w_second, y_row_of, sorted_y, ident, out):
    NT = X.shape[1]
    G = NT // GT
    N_HEADS, DH = T["L1_xattn_wq"].shape[1], T["L1_xattn_wq"].shape[2]
    J = N_HEADS // 2
    H = T["L1_ffn_w1"].shape[1]
    HC = H // P
    Q_SCALE = DH ** -0.5
    with ExitStack() as ctx:
        m = Space(nc, ctx, "c")
        wq, wk, wv, f1 = layer1
        wo = m.sb("wo", [P, J, D])
        f2 = m.sb("f2", [P, HC, D])
        fb1, fb2 = m.sb("fb1", [P, HC]), m.sb("fb2", [P, D])
        ctx_rows = m.sb("ctx_rows", [P, GT, D])
        mask = [m.sb(f"mask{i}", [P, GT, S]) for i in range(2)]
        xn_rows, xn4_rows = m.sb("xn_rows", [P, GT, D]), m.sb("xn4_rows", [P, GT, D])
        xn_t = Split(m, "xn_t", [P, GW])
        xn4_t = xn_t
        ctx_t = Split(m, "ctx_t", [P, GT, NB + 1, S])
        stats, mv = m.sb("stats", [P, GT, 6]), m.sb("mv", [P, GT, 2])
        var, rstd, minus_half = m.sb("var", [P, GT]), m.sb("rstd", [P, GT]), m.sb("minus_half", [P, GT])
        q_t, k_t = m.sb("q_t", [P, J, GW]), m.sb("k_t", [P, J, GW])
        v_s = [m.sb(f"v_s{i}", [P, GT, 2, J * DH]) for i in range(2)]
        o_t = m.sb("o_t", [P, J, GW])
        shifted = m.sb("shifted", [P, 2, J * S])
        e_s = shifted
        probs = [m.sb(f"probs{i}", [P, J, 2, S]) for i in range(2)]
        r_max, r_sum, r_rec = (m.sb(n, [P, 2 * J]) for n in ("r_max", "r_sum", "r_rec"))
        p_t = [m.sb(f"p_t{i}", [P, J // 2 * P]) for i in range(2)]
        h_t = m.sb("h_t", [P, HC, GW])
        back = m.sb("back", [P, 2, GT, D])

        ps_s = m.ps("ps_s", [P, 2, J * S])
        ps_p = [m.ps(f"ps_p{i}", [P, 512]) for i in range(2)]
        ps_o = [m.ps(f"ps_o{i}", [P, 512]) for i in range(2)]
        ps_w = [m.ps(f"ps_w{i}", [P, 512]) for i in range(2)]

        w_loaded, half_set = m.sem("w_loaded"), m.sem("half_set")
        loaded, mask_loaded = m.sem("loaded"), [m.sem(f"mask_loaded{i}") for i in range(2)]
        var_ready, rstd_ready = m.sem("var_ready"), m.sem("rstd_ready")
        xn_ready, xn4_ready = m.sem("xn_ready"), m.sem("xn4_ready")
        work_full, work_free = m.sem("work_full"), [m.sem(f"work_free{i}") for i in range(2)]
        s_psum, s_taken, s_shifted, s_exp, probs_ready = (m.sem(n) for n in ("s_psum", "s_taken", "s_shifted", "s_exp", "probs_ready"))
        pt_psum, pt_ready, pv_psum, pv_taken = (m.sem(n) for n in ("pt_psum", "pt_ready", "pv_psum", "pv_taken"))
        order, y_ready, passed = m.sem("order"), m.sem("y_ready"), m.sem("passed")
        pv_half = m.sem("pv_half")
        high_ready = m.sem("high_ready")
        gathered, added = m.sem("gathered"), m.sem("added")
        stored = [m.sem(f"stored{i}") for i in range(2)]

        x_out, q_dram = rows(out), rows(T["ctx_1024"])
        mask_dram = T["mask_Bx1xSxS2_ff0"].rearrange("b o f t -> (b o f) t").rearrange("(n p) t -> p n t", p=P)

        ORDER = (("v_begin", 2), ("o", 1), ("v_rest", 2 * GT - 2), ("x4", 1), ("up", HC), ("down", 1), ("xt", 1), ("q", J), ("k", J), ("ct", 1))

        def numbered(*names):
            first, n = {}, 0
            for name, count in names:
                first[name], n = n, n + count
            return first, n

        FIRST, N_FIRST = numbered(("ct_0", 1), ("k", J), ("v_begin", 2), ("v_rest", 2 * GT - 2), ("xt", 1), ("q", J), ("ct", 1))
        G0, N_G0 = numbered(*(p for p in ORDER if p[0] not in ("o", "x4", "up", "down")))
        USE, PER = numbered(*ORDER)
        AFTER, N_AFTER = numbered(("o", 1), ("x4", 1), ("up", HC), ("down", 1))
        BASE = N_FIRST + N_G0 - PER
        LAST = BASE + PER * (G - 1) - 1

        DVE_Q = 3

        class Use:

            def __init__(self, i, n):
                self.bank = n % 2
                self.full = 2 * PER * i + n + 1
                self.before = PER * i + n // 2
                self.first = isinstance(self.before, int) and self.before == 0

        def use(i, c, name, j=0):
            if name == "v":
                name, j = ("v_begin", j) if j < 2 else ("v_rest", j - 2)
            if c == "pro":
                return Use(0, FIRST[name] + j)
            g = 2 * i + c
            if isinstance(g, int):
                return Use(0, N_FIRST + G0[name] + j if g == 0 else BASE + PER * g + USE[name] + j if g < G - 1 else
                           LAST + N_AFTER * (g - (G - 1)) + AFTER[name] + j)
            return Use(i, BASE + PER * c + USE[name] + j)

        def groups(engine, body):
            body(0, 0)
            body(0, 1)
            with engine.Fori(0, (G - 4) // 2) as i:
                for c in (2, 3):
                    body(i, c)
            for c in (2, 3):
                body((G - 4) // 2, c)

        def is_g(i, c, g):
            return isinstance(i, int) and 2 * i + c == g

        def prev_use(i, c, name, j=0):
            if is_g(i, c, 0):
                return use(0, "pro", name, j)
            if isinstance(i, int):
                return use(0, 2 * i + c - 1, name, j)
            return Use(i, BASE + PER * (c - 1) + USE[name] + j)

        def norm_number(g, which):
            if isinstance(g, int) and (g == 0 or g >= G - 1):
                return 3 if g == 0 else 2 * G - 1 if g == G - 1 else 2 * G
            return 2 * g + (2 if which == "x4" else 3)

        block = ctx.enter_context(nc.Block())

        @block.sync
        def _(sp):
            def load_ctx(g):
                sp.dma_start(ctx_rows[:], q_dram[:, ds(GT * g, GT), :]).then_inc(loaded, 16)

            def load_mask(g, par):
                sp.dma_start(mask[par][:], mask_dram[:, ds(GT * g, GT), :]).then_inc(mask_loaded[par], 16)

            load_ctx(0)
            load_mask(0, 0)
            load_mask(1, 1)
            sp.dma_start(wo[:], T["L1_xattn_wo"].rearrange("n h d -> (n h) d").rearrange("(j p) d -> p j d", p=P)).then_inc(w_loaded, 16)
            sp.dma_start(f2[:], T["L1_ffn_w2"].rearrange("(j p) d -> p j d", p=P)).then_inc(w_loaded, 16)
            with nc.allow_non_contiguous_dma("512 biases, one per partition"):
                sp.dma_start(fb1[:], T["L1_ffn_b1"].rearrange("(j p) -> p j", p=P)).then_inc(w_loaded, 16)
            sp.dma_start(fb2[:], T["L1_ffn_b2"].partition_broadcast(P)).then_inc(w_loaded, 16)

            def store(g, par):
                sp.wait_ge(y_ready, g + 1)
                sp.dma_start(x_out[:, ds(GT * g, GT), :], X[:, ds(GT * g, GT), :]).then_inc(stored[par], 16)

            def body(i, c):
                g = 2 * i + c
                if not is_g(i, c, G - 1) and not is_g(i, c, G - 2):
                    sp.wait_ge(work_full, prev_use(i, c, "ct").full)
                    load_ctx(g + 2)
                    sp.wait_ge(s_taken, GT * (g + 1))
                    load_mask(g + 2, c % 2)
                if not is_g(i, c, 0):
                    store(g - 1, (c + 1) % 2)

            sp.wait_ge(work_full, use(0, "pro", "ct_0").full)
            load_ctx(1)
            groups(sp, body)
            store(G - 1, 1)
            for par in range(2):
                sp.wait_ge(stored[par], 16 * G // 2)

        @block.gpsimd
        def _(pool):
            pool.memset(minus_half[:], -0.5).then_inc(half_set, 1)

            def gather(g):
                if g > 0:
                    pool.wait_ge(added, g)
                for k in range(GT):
                    for choice in range(2):
                        pool.indirect_dma_start(out=back[:, choice, k, :], out_offset=None, in_=sorted_y,
                                                in_offset=bass.IndirectOffsetOnAxis(ap=y_row_of[:, choice, GT * g + k:GT * g + k + 1], axis=0)
                                                ).then_inc(gathered, 16)

            def root(n):
                pool.wait_ge(var_ready, n)
                pool.tensor_tensor(rstd[:], var[:], minus_half[:], ALU.pow).then_inc(rstd_ready, 1)

            gather(0)
            pool.wait_ge(half_set, 1)
            root(1)
            gather(1)
            root(2)
            gather(2)
            root(3)
            gather(3)
            n = 3
            for g in range(1, G + 1):
                n += 1
                root(n)
                if g + 2 < G:
                    n += 1
                    root(n)
                if g + 3 < G:
                    gather(g + 3)

        @block.tensor
        def _(pe):
            def begin(u):
                if not u.first:
                    pe.wait_ge(work_free[u.bank], u.before)
                return ps_w[u.bank]

            def transposes(u, source):
                w = begin(u)
                for k in range(GT):
                    last = pe.transpose(w[:, k * P:(k + 1) * P], source[:, k, :], ident[:])
                last.then_inc(work_full, 1)

            def xn_transposes(i, c, g):
                pe.wait_ge(xn_ready, GT * (g + 1))
                transposes(use(i, c, "xt"), xn_rows)

            def ctx_transposes(u, g):
                pe.wait_ge(loaded, 16 * (g + 1))
                transposes(u, ctx_rows)

            def evacuated(u):
                pe.wait_ge(work_free[u.bank], u.before + 1)

            def project_q(i, c):
                evacuated(use(i, c, "xt"))
                for j in range(J):
                    split_matmul(pe, begin(use(i, c, "q", j))[:], wq, xn_t, lambda w: w[:, j * P:(j + 1) * P], lambda x: x[:]).then_inc(work_full, 1)

            def project_k(i, c):
                for j in range(J):
                    split_matmul(pe, begin(use(i, c, "k", j))[:], wk, ctx_t, lambda w: w[:, j * P:(j + 1) * P],
                                 lambda x: x[:, :, 0:NB, :]).then_inc(work_full, 1)

            def project_v(i, c, ns):
                for n in ns:
                    k, h = n // 2, n % 2
                    split_matmul(pe, begin(use(i, c, "v", n))[:], ctx_t, wv,
                                 lambda x: x[:, k, h:h + NB, :].rearrange("p b t -> p (b t)"),
                                 lambda w: w[:, h * J * DH:(h + 1) * J * DH]).then_inc(work_full, 1)

            def scores(p, k, first):
                if not first:
                    wait_alone(pe, s_taken, p, passed)
                for j in range(J):
                    for b in range(NB):
                        for h in range(2):
                            r, o = slice(h * DH, h * DH + DH), k * P + b * S
                            last = pe.matmul(ps_s[b * S:b * S + S, h ^ b, j * S:(j + 1) * S], q_t[r, j, o:o + S],
                                             k_t[r, j, o:o + S], start=True, stop=True)
                last.then_inc(s_psum, 1)

            def transpose_probs(p, k):
                for half in range(2):
                    pe.wait_ge(probs_ready, 2 * p + half + 1)
                    if not (isinstance(p, int) and p == 0):
                        pe.wait_ge(pt_ready, 2 * p + half - 1)
                    for jj in range(J // 2):
                        last = pe.transpose(ps_p[half][:, jj * P:(jj + 1) * P],
                                            probs[k % 2][:, half * (J // 2) + jj, :, :].rearrange("p a t -> p (a t)"), ident[:])
                    last.then_inc(pt_psum, 1)

            def values(p, k, par, phase):
                if phase == 0:
                    wait_alone(pe, pt_ready, 2 * (p + 1), passed)
                    if not (isinstance(p, int) and p == 0):
                        wait_alone(pe, pv_taken, 2 * p, passed)
                else:
                    wait_alone(pe, pv_half, p + 1, passed)
                for jj in range(J // 2):
                    for b in range(NB):
                        for half in range(2):
                            h = (half + phase + b) % 2
                            r, features = slice((h ^ b) * S, (h ^ b) * S + S), slice(h * DH, h * DH + DH)
                            j, o = half * (J // 2) + jj, jj * P + b * S
                            last = pe.matmul(ps_o[half][features, o:o + S], v_s[par][r, k, h, j * DH:(j + 1) * DH],
                                             p_t[half][r, o:o + S], start=True, stop=True)
                last.then_inc(pv_half if phase == 0 else pv_psum, 1)

            def out_projection(i, c, g):
                pe.wait_ge(pv_taken, 2 * GT * (g + 1))
                w = begin(use(i, c, "o"))
                for k in range(GT):
                    for j in range(J):
                        last = pe.matmul(w[:, k * D:(k + 1) * D], o_t[:, j, k * P:(k + 1) * P], wo[:, j, :],
                                         start=(j == 0), stop=(j == J - 1))
                last.then_inc(work_full, 1)

            def x4_transposes(i, c, g):
                pe.wait_ge(xn4_ready, GT * (g + 1))
                transposes(use(i, c, "x4"), xn4_rows)

            def feed_up(i, c):
                u4 = use(i, c, "x4")
                pe.wait_ge(work_free[u4.bank], u4.before + 1)
                for j in range(HC):
                    split_matmul(pe, begin(use(i, c, "up", j))[:], f1, xn4_t, lambda w: w[:, j * P:(j + 1) * P],
                                 lambda x: x[:]).then_inc(work_full, 1)

            def feed_down(i, c):
                for j in (HC - 2, HC - 1):
                    u = use(i, c, "up", j)
                    pe.wait_ge(work_free[u.bank], u.before + 1)
                w = begin(use(i, c, "down"))
                for k in range(GT):
                    for j in range(HC):
                        last = pe.matmul(w[:, k * D:(k + 1) * D], h_t[:, j, k * P:(k + 1) * P], f2[:, j, :],
                                         start=(j == 0), stop=(j == HC - 1))
                last.then_inc(work_full, 1)

            ctx_transposes(use(0, "pro", "ct_0"), 0)
            evacuated(use(0, "pro", "ct_0"))
            project_k(0, "pro")
            project_v(0, "pro", range(2 * GT))
            xn_transposes(0, "pro", 0)
            pe.wait_ge(w_loaded, 16 * 4)
            project_q(0, "pro")
            ctx_transposes(use(0, "pro", "ct"), 1)
            for n in (J - 2, J - 1):
                evacuated(use(0, "pro", "q", n))

            def body(i, c):
                g = 2 * i + c
                par = c % 2
                first, last_g = is_g(i, c, 0), is_g(i, c, G - 1)
                for k in range(GT):
                    p = GT * g + k
                    before = not (first and k == 0)
                    v_par = par if k else 1 - par
                    if before:
                        transpose_probs(p - 1, (k - 1) % GT)
                    if k == 0:
                        for n in (J - 2, J - 1):
                            evacuated(prev_use(i, c, "k", n))
                    if k == 2 and not first:
                        x4_transposes(i, c, g - 1)
                    if k == 3 and not last_g:
                        xn_transposes(i, c, g + 1)
                    scores(p, k, not before)
                    if before:
                        values(p - 1, (k - 1) % GT, v_par, 0)
                    if k == 0 and before:
                        values(p - 1, (k - 1) % GT, v_par, 1)
                    if k == 0 and not last_g:
                        evacuated(prev_use(i, c, "ct"))
                        project_v(i, c, range(2))
                    if k == 0 and not first:
                        out_projection(i, c, g - 1)
                    if k == 1 and not last_g:
                        project_v(i, c, range(2, 2 * GT))
                    if k == 2 and not first:
                        feed_up(i, c)
                    if k == 3 and not last_g:
                        project_q(i, c)
                        project_k(i, c)
                    if k == 3 and not last_g and not is_g(i, c, G - 2):
                        ctx_transposes(use(i, c, "ct"), g + 2)
                    if k != 0:
                        values(p - 1, (k - 1) % GT, v_par, 1)
                    if k == 2 and not first:
                        feed_down(i, c)

            groups(pe, body)
            transpose_probs(4 * G - 1, 3)
            values(4 * G - 1, 3, 1, 0)
            values(4 * G - 1, 3, 1, 1)
            out_projection(0, G, G - 1)
            x4_transposes(0, G, G - 1)
            feed_up(0, G)
            feed_down(0, G)

        @block.scalar
        def _(act):
            def take(u, instruction_of):
                act.wait_ge(work_full, u.full)
                instruction_of(ps_w[u.bank]).then_inc(work_free[u.bank], 1)

            def take_t(u, dest):
                act.wait_ge(work_full, u.full)
                if dest is ctx_t:
                    w = ps_w[u.bank][:].rearrange("p (k b t) -> p k b t", b=NB, t=S)
                    act.copy(dest.high[:, :, 0:NB, :], w)
                    act.copy(dest.high[:, :, NB, :], w[:, :, 0, :]).then_inc(high_ready, 1)
                else:
                    act.copy(dest.high[:], ps_w[u.bank][:]).then_inc(high_ready, 1)

            def take_q(i, c, js=range(J)):
                for j in js:
                    take(use(i, c, "q", j), lambda w: act.mul(q_t[:, j, :], w[:], Q_SCALE))

            def take_k(i, c):
                for j in range(J):
                    take(use(i, c, "k", j), lambda w: act.copy(k_t[:, j, :], w[:]))

            def take_v(i, c, dest, ns=range(2 * GT)):
                for n in ns:
                    take(use(i, c, "v", n), lambda w: act.copy(dest[:, n // 2, n % 2, :], w[:]))

            V_BEFORE, Q_BEFORE, H_BEFORE = 5, 3, 2

            def take_probs(p):
                for half in range(2):
                    act.wait_ge(pt_psum, 2 * p + half + 1)
                    if not (isinstance(p, int) and p == 0):
                        act.wait_ge(pv_psum, p)
                    act.copy(p_t[half][:], ps_p[half][:]).then_inc(pt_ready, 1)

            def exponentials(p):
                act.wait_ge(s_shifted, p + 1)
                act.activation(e_s[:], shifted[:], ACT.Exp).then_inc(s_exp, 1)

            def take_values(p, k):
                act.wait_ge(pv_psum, p + 1)
                for half in range(2):
                    act.copy(o_t[:, half * (J // 2):(half + 1) * (J // 2), k * P:(k + 1) * P],
                             ps_o[half][:].rearrange("p (j c) -> p j c", c=P)).then_inc(pv_taken, 1)

            def take_hidden(i, c, js=range(HC)):
                for j in js:
                    take(use(i, c, "up", j), lambda w: act.activation(h_t[:, j, :], w[:], ACT.Relu, bias=fb1[:, j:j + 1]))

            take_t(use(0, "pro", "ct_0"), ctx_t)
            act.wait_ge(w_loaded, 16 * 4)
            take_k(0, "pro")
            take_v(0, "pro", v_s[0])
            take_t(use(0, "pro", "xt"), xn_t)
            take_q(0, "pro")
            take_t(use(0, "pro", "ct"), ctx_t)

            def body(i, c):
                g = 2 * i + c
                first, last_g = is_g(i, c, 0), is_g(i, c, G - 1)
                for k in range(GT):
                    p = GT * g + k
                    before = not (first and k == 0)
                    if before:
                        take_probs(p - 1)
                    if k == 0 and before:
                        take_values(p - 1, (k - 1) % GT)
                    if k == 0 and not last_g:
                        take_v(i, c, v_s[(c + 1) % 2], range(2))
                    if k == 1 and not last_g:
                        take_v(i, c, v_s[(c + 1) % 2], range(2, V_BEFORE))
                    if k == 2 and not first:
                        take_t(use(i, c, "x4"), xn4_t)
                    if k == 3 and not last_g:
                        take_t(use(i, c, "xt"), xn_t)
                        take_q(i, c, range(0, Q_BEFORE))
                    if k == 2 and not first:
                        take_hidden(i, c, range(0, H_BEFORE))
                    exponentials(p)
                    if k == 1 and not last_g:
                        take_v(i, c, v_s[(c + 1) % 2], range(V_BEFORE, 2 * GT))
                    if k == 2 and not first:
                        take_hidden(i, c, range(H_BEFORE, HC))
                    if k == 3 and not last_g:
                        take_q(i, c, [j for j in range(Q_BEFORE, J) if j != DVE_Q])
                        take_k(i, c)
                    if k == 3 and not last_g and not is_g(i, c, G - 2):
                        take_t(use(i, c, "ct"), ctx_t)
                    if k != 0:
                        take_values(p - 1, (k - 1) % GT)

            groups(act, body)
            take_probs(4 * G - 1)
            take_values(4 * G - 1, 3)
            take_t(use(0, G, "x4"), xn4_t)
            take_hidden(0, G)

        @block.vector
        def _(dve):
            state = {"order": 0}

            def step(ins, start, before_stats=False):
                state["order"] += 1
                ins.then_inc(order, 1)
                if before_stats:
                    wait_alone(dve, order, start + state["order"], passed)
                else:
                    dve.wait_ge(order, start + state["order"])

            def add_experts(g, start):
                dve.wait_ge(gathered, 16 * 2 * GT * (g + 1))
                x_g = X[:, ds(GT * g, GT), :]
                for choice, w in enumerate((w_first, w_second)):
                    b = back[:, choice, :, :]
                    step(dve.tensor_tensor(b, b, w[:, ds(GT * g, GT)].unsqueeze(2).to_broadcast([P, GT, D]), ALU.mult), start)
                    ins = dve.tensor_tensor(x_g, x_g, b, ALU.add)
                    if choice == 0:
                        step(ins, start)
                ins.then_inc(added, 1)
                wait_alone(dve, added, g + 1, passed)

            def row_of(g, k):
                return X[:, ds(GT * g + k, 1), :].rearrange("p a b -> p (a b)")

            def statistics(start, g):
                for k in range(GT - 1):
                    dve.bn_stats(stats[:, k, :], row_of(g, k))
                step(dve.bn_stats(stats[:, GT - 1, :], row_of(g, GT - 1)), start, True)
                for k in range(GT - 1):
                    dve.bn_aggr(mv[:, k, :], stats[:, k, :])
                step(dve.bn_aggr(mv[:, GT - 1, :], stats[:, GT - 1, :]), start)
                dve.tensor_scalar(var[:], mv[:, :, 1], LN_EPS, None, ALU.add).then_inc(var_ready, 1)

            def layernorm(g, dest, dest_ready, n):
                dve.wait_ge(rstd_ready, n)
                for k in range(GT):
                    dve.tensor_scalar(dest[:, k, :], row_of(g, k), mv[:, k, 0:1], rstd[:, k:k + 1],
                                      ALU.subtract, ALU.mult).then_inc(dest_ready, 1)

            def shift(p, k, par, start):
                dve.wait_ge(s_psum, p + 1)
                msk = mask[par][:, k, :].unsqueeze(1).to_broadcast([P, 2 * J, S])
                flat = shifted[:].rearrange("p h (j t) -> p (h j) t", t=S)
                ins = dve.tensor_tensor(flat, ps_s[:].rearrange("p h (j t) -> p (h j) t", t=S), msk, ALU.add)
                ins.then_inc(s_taken, 1)
                dve.wait_ge(s_taken, p + 1)
                step(dve.tensor_reduce(r_max[:], flat, AX.X, ALU.max), start)
                dve.tensor_tensor(flat, flat, r_max[:].unsqueeze(2).to_broadcast([P, 2 * J, S]), ALU.subtract).then_inc(s_shifted, 1)

            def low_part(u, n, dest):
                dve.wait_ge(high_ready, n)
                if dest is ctx_t:
                    w = ps_w[u.bank][:].rearrange("p (k b t) -> p k b t", b=NB, t=S)
                    dve.tensor_tensor(dest.low[:, :, 0:NB, :], w, dest.high[:, :, 0:NB, :], ALU.subtract)
                    last = dve.tensor_tensor(dest.low[:, :, NB, :], w[:, :, 0, :], dest.high[:, :, NB, :], ALU.subtract)
                else:
                    last = dve.tensor_tensor(dest.low[:], ps_w[u.bank][:], dest.high[:], ALU.subtract)
                last.then_inc(work_free[u.bank], 1)

            def normalise(p, k, start):
                dve.wait_ge(s_exp, p + 1)
                e3 = e_s[:].rearrange("p h (j t) -> p (h j) t", t=S)
                step(dve.tensor_reduce(r_sum[:], e3, AX.X, ALU.add), start)
                step(dve.reciprocal(r_rec[:], r_sum[:]), start)
                if not (isinstance(p, int) and p < 2):
                    dve.wait_ge(pt_psum, 2 * (p - 1))
                for half in range(2):
                    js = slice(half * (J // 2), (half + 1) * (J // 2))
                    dve.tensor_tensor(probs[k % 2][:, js, :, :].rearrange("p j h t -> p h j t"),
                                      e_s[:].rearrange("p h (j t) -> p h j t", t=S)[:, :, js, :],
                                      r_rec[:].rearrange("p (h j) -> p h j", h=2)[:, :, js].unsqueeze(3).to_broadcast([P, 2, J // 2, S]),
                                      ALU.mult).then_inc(probs_ready, 1)
                dve.wait_ge(probs_ready, 2 * (p + 1))

            def take(u, instruction_of):
                dve.wait_ge(work_full, u.full)
                instruction_of(ps_w[u.bank]).then_inc(work_free[u.bank], 1)

            def add_attention(i, c, g, start):
                u = use(i, c, "o")
                dve.wait_ge(work_full, u.full)
                x_g = X[:, ds(GT * g, GT), :]
                dve.tensor_tensor(x_g, x_g, ps_w[u.bank][:].rearrange("p (k d) -> p k d", d=D), ALU.add).then_inc(work_free[u.bank], 1)
                wait_alone(dve, work_free[u.bank], u.before + 1, passed)

            def finish(i, c, g, par, start):
                u = use(i, c, "down")
                dve.wait_ge(work_full, u.full)
                x_g = X[:, ds(GT * g, GT), :]
                dve.tensor_tensor(x_g, x_g, ps_w[u.bank][:].rearrange("p (k d) -> p k d", d=D),
                                  ALU.add).then_inc(work_free[u.bank], 1)
                dve.wait_ge(work_free[u.bank], u.before + 1)
                dve.tensor_tensor(x_g, x_g, fb2[:].unsqueeze(1).to_broadcast([P, GT, D]), ALU.add).then_inc(y_ready, 1)
                dve.wait_ge(y_ready, g + 1)

            EXPERTS, NORM, TILE = 3, 2, 3
            PRO = 2 * (EXPERTS + NORM)
            O0 = GT * TILE + EXPERTS + NORM
            OG = O0 + NORM
            low_part(use(0, "pro", "ct_0"), 1, ctx_t)
            dve.wait_ge(w_loaded, 16 * 4)
            add_experts(0, 0)
            statistics(0, 0)
            layernorm(0, xn_rows, xn_ready, 1)
            low_part(use(0, "pro", "xt"), 2, xn_t)
            dve.wait_ge(work_full, use(0, "pro", "xt").full)
            add_experts(1, 0)
            statistics(0, 1)
            layernorm(1, xn_rows, xn_ready, 2)
            low_part(use(0, "pro", "ct"), 3, ctx_t)

            def body(i, c):
                g = 2 * i + c
                first, last_g = is_g(i, c, 0), is_g(i, c, G - 1)
                second_before_last = is_g(i, c, G - 2)
                par = c % 2
                start = PRO if first else PRO + O0 + OG * (g - 1) - (EXPERTS + NORM if last_g else 0)
                highs = 3 if first else 3 * g + 2 - (1 if last_g else 0)
                state["order"] = 0
                dve.wait_ge(mask_loaded[par], 16 * (i + c // 2 + 1))
                for k in range(GT):
                    p = GT * g + k
                    if k == 1 and not first:
                        add_attention(i, c, g - 1, start)
                        statistics(start, g - 1)
                    if k == 2 and not first:
                        low_part(use(i, c, "x4"), highs + 1, xn4_t)
                    if k == 3 and not first:
                        finish(i, c, g - 1, (c + 1) % 2, start)
                    if k == 3 and not last_g:
                        low_part(use(i, c, "xt"), highs + (1 if first else 2), xn_t)
                    shift(p, k, par, start)
                    if k == 3 and not last_g:
                        take(use(i, c, "q", DVE_Q), lambda w: dve.tensor_scalar(q_t[:, DVE_Q, :], w[:], Q_SCALE, None, ALU.mult))
                    if k == 1 and not first:
                        if not is_g(i, c, 1):
                            wait_alone(dve, work_full, prev_use(i, c, "x4").full, passed)
                        layernorm(g - 1, xn4_rows, xn4_ready, norm_number(g, "x4"))
                    if k == 3 and not last_g and not second_before_last:
                        add_experts(g + 2, start)
                        statistics(start, g + 2)
                    normalise(p, k, start)
                    if k == 3 and not last_g and not second_before_last:
                        wait_alone(dve, work_full, use(i, c, "xt").full, passed)
                        layernorm(g + 2, xn_rows, xn_ready, norm_number(g, "xn"))
                    if k == 3 and not last_g and not second_before_last:
                        low_part(use(i, c, "ct"), highs + (2 if first else 3), ctx_t)

            groups(dve, body)
            state["order"] = 0
            start = PRO + O0 + OG * (G - 2) - EXPERTS - NORM + GT * TILE + NORM
            add_attention(0, G, G - 1, start)
            statistics(start, G - 1)
            dve.wait_ge(work_full, use(0, G - 1, "x4").full)
            layernorm(G - 1, xn4_rows, xn4_ready, norm_number(G, "x4"))
            low_part(use(0, G, "x4"), 3 * G, xn4_t)
            finish(G // 2, 0, G - 1, 1, start)


def build(nc, T, out):
    NT = T["x"].shape[0] * T["x"].shape[1] // P
    E = T["L0_ffn_gate_w"].shape[1]
    HC = T["L0_ffn_w1"].shape[2] // P
    SLOTS = 2 * P
    N_SORTED = (2 * NT * P + E * (SLOTS - 1)) // SLOTS
    REGION = NT * P // SLOTS + 1
    SORTED_ROWS = (E * REGION + N_SORTED - 2 * NT * P // SLOTS) * SLOTS
    sorted_x = nc.dram_tensor("sorted_x", [SORTED_ROWS, D], F32, kind="Internal").ap()
    sorted_y = nc.dram_tensor("sorted_y", [N_SORTED * SLOTS, D], F32, kind="Internal").ap()
    with ExitStack() as ctx:
        m = Space(nc, ctx, "k")
        X, ident = m.sb("X", [P, NT, D]), m.sb("ident", [P, P])
        w_first, w_second = m.sb("w_first", [P, NT]), m.sb("w_second", [P, NT])
        J, FH = T["L1_xattn_wq"].shape[1] // 2, T["L1_ffn_w1"].shape[1]
        layer1 = [Split(m, name, [P, width]) for name, width in (("wq", J * P), ("wk", J * P), ("wv", J * P), ("f1", FH))]
        y_row_of = m.sb("y_row_of", [P, 2, NT], mybir.dt.uint32)
        with ExitStack() as moe:
            m2 = Space(nc, moe, "e")
            expert_of = m2.sb("expert_of", [P, N_SORTED], mybir.dt.int32)
            tile_of = m2.sb("tile_of", [P, N_SORTED], mybir.dt.int32)
            experts = (m2.sb("w1_all", [P, E, HC * P + HC + D]), m2.sb("w2_all", [P, E * HC, D]))
            with ExitStack() as rest:
                m3 = Space(nc, rest, "f")
                XN2, LG = m3.sb("XN2", [P, NT, D]), m3.sb("LG", [P, NT, E])
                slot_of = m3.sb("slot_of", [P, 2, NT], mybir.dt.uint32)
                rank_all = m3.sb("rank_all", [P, NT, E])
                cum = [m3.sb(f"cum{i}", [P, E]) for i in range(2)]
                ones, zeros = m3.sb("ones", [P, P]), m3.sb("zeros", [P, SLOTS * D // P])
                routing = (rank_all, slot_of, cum, ones, zeros, m3.sem("scattered"), SLOTS, REGION, N_SORTED)
                phase_a(nc, T, X, XN2, LG, routing, experts, sorted_x, ident)
                phase_r(nc, XN2, LG, w_first, w_second, y_row_of, expert_of, tile_of, routing, sorted_x)
            phase_d(nc, T, layer1, experts, expert_of, tile_of, sorted_x, sorted_y, ident, SLOTS, N_SORTED)
        phase_c(nc, T, X, layer1, w_first, w_second, y_row_of, sorted_y, ident, out)


def kernel(**inputs):
    import numpy as _np
    import concourse.bacc as _bacc
    from concourse import mybir as _mybir
    from concourse.bass_utils import run_bass_kernel_spmd as _run

    nc = _bacc.Bacc("TRN2", target_bir_lowering=False, num_devices=1)
    arrays, tensors = {}, {}
    for name in inputs:
        a = _np.ascontiguousarray(inputs[name])
        arrays[f"in_{name}"] = a
        tensors[name] = nc.dram_tensor(f"in_{name}", a.shape, _mybir.dt.from_np(a.dtype), kind="ExternalInput").ap()
    out = nc.dram_tensor("out", inputs["x"].shape, _mybir.dt.float32, kind="ExternalOutput").ap()
    build(nc, tensors, out)
    r = _run(nc, [arrays], core_ids=[0])
    return r.results[0]["out"]
```
